# Optimizing a Trainium2 kernel written in Bass

```python
import numpy as np
import jax
import jax.numpy as jnp

def _softmax(x, axis=-1):
    return jax.nn.softmax(x, axis=axis)

def _gelu(x):
    return jax.nn.gelu(x, approximate=True)

def _silu(x):
    return jax.nn.silu(x)

def _sigmoid(x):
    return jax.nn.sigmoid(x)

def _layernorm(x, axis=-1, eps=1e-05):
    m = jnp.mean(x, axis=axis, keepdims=True)
    v = jnp.var(x, axis=axis, keepdims=True)
    return (x - m) / jnp.sqrt(v + eps)

def _scatter_add(tgt, idx, src, axis=0):
    return tgt.at[idx].add(src)

def _segment_sum(src, seg, n):
    return jax.ops.segment_sum(src, seg, n)
kernel_name = 'mk_xattn_ffn_d1_seqx_r2_ea7b79'

def setup_inputs(seed: int=0):
    np.random.seed(seed)
    _w = jnp.asarray

    def _rec_inputs():
        import jax
        import jax.numpy as jnp
        _rk = jax.random.key(seed)
        x = 7.22e-05 + 1 * jax.random.normal(jax.random.fold_in(_rk, 1), (32, 100, 512), jnp.float32)
        _lenS = 100 - jax.random.randint(jax.random.fold_in(_rk, 7), (32,), 0, max(1, 100 // 4) + 1, jnp.int32)
        _lenS2 = 722 - jax.random.randint(jax.random.fold_in(_rk, 8), (32,), 0, max(1, 722 // 4) + 1, jnp.int32)
        _ctx_1024P = jax.random.normal(jax.random.fold_in(_rk, 11), (32, 16, 512), jnp.float32)
        _ctx_1024c = jax.random.dirichlet(jax.random.fold_in(_rk, 511), 0.3 * jnp.ones((16,), jnp.float32), (32, 722))
        _ctx_1024t = jnp.einsum('bsk,bkd->bsd', _ctx_1024c, _ctx_1024P)
        _ctx_1024t = _ctx_1024t * jax.lax.rsqrt(jnp.mean(jnp.square(_ctx_1024t)) + 1e-12) * 0.953939
        ctx_1024 = 4.13588e-05 + 0.999923 * (_ctx_1024t + 0.3 * jax.random.normal(jax.random.fold_in(_rk, 611), (32, 722, 512), jnp.float32))
        return (x, ctx_1024)
    x, ctx_1024 = _rec_inputs()

    def _L0_xattn_setup():
        import jax, jax.numpy as jnp
        import numpy as np
        H, D, DIM = (8, 128, 512)
        QB, N = (16, 256)

        def layer_norm(x, g, b, eps=1e-05):
            mu = x.mean(-1, keepdims=True)
            var = ((x - mu) ** 2).mean(-1, keepdims=True)
            return (x - mu) / jnp.sqrt(var + eps) * g + b
        key = jax.random.key(seed)
        ks = jax.random.split(key, 8)
        rn = lambda k, shape, s=1.0: jax.random.normal(k, shape, jnp.float32) * s
        return {'q': rn(ks[0], (QB, N, DIM)), 'k': rn(ks[1], (QB, N, DIM)), 'v': rn(ks[2], (QB, N, DIM)), 'ln_g': jnp.ones(DIM, jnp.float32), 'ln_b': jnp.zeros(DIM, jnp.float32), 'w_in': rn(ks[3], (H * D, DIM), 0.02), 'wp_w1': rn(ks[4], (D, 2 * D), 0.05), 'wp_b1': jnp.zeros(D, jnp.float32), 'wp_ln_g': jnp.ones(D, jnp.float32), 'wp_ln_b': jnp.zeros(D, jnp.float32), 'wp_w2': rn(ks[5], (3, D), 0.05), 'wp_b2': jnp.zeros(3, jnp.float32), 'w_out': rn(ks[6], (DIM, H * D), 0.02), 'b_out': jnp.zeros(DIM, jnp.float32)}
    _L0_xattn_all = _L0_xattn_setup()
    _L0_xattn_in = {k: v for k, v in _L0_xattn_all.items() if k in ('ln_g', 'ln_b', 'w_in', 'wp_w1', 'wp_b1', 'wp_ln_g', 'wp_ln_b', 'wp_w2', 'wp_b2', 'w_out', 'b_out')}
    del _L0_xattn_all

    def _L0_ffn_setup():
        import jax, jax.numpy as jnp
        import numpy as np
        NUM_OPS, B, T, D = (8, 8, 256, 512)
        key = jax.random.key(seed)
        k1, k2, k3, k4 = jax.random.split(key, 4)
        x = jax.random.normal(k1, (B, T, D), dtype=jnp.float32)
        W = jax.random.normal(k2, (NUM_OPS, D, D), dtype=jnp.float32) * 0.02
        b = jnp.zeros((NUM_OPS, D), dtype=jnp.float32)
        logits = 0.001 * jax.random.normal(k3, (NUM_OPS,), dtype=jnp.float32)
        u = jax.random.uniform(k4, (NUM_OPS,), dtype=jnp.float32, minval=1e-06, maxval=1.0 - 1e-06)
        return {'x': x, 'W': W, 'b': b, 'logits': logits, 'u': u}
    _L0_ffn_all = _L0_ffn_setup()
    _L0_ffn_in = {k: v for k, v in _L0_ffn_all.items() if k in ('W', 'b', 'logits', 'u')}
    del _L0_ffn_all
    return {'x': x, 'ctx_1024': ctx_1024, 'L0_xattn_ln_g': _L0_xattn_in['ln_g'], 'L0_xattn_ln_b': _L0_xattn_in['ln_b'], 'L0_xattn_w_in': _L0_xattn_in['w_in'], 'L0_xattn_wp_w1': _L0_xattn_in['wp_w1'], 'L0_xattn_wp_b1': _L0_xattn_in['wp_b1'], 'L0_xattn_wp_ln_g': _L0_xattn_in['wp_ln_g'], 'L0_xattn_wp_ln_b': _L0_xattn_in['wp_ln_b'], 'L0_xattn_wp_w2': _L0_xattn_in['wp_w2'], 'L0_xattn_wp_b2': _L0_xattn_in['wp_b2'], 'L0_xattn_w_out': _L0_xattn_in['w_out'], 'L0_xattn_b_out': _L0_xattn_in['b_out'], 'L0_ffn_W': _L0_ffn_in['W'], 'L0_ffn_b': _L0_ffn_in['b'], 'L0_ffn_logits': _L0_ffn_in['logits'], 'L0_ffn_u': _L0_ffn_in['u']}

def reference(x, ctx_1024, L0_xattn_ln_g, L0_xattn_ln_b, L0_xattn_w_in, L0_xattn_wp_w1, L0_xattn_wp_b1, L0_xattn_wp_ln_g, L0_xattn_wp_ln_b, L0_xattn_wp_w2, L0_xattn_wp_b2, L0_xattn_w_out, L0_xattn_b_out, L0_ffn_W, L0_ffn_b, L0_ffn_logits, L0_ffn_u):
    import jax
    import jax.numpy as jnp

    def _L0_xattn_ref(q, k, v, ln_g, ln_b, w_in, wp_w1, wp_b1, wp_ln_g, wp_ln_b, wp_w2, wp_b2, w_out, b_out):
        import jax, jax.numpy as jnp
        import numpy as np
        H, D, DIM = (8, 128, 512)
        QB, N = (16, 256)

        def layer_norm(x, g, b, eps=1e-05):
            mu = x.mean(-1, keepdims=True)
            var = ((x - mu) ** 2).mean(-1, keepdims=True)
            return (x - mu) / jnp.sqrt(var + eps) * g + b

        def proj(t):
            x = layer_norm(t, ln_g, ln_b) @ w_in.T
            Qd, Nd = (t.shape[0], t.shape[1])
            return x.reshape(Qd, Nd, H, D).transpose(2, 0, 1, 3)
        f_q, f_k, f_v = (proj(q), proj(k), proj(v))
        dots = jnp.einsum('hqnd,hqmd->hqnm', f_q, f_k)
        qn = jnp.linalg.norm(f_q, axis=-1)
        kn = jnp.linalg.norm(f_k, axis=-1)
        cosine_sim = dots / (qn[..., :, None] * kn[..., None, :])
        q_centered = f_q - f_q.mean(-1, keepdims=True)
        q_var = jnp.var(f_q, axis=-1, ddof=1)
        k_var = jnp.var(f_k, axis=-1, ddof=1)
        q_ratio = 2.0 * jnp.minimum(q_var, 1.0) / (q_var + 1.0)
        k_ratio = 2.0 * jnp.minimum(k_var, 1.0) / (k_var + 1.0)
        var_component = jnp.einsum('hqn,hqm->hqnm', q_ratio, k_ratio)
        q_flat = q_centered.reshape(H, -1, D)
        feat_corr = jnp.einsum('hnd,hne->hde', q_flat, q_flat) / q_flat.shape[1]
        feat_corr = feat_corr * (1.0 - jnp.eye(D, dtype=feat_corr.dtype))
        decorr_score = jnp.linalg.norm(feat_corr, axis=(-2, -1)) / (D * D)
        decorr_scale = jnp.exp(-5.0 * decorr_score)[:, None, None, None]
        cov_component = cosine_sim * decorr_scale
        q_global = f_q.mean(axis=(1, 2))
        k_global = f_k.mean(axis=(1, 2))
        feats = jnp.concatenate([q_global, k_global], axis=-1)
        h1 = jnp.maximum(layer_norm(feats @ wp_w1.T + wp_b1, wp_ln_g, wp_ln_b), 0.0)
        weights = jax.nn.softmax(h1 @ wp_w2.T + wp_b2, axis=-1)
        cw = weights[:, 0][:, None, None, None]
        vw = weights[:, 1][:, None, None, None]
        ww = weights[:, 2][:, None, None, None]
        mixed = cw * cosine_sim + vw * cov_component + ww * var_component
        out = jnp.einsum('hqnm,hqmd->hqnd', mixed, f_v)
        out = out.transpose(1, 2, 0, 3).reshape(q.shape[0], q.shape[1], H * D)
        return out @ w_out.T + b_out

    def _L0_ffn_ref(x, W, b, logits, u):
        import jax, jax.numpy as jnp
        import numpy as np
        NUM_OPS, B, T, D = (8, 8, 256, 512)
        gumbel = -jnp.log(-jnp.log(u))
        idx = jnp.argmax(jax.nn.log_softmax(logits) + gumbel)
        out = jnp.einsum('btd,de->bte', x, W[idx]) + b[idx]
        return out
    x = x + _L0_xattn_ref(_layernorm(x, axis=-1), ctx_1024, ctx_1024, L0_xattn_ln_g, L0_xattn_ln_b, L0_xattn_w_in, L0_xattn_wp_w1, L0_xattn_wp_b1, L0_xattn_wp_ln_g, L0_xattn_wp_ln_b, L0_xattn_wp_w2, L0_xattn_wp_b2, L0_xattn_w_out, L0_xattn_b_out)
    x = x + _L0_ffn_ref(_layernorm(x, axis=-1), L0_ffn_W, L0_ffn_b, L0_ffn_logits, L0_ffn_u)
    return x

_drawn_inputs = setup_inputs


def setup_inputs(seed=0):
    import zlib

    import numpy as np

    out = dict(_drawn_inputs(seed))
    spreads = {'L0_xattn_ln_g': (1.0, 0.2),
     'L0_xattn_ln_b': (0.0, 0.1),
     'L0_xattn_wp_b1': (0.0, 0.1),
     'L0_xattn_wp_ln_g': (1.0, 0.2),
     'L0_xattn_wp_ln_b': (0.0, 0.1),
     'L0_xattn_wp_b2': (0.0, 0.471),
     'L0_xattn_b_out': (0.0, 0.649),
     'L0_ffn_b': (0.0, 0.628)}
    factors = {}
    for name, (base, spread) in spreads.items():
        noise = np.random.default_rng([zlib.crc32(name.encode()), seed]).standard_normal(out[name].shape)
        drawn = base * np.exp(spread * noise) if base else spread * noise
        out[name] = jnp.asarray(drawn.astype(out[name].dtype))
    for name, factor in factors.items():
        out[name] = (out[name] * factor).astype(out[name].dtype)
    return out
```

```python
from contextlib import ExitStack

import concourse.bass as bass
from concourse import mybir

ALU = mybir.AluOpType
ACT = mybir.ActivationFunctionType
F32 = mybir.dt.float32
F16 = mybir.dt.float16
I32 = mybir.dt.int32
U32 = mybir.dt.uint32
AX = mybir.AxisListType
RMAX = bass.bass_isa.ReduceOp.max
P = 128
EPS = 1e-5
XS = 16.0
QR_SCALE = 64.0
EXPONENT = 0x7F800000


def build(nc, x, ctx_1024, ln_g, ln_b, w_in, wp_w1, wp_b1, wp_ln_g, wp_ln_b, wp_w2, wp_b2,
          w_out, b_out, ffn_W, ffn_b, ffn_logits, ffn_u, out):
    NB, NQ, DIM = x.shape
    NK = ctx_1024.shape[1]
    HD = w_in.shape[0]
    D = P
    H = HD // D
    CH = DIM // P
    HH = H // 2
    HW = HH * D
    NR = NB * NQ
    QT = NR // P
    KT = -(-NK // P)
    KLAST = NK - (KT - 1) * P
    NKT = NB * KT
    MC = D + 2
    MB = 3
    BH = P // H
    NG = NB // BH
    SPLIT = BH * NQ
    QG = -(-SPLIT // P) * P
    G1 = SPLIT // P * P
    MID = SPLIT // P
    assert QT * P == NR and NG == 2 and NR - G1 == QG and QT % 2 == 1 and MID % 2 == 0 and KT % 2 == 0

    xf = x.rearrange("b n d -> (b n) d")
    outf = out.rearrange("b n d -> (b n) d")

    with ExitStack() as ctx:
        def sb(name, shape, dt=F32):
            return ctx.enter_context(nc.sbuf_tensor(name, shape, dt))

        def sem(name):
            return ctx.enter_context(nc.semaphore(name))

        banks = [ctx.enter_context(nc.psum_tensor(f"bank{i}", [P, 512], F32)) for i in range(8)]

        qu = sb("qu", [P, H, NR])
        wh = sb("wh", [P, CH, HD], F16)
        wl = sb("wl", [P, CH, HD], F16)
        woT = sb("woT", [P, H, DIM])
        fh = sb("fh", [P, CH, DIM], F16)
        fl = sb("fl", [P, CH, DIM], F16)
        xh = sb("xh", [P, 2, DIM])
        acc_q = sb("acc_q", [P, DIM])
        acc_k = sb("acc_k", [P, DIM])
        ksum = sb("ksum", [P, H, NB])
        qr = sb("qr", [P, QT, H])
        fs = sb("fs", [P, H])
        ident = sb("ident", [P, P])
        w1T = sb("w1T", [P, 2, P])
        w2T = sb("w2T", [P, 3])
        b1s = sb("b1s", [H, P])
        g1s = sb("g1s", [H, P])
        be1s = sb("be1s", [H, P])
        b2s = sb("b2s", [H, 3])
        ones = sb("ones", [P, P])
        cf = sb("cf", [P, 24])
        nmax = sb("nmax", [P, H])
        bst = sb("bst", [P, 2, 6])
        bcnt = sb("bcnt", [P, 1])
        mv = sb("mv", [P, 2, 2])
        std = sb("std", [P, 2])
        aff = sb("aff", [P, 2, 2])
        hb = sb("hb", [P, 2, H, 6])
        sq = sb("sq", [P, H, 2])
        ss = sb("ss", [P, 2, H])
        nrm = sb("nrm", [P, 2, H])
        rt = sb("rt", [P, 2, H])
        rc = sb("rc", [P, 2, H])
        mean2 = sb("mean2", [P, H])
        rsm = sb("rsm", [P, 9, H])
        scratch = sb("scratch", [P, 12000])

        (EPS_K, EPS_Q, WMAX, WP, WS, INV_A, INV_A2, C_NUM, C_DENK, C_DENQ, FMAX, FP, FSC, F_INV,
         OMAX, OP, OS, UMAX, UP, US, O_INV, TMP, EPS_1, WMAXP) = range(24)

        def col(c, n=P):
            return cf[0:n, c:c + 1]

        class Carve:

            def __init__(self, base, limit):
                self.base, self.at, self.limit = base, 0, limit

            def f32(self, n):
                v = self.base[:, self.at:self.at + n]
                self.at += n
                assert self.at <= self.limit
                return v

            def f16(self, n):
                return self.f32(n // 2).bitcast(F16)

        def chain(eng, s, base=0):
            count = [0]

            def link(ins):
                count[0] += 1
                ins.then_inc(s, 1)
                eng.wait_ge(s, base + count[0])
            return link

        def wait(eng, s, v):
            if isinstance(v, int) and v <= 0:
                return
            eng.wait_ge(s, v)

        def power_of_two(eng, link, m, p, inv, scale):
            link(eng.tensor_scalar(m, m, 1e-30, None, ALU.max))
            link(eng.tensor_scalar(p.bitcast(I32), m.bitcast(I32), EXPONENT, None, ALU.bitwise_and))
            link(eng.reciprocal(inv, p))
            link(eng.tensor_scalar(inv, inv, scale, None, ALU.mult))

        area = qu[:, :, :].rearrange("p h n -> p (h n)")
        cw = Carve(area, H * NR)
        w_raw = cw.f32(H * DIM).rearrange("p (h i) -> p h i", h=H)
        wo_raw = cw.f32(CH * HD).rearrange("p (c n) -> p c n", c=CH)
        f_raw = cw.f32(CH * DIM).rearrange("p (c n) -> p c n", c=CH)
        f_last = cw.f32(DIM)
        g_bc = cw.f32(DIM)
        b_bc = cw.f32(DIM)
        junk = cw.f32(DIM)
        last_col = cw.f32(H)
        bias_col = cw.f32(H)
        w1_raw = cw.f32(2 * P)
        w2_raw = cw.f32(P)
        route = cw.f32(64)

        ld_route, ld_w, ld_wo, ld_f, ld_fb, ld_small = (sem(f"ld_{n}") for n in ("route", "w", "wo", "f", "fb", "small"))
        ident_ready, const_ready = sem("ident_ready"), sem("const_ready")
        route_act, route_dve, route_idx = sem("route_act"), sem("route_dve"), sem("route_idx")
        w_dve, w_max, w_all = sem("w_dve"), sem("w_max"), sem("w_all")
        f_sub, f_max, f_all = sem("f_sub"), sem("f_max"), sem("f_all")
        o_max, o_all = sem("o_max"), sem("o_all")
        w_scaled = sem("w_scaled")
        wt_pe, wt_hi, wt_lo = sem("wt_pe"), sem("wt_hi"), sem("wt_lo")
        ot_pe, ot_act = sem("ot_pe"), sem("ot_act")
        small_pe, small_act = sem("small_pe"), sem("small_act")
        f_hi, f_lo = sem("f_hi"), sem("f_lo")

        logits_t, u_t = route[0:1, 0:8], route[0:1, 8:16]
        r_m, r_e, r_s, r_ls = route[0:1, 16:17], route[0:1, 17:25], route[0:1, 25:26], route[0:1, 26:27]
        r_g, r_sc = route[0:1, 27:35], route[0:1, 35:43]
        r_top, r_idx = route[0:1, 43:51], route[0:1, 51:59].bitcast(U32)
        n_ops = ffn_W.shape[0]

        with nc.Block() as block:
            @block.sync
            def _(sp):
                sp.dma_start(logits_t, ffn_logits.rearrange("(a n) -> a n", a=1)).then_inc(ld_route, 16)
                sp.dma_start(u_t, ffn_u.rearrange("(a n) -> a n", a=1)).then_inc(ld_route, 16)
                sp.dma_start(g_bc, ln_g.partition_broadcast(P)).then_inc(ld_w, 16)
                sp.dma_start(b_bc, ln_b.partition_broadcast(P)).then_inc(ld_w, 16)
                sp.dma_start(w_raw, w_in.rearrange("(h d) i -> d h i", d=D)).then_inc(ld_w, 16)
                sp.dma_start(wo_raw, w_out.rearrange("(c p) n -> p c n", p=P)).then_inc(ld_wo, 16)
                sp.wait_ge(route_idx, 1)
                idx = sp.value_load(r_idx[0:1, 0:1], min_val=0, max_val=n_ops - 1)
                sp.dma_start(f_raw, ffn_W[bass.ds(idx, 1), :, :].rearrange("a (c p) n -> p (a c) n", p=P)).then_inc(ld_f, 16)
                sp.dma_start(f_last, ffn_W[bass.ds(idx, 1), DIM - 1, :].rearrange("a n -> (a n)").partition_broadcast(P)).then_inc(ld_f, 16)
                sp.wait_ge(f_sub, 1)
                sp.dma_start(f_raw[P - 1:P, CH - 1, :], ffn_b[bass.ds(idx, 1), :]).then_inc(ld_fb, 16)

            @block.gpsimd
            def _(pool):
                pool.memset(ident[:, :], 0.0).then_inc(ident_ready, 1)
                pool.wait_ge(ident_ready, 1)
                pool.affine_select(out=ident[:, :], in_=ident[:, :], compare_op=ALU.not_equal, fill=1.0, base=0,
                                   pattern=[[-1, P]], channel_multiplier=1).then_inc(ident_ready, 1)
                pool.memset(acc_q[:, :], 0.0)
                pool.memset(acc_k[:, :], 0.0)
                pool.memset(nmax[:, :], 0.0)
                pool.memset(ones[:, :], 1.0)
                pool.memset(xh[:, :, DIM - 1:DIM], XS).then_inc(const_ready, 1)
                pool.wait_ge(w_max, 1)
                pool.partition_all_reduce(col(WMAX), col(WMAXP), P, RMAX).then_inc(w_all, 1)
                pool.wait_ge(o_max, 1)
                pool.partition_all_reduce(col(OMAX), col(TMP), P, RMAX).then_inc(o_all, 1)
                pool.wait_ge(f_max, 1)
                pool.partition_all_reduce(col(FMAX), col(UP), P, RMAX).then_inc(f_all, 1)

            @block.scalar
            def _(act):
                act.dma_start(w1_raw, wp_w1).then_inc(ld_small, 16)
                act.dma_start(w2_raw[0:3, :], wp_w2).then_inc(ld_small, 16)
                act.dma_start(b1s[:, :], wp_b1.partition_broadcast(H)).then_inc(ld_small, 16)
                act.dma_start(g1s[:, :], wp_ln_g.partition_broadcast(H)).then_inc(ld_small, 16)
                act.dma_start(be1s[:, :], wp_ln_b.partition_broadcast(H)).then_inc(ld_small, 16)
                act.dma_start(b2s[:, :], wp_b2.partition_broadcast(H)).then_inc(ld_small, 16)
                act.wait_ge(route_dve, 1)
                link = chain(act, route_act)
                link(nc.scalar.activation(r_e, r_e, ACT.Exp, accum_out=r_s))
                link(nc.scalar.activation(r_ls, r_s, ACT.Ln))
                link(nc.scalar.activation(r_g, u_t, ACT.Ln))
                link(nc.scalar.activation(r_g, r_g, ACT.Ln, scale=-1.0))
                for n in range(H):
                    act.wait_ge(ot_pe, n + 1)
                    nc.scalar.activation(woT[:, n, :], banks[4 + n % 3][:, :], ACT.Copy).then_inc(ot_act, 1)
                act.wait_ge(w_scaled, 1)
                for n in range(2 * CH):
                    act.wait_ge(wt_pe, n + 1)
                    nc.scalar.activation(wh[:, n // 2, n % 2 * HW:n % 2 * HW + HW], banks[n % 4][:, :], ACT.Copy,
                                         scale=col(WS)).then_inc(wt_hi, 1)
                act.wait_ge(small_pe, 1)
                nc.scalar.activation(w1T[:, :, :], banks[7][:, 0:2 * P].rearrange("p (c n) -> p c n", c=2), ACT.Copy)
                nc.scalar.activation(w2T[:, :], banks[7][:, 2 * P:2 * P + 3], ACT.Copy).then_inc(small_act, 1)
                act.wait_ge(f_lo, 1)
                nc.scalar.activation(fh[:, :, :], f_raw, ACT.Copy, scale=col(FSC)).then_inc(f_hi, 1)
                act.wait_ge(ld_small, 96)
                act.wait_ge(f_hi, 1)

            @block.tensor
            def _(pe):
                pe.wait_ge(ident_ready, 2)
                pe.wait_ge(ld_small, 96)
                for c in range(2):
                    nc.tensor.transpose(banks[7][:, c * P:c * P + P], w1_raw[:, c * P:c * P + P], ident[:, :])
                nc.tensor.transpose(banks[7][:, 2 * P:2 * P + 3], w2_raw[0:3, :], ident[0:3, 0:3]).then_inc(small_pe, 1)
                pe.wait_ge(ld_wo, 16)
                for h in range(H):
                    if h >= 3:
                        pe.wait_ge(ot_act, h - 2)
                    for c in range(CH):
                        last = nc.tensor.transpose(banks[4 + h % 3][:, c * P:c * P + P], wo_raw[:, c, h * D:h * D + D], ident[:, :])
                    last.then_inc(ot_pe, 1)
                pe.wait_ge(w_max, 1)
                for n in range(2 * CH):
                    if n >= 4:
                        pe.wait_ge(wt_lo, n - 3)
                    for k in range(HH):
                        last = nc.tensor.transpose(banks[n % 4][:, k * P:k * P + P],
                                                   w_raw[:, n % 2 * HH + k, n // 2 * P:n // 2 * P + P], ident[:, :])
                    last.then_inc(wt_pe, 1)

            @block.vector
            def _(dve):
                for c, v in ((EPS_K, EPS / XS ** 2), (EPS_Q, EPS * EPS / XS ** 2), (EPS_1, EPS)):
                    nc.vector.memset(col(c), v)
                link = chain(dve, route_dve)
                dve.wait_ge(ld_route, 32)
                nc.vector.reduce_max(r_m, logits_t, AX.X).then_inc(w_dve, 1)
                dve.wait_ge(w_dve, 1)
                link(nc.vector.tensor_scalar(r_e, logits_t, r_m, None, ALU.subtract))
                wlink = chain(dve, w_dve, 1)
                wlink(nc.vector.tensor_scalar(r_sc, logits_t, r_m, None, ALU.subtract))
                dve.wait_ge(route_act, 4)
                wlink(nc.vector.tensor_scalar(r_sc, r_sc, r_ls, None, ALU.subtract))
                wlink(nc.vector.tensor_tensor(r_sc, r_sc, r_g, ALU.subtract))
                nc.vector.max(r_top, r_sc).then_inc(w_dve, 1)
                dve.wait_ge(w_dve, 5)
                nc.vector.max_index(r_idx, r_top, r_sc).then_inc(route_idx, 1)
                wlink = chain(dve, w_dve, 5)
                dve.wait_ge(ld_w, 48)
                for h in range(H):
                    wlink(nc.vector.tensor_tensor_reduce(out=junk, in0=w_raw[:, h, :], in1=b_bc, scale=1.0, scalar=0.0,
                                                         op0=ALU.mult, op1=ALU.add, accum_out=bias_col[:, h:h + 1]))
                g_all = g_bc.unsqueeze(1).to_broadcast([P, H, DIM])
                wlink(nc.vector.tensor_tensor(w_raw, w_raw, g_all, ALU.mult))
                wlink(nc.vector.tensor_copy(last_col, w_raw[:, :, DIM - 1]))
                for h in range(H):
                    last = nc.vector.tensor_scalar(w_raw[:, h, :], w_raw[:, h, :], last_col[:, h:h + 1], None, ALU.subtract)
                wlink(last)
                wlink(nc.vector.tensor_copy(w_raw[:, :, DIM - 1], bias_col))
                nc.vector.tensor_reduce(col(WMAXP), w_raw, AX.XY, ALU.max, apply_absolute_value=True).then_inc(w_max, 1)
                dve.wait_ge(ld_wo, 16)
                nc.vector.tensor_reduce(col(TMP), wo_raw, AX.XY, ALU.max, apply_absolute_value=True).then_inc(o_max, 1)
                dve.wait_ge(w_all, 1)
                wlink = chain(dve, w_dve, 5 + H + 4)
                power_of_two(nc.vector, wlink, col(WMAX), col(WP), col(WS), 1.0)
                wlink(nc.vector.tensor_scalar(col(INV_A), col(WP), 1.0 / XS, None, ALU.mult))
                wlink(nc.vector.tensor_tensor(col(INV_A2), col(INV_A), col(INV_A), ALU.mult))
                wlink(nc.vector.tensor_scalar(col(C_NUM), col(INV_A2), 1.0 / (D - 1), None, ALU.mult))
                wlink(nc.vector.tensor_scalar(col(C_DENK), col(C_NUM), 0.5, None, ALU.mult))
                nc.vector.tensor_scalar(col(C_DENQ), col(C_NUM), 0.5 / QR_SCALE, None, ALU.mult).then_inc(w_scaled, 1)
                for n in range(2 * CH):
                    dve.wait_ge(wt_hi, n + 1)
                    at = slice(n % 2 * HW, n % 2 * HW + HW)
                    nc.vector.scalar_tensor_tensor(out=wl[:, n // 2, at], in0=banks[n % 4][:, :], scalar=col(WS),
                                                   in1=wh[:, n // 2, at], op0=ALU.mult, op1=ALU.subtract).then_inc(wt_lo, 1)
                dve.wait_ge(ld_f, 32)
                nc.vector.tensor_tensor(f_raw, f_raw, f_last.unsqueeze(1).to_broadcast([P, CH, DIM]), ALU.subtract).then_inc(f_sub, 1)
                dve.wait_ge(ld_fb, 16)
                nc.vector.tensor_reduce(col(UP), f_raw, AX.XY, ALU.max, apply_absolute_value=True).then_inc(f_max, 1)
                dve.wait_ge(f_all, 1)
                wlink = chain(dve, w_dve, 5 + H + 4 + 8)
                power_of_two(nc.vector, wlink, col(FMAX), col(FP), col(FSC), 2.0)
                nc.vector.tensor_scalar(col(F_INV), col(FP), 1.0 / (2.0 * XS), None, ALU.mult).then_inc(f_lo, 1)
                dve.wait_ge(f_hi, 1)
                for c in range(CH):
                    last = nc.vector.scalar_tensor_tensor(out=fl[:, c, :], in0=f_raw[:, c, :], scalar=col(FSC), in1=fh[:, c, :],
                                                   op0=ALU.mult, op1=ALU.subtract)
                dve.wait_ge(o_all, 1)
                power_of_two(nc.vector, wlink, col(OMAX), col(OP), col(OS), 1.0)


        def head_view(par, n, k):
            return hb[0:n, par, :, :].rearrange("p h (e k) -> p h e k", e=2)[:, :, :, k]

        def transpose_rows(bank, src, n):
            for c in range(CH):
                last = nc.tensor.transpose(bank[:, c * P:c * P + n], src[0:n, c * P:c * P + P], ident[0:n, 0:n])
            return last

        def chunks(bank, n):
            return bank[:, :].rearrange("p (c n) -> p c n", n=P)[:, :, 0:n]

        def split_product(bank, n, hi, lo, w_hi, w_lo, start, stop):
            nc.tensor.matmul(bank[0:n, :], hi, w_hi, start=start, stop=False, skip_group_check=True)
            nc.tensor.matmul(bank[0:n, :], hi, w_lo, start=False, stop=False, skip_group_check=True)
            return nc.tensor.matmul(bank[0:n, :], lo, w_hi, start=False, stop=stop, skip_group_check=True)

        def project(bank, hi, lo, n, half):
            at = slice(half * HW, half * HW + HW)
            for c in range(CH):
                last = split_product(bank, n, hi[:, c, 0:n], lo[:, c, 0:n], wh[:, c, at], wl[:, c, at], c == 0, c == CH - 1)
            return last

        def head_stats(bank, par, n, half):
            for k in range(HH):
                last = nc.vector.bn_stats(hb[0:n, par, half * HH + k, :], bank[0:n, k * D:k * D + D])
            return last

        def head_squares(link, par, n):
            m, v, t = head_view(par, n, 1), head_view(par, n, 2), sq[0:n, :, :]
            link(nc.vector.tensor_tensor(t, m, m, ALU.mult))
            link(nc.vector.scalar_tensor_tensor(out=t, in0=t, scalar=float(D // 2), in1=v, op0=ALU.mult, op1=ALU.add))
            return nc.vector.tensor_tensor(ss[0:n, par, :], t[:, :, 0], t[:, :, 1], ALU.add)

        def ratio_parts(link, par, n):
            def part(k, e):
                return hb[0:n, par, :, 3 * e + k]
            dm, m2 = rsm[0:n, par, :], rsm[0:n, 2 + par, :]
            link(nc.gpsimd.tensor_tensor(dm, part(1, 0), part(1, 1), ALU.subtract))
            link(nc.gpsimd.tensor_tensor(dm, dm, dm, ALU.mult))
            return nc.gpsimd.tensor_tensor(m2, part(2, 0), part(2, 1), ALU.add)

        def ratio_terms(link, par, n, c_den, half_unit):
            dm, m2, num, den = rsm[0:n, par, :], rsm[0:n, 2 + par, :], rsm[0:n, 4 + par, :], rsm[0:n, 6 + par, :]
            link(nc.vector.scalar_tensor_tensor(out=m2, in0=dm, scalar=float(D // 4), in1=m2, op0=ALU.mult, op1=ALU.add))
            nc.vector.tensor_scalar(num, m2, col(C_NUM, n), 1.0, ALU.mult, ALU.min)
            link(nc.vector.tensor_scalar(den, m2, col(c_den, n), half_unit, ALU.mult, ALU.add))
            return nc.vector.reciprocal(den, den)

        def spread(v, n, heads):
            return v.unsqueeze(2).to_broadcast([n, heads, D])

        def by_head(v):
            return v.rearrange("p (h d) -> p h d", d=D)

        def rows(i):
            return slice(i * P, i * P + P) if isinstance(i, int) else bass.ds(i * P, P)

        def over_tiles(eng, first, last, head, tail, step):
            for i in range(first, first + head):
                step(i, i % 2)
            start, pairs = first + head, (last + 1 - first - head - tail) // 2
            with eng.Fori(0, pairs) as j:
                step(j * 2 + start, start % 2)
                step(j * 2 + (start + 1), (start + 1) % 2)
            for i in range(start + 2 * pairs, last + 1):
                step(i, i % 2)

        def has(i):
            return not isinstance(i, int) or 0 <= i < QT

        cv = Carve(scratch[:, :], 12000)
        xin = cv.f32(2 * DIM).rearrange("p (r d) -> p r d", r=2)
        xTh = cv.f16(2 * DIM).rearrange("p (b c n) -> p b c n", b=2, c=CH)
        xTl = cv.f16(2 * DIM).rearrange("p (b c n) -> p b c n", b=2, c=CH)
        qs = cv.f32(2 * HD).rearrange("p (b n) -> p b n", b=2)
        qc = cv.f32(2 * HD).rearrange("p (b n) -> p b n", b=2)
        qch = cv.f16(2 * HD).rearrange("p (b n) -> p b n", b=2)
        qcl = cv.f16(2 * HD).rearrange("p (b n) -> p b n", b=2)
        fsb = cv.f32(HD).rearrange("p (h d) -> p h d", h=H)

        q_ld = [sem("q_ld0"), sem("q_ld1")]
        (q_bn, q_mv, q_std, q_rinv, q_aff, q_xhat, q_acc, q_xT, q_hi, q_lo, q_proj, q_sums, q_ss, q_nrm, q_rc, q_hat,
         q_mean, q_cent, q_qch, q_qcl, q_tr, q_trc, q_fc, q_part, q_parts, q_term, q_rden, q_r, q_fev) = (sem("q_" + n) for n in (
             "bn mv std rinv aff xhat acc xT hi lo proj sums ss nrm rc hat "
             "mean cent qch qcl tr trc fc part parts term rden r fev").split())
        XT, PR, TR, FC = banks[0], banks[1:5], banks[5], banks[6:8]

        with nc.Block() as block:
            @block.sync
            def _(sp):
                def step(i, k):
                    wait(sp, q_xhat, i - 1)
                    sp.dma_start(xin[:, k, :], xf[rows(i), :]).then_inc(q_ld[k], 16)
                over_tiles(sp, 0, QT - 1, 4, 3, step)

            @block.tensor
            def _(pe):
                def turn(i, k):
                    pe.wait_ge(q_xhat, i + 1)
                    wait(pe, q_lo, i)
                    transpose_rows(XT, xh[:, k, :], P).then_inc(q_xT, 1)

                def proj(i, k, half):
                    pe.wait_ge(q_lo, i + 1)
                    wait(pe, q_cent, 2 * i + half - 3)
                    project(PR[(2 * k + half) % 4], xTh[:, k], xTl[:, k], P, half).then_inc(q_proj, 1)

                def turn_hat(i, k, half):
                    pe.wait_ge(q_hat, 2 * i + half + 1)
                    wait(pe, q_trc, 2 * i + half)
                    for n in range(HH):
                        at = half * HW + n * D
                        last = nc.tensor.transpose(TR[:, n * P:n * P + P], qs[:, k, at:at + D], ident[:, :])
                    last.then_inc(q_tr, 1)

                def correlate(i, k):
                    pe.wait_ge(q_qcl, 2 * i + 2)
                    for h in range(H):
                        at = slice(h * D, h * D + D)
                        bank = FC[h // HH][:, (h % HH) * D:(h % HH) * D + D]
                        first, end = isinstance(i, int) and i == 0 and h % HH == 0, isinstance(i, int) and i == QT - 1
                        last = split_product(bank, P, qch[:, k, at], qcl[:, k, at], qch[:, k, at], qcl[:, k, at], first, end)
                    last.then_inc(q_fc, 1)

                turn(0, 0)

                def step(i, k):
                    if has(i + 1):
                        turn(i + 1, 1 - k)
                    proj(i, k, 0)
                    if has(i - 2):
                        correlate(i - 2, k)
                    if has(i - 1):
                        turn_hat(i - 1, 1 - k, 0)
                    proj(i, k, 1)
                    if has(i - 1):
                        turn_hat(i - 1, 1 - k, 1)
                over_tiles(pe, 0, QT - 1, 4, 3, step)
                turn_hat(QT - 1, (QT - 1) % 2, 0)
                turn_hat(QT - 1, (QT - 1) % 2, 1)
                correlate(QT - 2, (QT - 2) % 2)
                correlate(QT - 1, (QT - 1) % 2)

            @block.scalar
            def _(act):
                def deviation(i, k):
                    act.wait_ge(q_mv, i + 1)
                    nc.scalar.activation(std[:, k:k + 1], mv[:, k, 1:2], ACT.Sqrt, bias=col(EPS_Q),
                                         scale=(1.0 + EPS) / XS ** 2).then_inc(q_std, 1)

                def normalise(i, k):
                    act.wait_ge(q_aff, i + 1)
                    wait(act, q_xT, i - 1)
                    wait(act, q_acc, i - 1)
                    nc.scalar.activation(xh[:, k, 0:DIM - 1], xin[:, k, 0:DIM - 1], ACT.Identity, bias=aff[:, k, 1:2],
                                         scale=aff[:, k, 0:1]).then_inc(q_xhat, 1)

                def high(i, k):
                    act.wait_ge(q_xT, i + 1)
                    wait(act, q_proj, 2 * i - 2)
                    nc.scalar.activation(xTh[:, k], chunks(XT, P), ACT.Copy).then_inc(q_hi, 1)

                def norm(i, k):
                    act.wait_ge(q_ss, i + 1)
                    nc.scalar.activation(nrm[:, k, :], ss[:, k, :], ACT.Sqrt).then_inc(q_nrm, 1)

                def hat_out(i, k, half):
                    act.wait_ge(q_tr, 2 * i + half + 1)
                    nc.scalar.activation(qu[:, half * HH:half * HH + HH, rows(i)], by_head(TR[:, :]), ACT.Copy).then_inc(q_trc, 1)

                def centred_high(i, k, half):
                    act.wait_ge(q_cent, 2 * i + half + 1)
                    wait(act, q_fc, i - 1)
                    at = slice(half * HW, half * HW + HW)
                    nc.scalar.activation(qch[:, k, at], qc[:, k, at], ACT.Copy).then_inc(q_qch, 1)

                for i in range(2):
                    deviation(i, i)
                    normalise(i, i)
                high(0, 0)

                def step(i, k):
                    if has(i - 1):
                        norm(i - 1, 1 - k)
                    if has(i + 2):
                        deviation(i + 2, k)
                    if has(i + 1):
                        high(i + 1, 1 - k)
                    if has(i + 2):
                        normalise(i + 2, k)
                    if has(i - 1):
                        hat_out(i - 1, 1 - k, 0)
                        centred_high(i - 1, 1 - k, 0)
                        centred_high(i - 1, 1 - k, 1)
                        hat_out(i - 1, 1 - k, 1)
                over_tiles(act, 0, QT - 1, 4, 3, step)
                i, k = QT - 1, (QT - 1) % 2
                norm(i, k)
                for half in range(2):
                    centred_high(i, k, half)
                for half in range(2):
                    hat_out(i, k, half)

            @block.gpsimd
            def _(pool):
                def sum_rows(i, k):
                    pool.wait_ge(q_xhat, i + 1)
                    wait(pool, q_acc, i)
                    nc.gpsimd.tensor_tensor(acc_q[:, :], acc_q[:, :], xh[:, k, :], ALU.add).then_inc(q_acc, 1)

                def parts(i, k):
                    pool.wait_ge(q_ss, i + 1)
                    wait(pool, q_r, i - 1)
                    ratio_parts(chain(pool, q_part, i * 2), k, P).then_inc(q_parts, 1)

                def ratio(i, k):
                    pool.wait_ge(q_rden, i + 1)
                    dst = qr[:, i, :] if isinstance(i, int) else qr[:, bass.ds(i, 1), :].rearrange("p a h -> p (a h)")
                    nc.gpsimd.tensor_tensor(dst, rsm[:, 4 + k, :], rsm[:, 6 + k, :], ALU.mult).then_inc(q_r, 1)

                def centred_low(i, k, half):
                    pool.wait_ge(q_qch, 2 * i + half + 1)
                    at = slice(half * HW, half * HW + HW)
                    nc.gpsimd.tensor_tensor(qcl[:, k, at], qc[:, k, at], qch[:, k, at], ALU.subtract).then_inc(q_qcl, 1)

                sum_rows(0, 0)

                def step(i, k):
                    if has(i - 1):
                        parts(i - 1, 1 - k)
                    if has(i + 1):
                        sum_rows(i + 1, 1 - k)
                    if has(i - 1):
                        centred_low(i - 1, 1 - k, 0)
                        centred_low(i - 1, 1 - k, 1)
                        ratio(i - 1, 1 - k)
                over_tiles(pool, 0, QT - 1, 4, 3, step)
                i, k = QT - 1, (QT - 1) % 2
                parts(i, k)
                centred_low(i, k, 0)
                centred_low(i, k, 1)
                ratio(i, k)

            @block.vector
            def _(dve):
                def moments(i, k):
                    dve.wait_ge(q_ld[k], (i - k) * 8 + 16)
                    nc.vector.bn_stats(bst[:, k, :], xin[:, k, :]).then_inc(q_bn, 1)
                    dve.wait_ge(q_bn, i + 1)
                    nc.vector.tensor_copy(bcnt[:, :], bst[:, k, 0:1])
                    nc.vector.bn_aggr(mv[:, k, :], bst[:, k, :]).then_inc(q_mv, 1)

                def affine(i, k):
                    dve.wait_ge(q_std, i + 1)
                    wait(dve, q_xhat, i - 1)
                    nc.vector.reciprocal(aff[:, k, 0:1], std[:, k:k + 1]).then_inc(q_rinv, 1)
                    dve.wait_ge(q_rinv, i + 1)
                    nc.vector.tensor_scalar(aff[:, k, 1:2], mv[:, k, 0:1], aff[:, k, 0:1], -1.0, ALU.mult, ALU.mult).then_inc(q_aff, 1)

                def rest(i, k):
                    dve.wait_ge(q_hi, i + 1)
                    nc.vector.tensor_tensor(xTl[:, k], chunks(XT, P), xTh[:, k], ALU.subtract).then_inc(q_lo, 1)

                def stats(i, k, half):
                    dve.wait_ge(q_proj, 2 * i + half + 1)
                    wait(dve, q_parts, i - 1)
                    last = head_stats(PR[(2 * k + half) % 4], k, P, half)
                    if half == 1:
                        link = chain(dve, q_sums, i * 3)
                        link(last)
                        head_squares(link, k, P).then_inc(q_ss, 1)

                def hats(i, k):
                    dve.wait_ge(q_nrm, i + 1)
                    nc.vector.reciprocal(rc[:, k, :], nrm[:, k, :]).then_inc(q_rc, 1)
                    dve.wait_ge(q_rc, i + 1)
                    for half in range(2):
                        J = 2 * i + half
                        bank, at, hs = by_head(PR[(2 * k + half) % 4][:, :]), slice(half * HW, half * HW + HW), slice(half * HH, half * HH + HH)
                        wait(dve, q_tr, J - 3)
                        nc.vector.tensor_tensor(by_head(qs[:, k, at]), bank, spread(rc[:, k, hs], P, HH), ALU.mult).then_inc(q_hat, 1)

                def centre(i, k):
                    nc.vector.tensor_tensor(mean2[:, :], hb[:, k, :, 1], hb[:, k, :, 4], ALU.add).then_inc(q_mean, 1)
                    dve.wait_ge(q_mean, i + 1)
                    for half in range(2):
                        J = 2 * i + half
                        bank, at, hs = by_head(PR[(2 * k + half) % 4][:, :]), slice(half * HW, half * HW + HW), slice(half * HH, half * HH + HH)
                        wait(dve, q_qcl, J - 3)
                        nc.vector.scalar_tensor_tensor(out=by_head(qc[:, k, at]), in0=bank, scalar=2.0, in1=spread(mean2[:, hs], P, HH),
                                                       op0=ALU.mult, op1=ALU.subtract).then_inc(q_cent, 1)

                def invert(i, k):
                    dve.wait_ge(q_parts, i + 1)
                    ratio_terms(chain(dve, q_term, i * 2), k, P, C_DENQ, 0.5 / QR_SCALE).then_inc(q_rden, 1)

                for i in range(2):
                    moments(i, i)
                    affine(i, i)
                rest(0, 0)

                def step(i, k):
                    if has(i + 2):
                        moments(i + 2, k)
                    if has(i - 1):
                        hats(i - 1, 1 - k)
                    if has(i + 2):
                        affine(i + 2, k)
                    if has(i - 1):
                        centre(i - 1, 1 - k)
                    if has(i + 1):
                        rest(i + 1, 1 - k)
                    stats(i, k, 0)
                    if has(i - 1):
                        invert(i - 1, 1 - k)
                    stats(i, k, 1)
                over_tiles(dve, 0, QT - 1, 4, 3, step)
                i, k = QT - 1, (QT - 1) % 2
                hats(i, k)
                centre(i, k)
                invert(i, k)
                link = chain(dve, q_fev)
                dve.wait_ge(q_fc, QT)
                for g in range(2):
                    link(nc.vector.scalar_tensor_tensor(out=fsb[:, g * HH:g * HH + HH, :], in0=ident[:, :].unsqueeze(1).to_broadcast([P, HH, D]),
                                                        scalar=-1.0, in1=by_head(FC[g][:, :]), op0=ALU.add, op1=ALU.mult))
                link(nc.vector.tensor_tensor(fsb, fsb, fsb, ALU.mult))
                link(nc.vector.tensor_reduce(fs[:, :], fsb, AX.X, ALU.add))

        cv = Carve(scratch[:, :], 12000)
        cin = cv.f32(KT * DIM).rearrange("p (t d) -> p t d", t=KT)
        kTh = cv.f16(2 * DIM).rearrange("p (b c n) -> p b c n", b=2, c=CH)
        kTl = cv.f16(2 * DIM).rearrange("p (b c n) -> p b c n", b=2, c=CH)
        ks = cv.f32(2 * HD).rearrange("p (b n) -> p b n", b=2)
        kh = cv.f16(2 * H * MC).rearrange("p (b h m) -> p b h m", b=2, h=H)
        kl = cv.f16(2 * HD).rearrange("p (b h d) -> p b h d", b=2, h=H)
        msb = cv.f32(H * MC).rearrange("p (h m) -> p h m", h=H)

        k_ld = [sem(f"k_ld{t}") for t in range(KT)]
        (k_bn, k_mv, k_std, k_rinv, k_aff, k_xhat, k_acc, k_xT, k_hi, k_lo, k_proj, k_sums, k_ss, k_nrm, k_rt, k_rc, k_kt,
         k_khi, k_klo, k_part, k_parts, k_term, k_rden, k_rstep, k_r, k_m, k_mev, k_sum, k_u, k_uev) = (sem("k_" + n) for n in (
             "bn mv std rinv aff xhat acc xT hi lo proj sums ss nrm rt rc kt "
             "khi klo part parts term rden rstep r m mev sum u uev").split())
        XT, PR, MM, UU = banks[0], banks[1:4], banks[4:7], banks[7]
        FULL = (KT - 1) * P

        def size(t):
            return P if t % KT < KT - 1 else KLAST

        def over_batches(eng, batch):
            batch(0)
            with eng.Fori(1, NB - 1) as b:
                batch(b)
            batch(NB - 1)

        def there(b, t):
            return not isinstance(b, int) or 0 <= b * KT + t < NKT

        def one(b):
            return slice(b, b + 1) if isinstance(b, int) else bass.ds(b, 1)

        with nc.Block() as block:
            @block.sync
            def _(sp):
                def batch(b):
                    for t in range(KT):
                        wait(sp, k_xhat, b * KT + (t - KT + 1))
                        if t < KT - 1:
                            src = ctx_1024[one(b), 0:FULL, :].rearrange("a (p j) d -> p (a j) d", j=KT - 1)[:, t, :]
                        else:
                            src = ctx_1024[one(b), FULL:NK, :].rearrange("a p d -> (a p) d")
                        sp.dma_start(cin[0:size(t), t, :], src).then_inc(k_ld[t], 16)
                over_batches(sp, batch)

            @block.tensor
            def _(pe):
                def turn(b, t):
                    T, n = b * KT + t, size(t)
                    pe.wait_ge(k_xhat, T + 1)
                    wait(pe, k_lo, T)
                    transpose_rows(XT, xh[:, t % 2, :], n).then_inc(k_xT, 1)

                def proj(b, t, half):
                    T, n = b * KT + t, size(t)
                    pe.wait_ge(k_lo, T + 1)
                    wait(pe, k_kt, 2 * T + half - 2)
                    project(PR[(2 * t + half) % 3], kTh[:, t % 2], kTl[:, t % 2], n, half).then_inc(k_proj, 1)

                def outer(b, t):
                    T, n, k = b * KT + t, size(t), t % 2
                    pe.wait_ge(k_klo, 2 * T + 2)
                    pe.wait_ge(k_r, T + 1)
                    if t % KT == 0:
                        wait(pe, k_mev, b + t // KT)
                    for h in range(H):
                        bank, at = MM[h // MB], h % MB * MC
                        hi, lo = kh[0:n, k, h, 0:D], kl[0:n, k, h, :]
                        end = t % KT == KT - 1
                        nc.tensor.matmul(bank[:, at:at + MC], hi, kh[0:n, k, h, :], start=(t % KT == 0 and h % MB == 0), stop=False,
                                         skip_group_check=True)
                        nc.tensor.matmul(bank[:, at:at + D], hi, lo, start=False, stop=False, skip_group_check=True)
                        last = nc.tensor.matmul(bank[:, at:at + D + 1], lo, kh[0:n, k, h, 0:D + 1], start=False, stop=end,
                                                skip_group_check=True)
                    last.then_inc(k_m, 1)

                def apply(b, g):
                    pe.wait_ge(k_mev, b + 1)
                    wait(pe, k_uev, 2 * b + g)
                    for n in range(HH):
                        h = g * HH + n
                        at = slice(b * NQ, b * NQ + NQ) if isinstance(b, int) else bass.ds(b * NQ, NQ)
                        last = nc.tensor.matmul(UU[:, n * NQ:n * NQ + NQ], msb[:, h, 0:D], qu[:, h, at], start=True, stop=True,
                                                skip_group_check=True)
                    last.then_inc(k_u, 1)

                turn(0, 0)

                def batch(b):
                    for t in range(KT):
                        if there(b, t + 1):
                            turn(b, t + 1)
                        proj(b, t, 0)
                        if there(b, t - 2):
                            outer(b, t - 2)
                        proj(b, t, 1)
                        if t in (2, 3) and there(b, t - KT):
                            apply(b - 1, t - 2)
                over_batches(pe, batch)
                outer(NB - 1, KT - 2)
                outer(NB - 1, KT - 1)
                apply(NB - 1, 0)
                apply(NB - 1, 1)

            @block.scalar
            def _(act):
                def deviation(b, t):
                    T, n, k = b * KT + t, size(t), t % 2
                    act.wait_ge(k_mv, T + 1)
                    nc.scalar.activation(std[0:n, k:k + 1], mv[0:n, k, 1:2], ACT.Sqrt, bias=col(EPS_K, n),
                                         scale=1.0 / XS ** 2).then_inc(k_std, 1)

                def normalise(b, t):
                    T, n, k = b * KT + t, size(t), t % 2
                    act.wait_ge(k_aff, T + 1)
                    wait(act, k_xT, T - 1)
                    wait(act, k_acc, T - 1)
                    nc.scalar.activation(xh[0:n, k, 0:DIM - 1], cin[0:n, t % KT, 0:DIM - 1], ACT.Identity, bias=aff[0:n, k, 1:2],
                                         scale=aff[0:n, k, 0:1]).then_inc(k_xhat, 1)

                def high(b, t):
                    T, n, k = b * KT + t, size(t), t % 2
                    act.wait_ge(k_xT, T + 1)
                    wait(act, k_proj, 2 * T - 2)
                    nc.scalar.activation(kTh[:, k, :, 0:n], chunks(XT, n), ACT.Copy).then_inc(k_hi, 1)

                def roots(b, t):
                    T, n, k = b * KT + t, size(t), t % 2
                    act.wait_ge(k_ss, T + 1)
                    nc.scalar.activation(nrm[0:n, k, :], ss[0:n, k, :], ACT.Sqrt).then_inc(k_nrm, 1)
                    act.wait_ge(k_nrm, T + 1)
                    wait(act, k_r, T - 1)
                    nc.scalar.activation(rt[0:n, k, :], nrm[0:n, k, :], ACT.Sqrt).then_inc(k_rt, 1)

                def k_high(b, t, half):
                    T, n, k = b * KT + t, size(t), t % 2
                    act.wait_ge(k_kt, 2 * T + half + 1)
                    wait(act, k_m, T - 1)
                    hs = slice(half * HH, half * HH + HH)
                    nc.scalar.activation(kh[0:n, k, hs, 0:D], by_head(ks[0:n, k, half * HW:half * HW + HW]), ACT.Copy).then_inc(k_khi, 1)

                def m_out(b):
                    act.wait_ge(k_m, (b + 1) * KT)
                    wait(act, k_u, 2 * b)
                    wait(act, k_sum, b)
                    for g, bank in enumerate(MM):
                        hs = slice(g * MB, min(g * MB + MB, H))
                        w = (hs.stop - hs.start) * MC
                        last = nc.scalar.activation(msb[:, hs, :], bank[:, 0:w].rearrange("p (h m) -> p h m", m=MC), ACT.Copy)
                    last.then_inc(k_mev, 1)

                def u_out(b, g):
                    act.wait_ge(k_u, 2 * b + g + 1)
                    at = slice(b * NQ, b * NQ + NQ) if isinstance(b, int) else bass.ds(b * NQ, NQ)
                    nc.scalar.activation(qu[:, g * HH:g * HH + HH, at], UU[:, 0:HH * NQ].rearrange("p (h n) -> p h n", h=HH),
                                         ACT.Copy).then_inc(k_uev, 1)

                for t in range(2):
                    deviation(0, t)
                    normalise(0, t)
                high(0, 0)

                def batch(b):
                    for t in range(KT):
                        if there(b, t - 1):
                            roots(b, t - 1)
                        if there(b, t + 2):
                            deviation(b, t + 2)
                        if there(b, t + 1):
                            high(b, t + 1)
                        if there(b, t + 2):
                            normalise(b, t + 2)
                        if there(b, t - 1):
                            k_high(b, t - 1, 0)
                            k_high(b, t - 1, 1)
                        if t == 1 and there(b, t - KT):
                            m_out(b - 1)
                        if t in (3, 4) and there(b, t - KT):
                            u_out(b - 1, t - 3)
                over_batches(act, batch)
                roots(NB - 1, KT - 1)
                k_high(NB - 1, KT - 1, 0)
                k_high(NB - 1, KT - 1, 1)
                m_out(NB - 1)
                u_out(NB - 1, 0)
                u_out(NB - 1, 1)

            @block.gpsimd
            def _(pool):
                def sum_rows(b, t):
                    T, n, k = b * KT + t, size(t), t % 2
                    pool.wait_ge(k_xhat, T + 1)
                    wait(pool, k_acc, T)
                    nc.gpsimd.tensor_tensor(acc_k[0:n, :], acc_k[0:n, :], xh[0:n, k, :], ALU.add).then_inc(k_acc, 1)

                def parts(b, t):
                    T, n, k = b * KT + t, size(t), t % 2
                    pool.wait_ge(k_ss, T + 1)
                    ratio_parts(chain(pool, k_part, T * 2), k, n).then_inc(k_parts, 1)

                def ratio(b, t):
                    T, n, k = b * KT + t, size(t), t % 2
                    link = chain(pool, k_rstep, T * 3)
                    r = rsm[0:n, 8, :]
                    pool.wait_ge(k_rden, T + 1)
                    wait(pool, k_m, T - 1)
                    link(nc.gpsimd.tensor_tensor(r, rsm[0:n, 4 + k, :], rsm[0:n, 6 + k, :], ALU.mult))
                    link(nc.gpsimd.tensor_tensor(r, r, rt[0:n, k, :], ALU.mult))
                    link(nc.gpsimd.tensor_tensor(kh[0:n, k, :, D], r, ones[0:n, 0:H], ALU.mult))
                    nc.gpsimd.tensor_tensor(kh[0:n, k, :, D + 1], r, kh[0:n, k, :, D], ALU.subtract).then_inc(k_r, 1)

                def k_low(b, t, half):
                    T, n, k = b * KT + t, size(t), t % 2
                    hs = slice(half * HH, half * HH + HH)
                    pool.wait_ge(k_khi, 2 * T + half + 1)
                    nc.gpsimd.tensor_tensor(kl[0:n, k, hs, :], by_head(ks[0:n, k, half * HW:half * HW + HW]), kh[0:n, k, hs, 0:D],
                                            ALU.subtract).then_inc(k_klo, 1)

                sum_rows(0, 0)

                def batch(b):
                    for t in range(KT):
                        if there(b, t - 1):
                            parts(b, t - 1)
                        if there(b, t + 1):
                            sum_rows(b, t + 1)
                        if there(b, t - 1):
                            k_low(b, t - 1, 0)
                            ratio(b, t - 1)
                            k_low(b, t - 1, 1)
                over_batches(pool, batch)
                parts(NB - 1, KT - 1)
                k_low(NB - 1, KT - 1, 0)
                ratio(NB - 1, KT - 1)
                k_low(NB - 1, KT - 1, 1)

            @block.vector
            def _(dve):
                def moments(b, t):
                    T, n, k = b * KT + t, size(t), t % 2
                    dve.wait_ge(k_ld[t % KT], (b + t // KT) * 16 + 16)
                    nc.vector.bn_stats(bst[0:n, k, :], cin[0:n, t % KT, :]).then_inc(k_bn, 1)
                    dve.wait_ge(k_bn, T + 1)
                    nc.vector.tensor_copy(bcnt[0:n, :], bst[0:n, k, 0:1])
                    nc.vector.bn_aggr(mv[0:n, k, :], bst[0:n, k, :]).then_inc(k_mv, 1)

                def affine(b, t):
                    T, n, k = b * KT + t, size(t), t % 2
                    dve.wait_ge(k_std, T + 1)
                    wait(dve, k_xhat, T - 1)
                    nc.vector.reciprocal(aff[0:n, k, 0:1], std[0:n, k:k + 1]).then_inc(k_rinv, 1)
                    dve.wait_ge(k_rinv, T + 1)
                    nc.vector.tensor_scalar(aff[0:n, k, 1:2], mv[0:n, k, 0:1], aff[0:n, k, 0:1], -1.0, ALU.mult, ALU.mult).then_inc(k_aff, 1)

                def rest(b, t):
                    T, n, k = b * KT + t, size(t), t % 2
                    dve.wait_ge(k_hi, T + 1)
                    nc.vector.tensor_tensor(kTl[:, k, :, 0:n], chunks(XT, n), kTh[:, k, :, 0:n], ALU.subtract).then_inc(k_lo, 1)

                def stats(b, t, half):
                    T, n, k = b * KT + t, size(t), t % 2
                    dve.wait_ge(k_proj, 2 * T + half + 1)
                    wait(dve, k_parts, T - 1)
                    last = head_stats(PR[(2 * t + half) % 3], k, n, half)
                    if half == 1:
                        link = chain(dve, k_sums, T * 3)
                        link(last)
                        head_squares(link, k, n).then_inc(k_ss, 1)

                def tilde(b, t):
                    T, n, k = b * KT + t, size(t), t % 2
                    dve.wait_ge(k_rt, T + 1)
                    nc.vector.reciprocal(rc[0:n, k, :], rt[0:n, k, :]).then_inc(k_rc, 1)
                    dve.wait_ge(k_rc, T + 1)
                    for half in range(2):
                        hs = slice(half * HH, half * HH + HH)
                        wait(dve, k_klo, 2 * T + half - 3)
                        nc.vector.tensor_tensor(by_head(ks[0:n, k, half * HW:half * HW + HW]), by_head(PR[(2 * t + half) % 3][0:n, :]),
                                                spread(rc[0:n, k, hs], n, HH), ALU.mult).then_inc(k_kt, 1)

                def invert(b, t):
                    T, n, k = b * KT + t, size(t), t % 2
                    dve.wait_ge(k_parts, T + 1)
                    ratio_terms(chain(dve, k_term, T * 2), k, n, C_DENK, 0.5).then_inc(k_rden, 1)
                    nc.vector.tensor_tensor(nmax[0:n, :], nmax[0:n, :], nrm[0:n, k, :], ALU.max)

                def sum_out(b):
                    dve.wait_ge(k_mev, b + 1)
                    dst = ksum[:, :, one(b)].rearrange("p h a -> p (h a)")
                    nc.vector.tensor_tensor(dst, msb[:, :, D], msb[:, :, D + 1], ALU.add).then_inc(k_sum, 1)

                for t in range(2):
                    moments(0, t)
                    affine(0, t)
                rest(0, 0)

                def batch(b):
                    for t in range(KT):
                        if there(b, t + 2):
                            moments(b, t + 2)
                        if there(b, t - 1):
                            tilde(b, t - 1)
                        if there(b, t + 2):
                            affine(b, t + 2)
                        if there(b, t + 1):
                            rest(b, t + 1)
                        stats(b, t, 0)
                        if there(b, t - 1):
                            invert(b, t - 1)
                        if t == 3 and there(b, t - KT):
                            sum_out(b - 1)
                        stats(b, t, 1)
                over_batches(dve, batch)
                tilde(NB - 1, KT - 1)
                invert(NB - 1, KT - 1)
                sum_out(NB - 1)

        cv = Carve(scratch[:, :], 12000)
        qh = cv.f16(NG * QG).rearrange("p (g n) -> p g n", g=NG)
        ql = cv.f16(NG * QG).rearrange("p (g n) -> p g n", g=NG)
        rh = cv.f16(NG * DIM).rearrange("p (g n) -> p g n", g=NG)
        rl = cv.f16(NG * DIM).rearrange("p (g n) -> p g n", g=NG)
        keep = cv.at
        qth = cv.f16(NR)
        qtl = cv.f16(NR)
        smask = cv.f32(H * NG * P).rearrange("p (h g b k) -> p h g b k", h=H, g=NG, k=H)
        xm = cv.f32(2 * CH).rearrange("p (k c) -> p k c", k=2)
        xmh = cv.f16(2 * CH).rearrange("p (k c) -> p k c", k=2)
        xml = cv.f16(2 * CH).rearrange("p (k c) -> p k c", k=2)
        feat = cv.f32(2 * H).rearrange("p (k h) -> p k h", k=2)
        h1 = cv.f32(P)
        h1T = cv.f32(H)
        sm = cv.f32(32)
        diag = cv.f32(2 * H).rearrange("p (k h) -> p k h", k=2)
        aw = cv.f32(2 * H).rearrange("p (k h) -> p k h", k=2)
        x_zero, x_qt, x_qth, x_qtl, x_bd = (sem("x_" + n) for n in "zero qt qth qtl bd".split())
        x_pe, x_act, x_dve, x_umax, x_a, x_smask, x_rb, x_rh, x_rl, x_oh, x_ol = (
            sem("x_" + n) for n in "pe act dve umax a smask rb rh rl oh ol".split())
        QB = 4
        NQB = -(-QT // QB)

        with nc.Block() as block:
            @block.sync
            def _(sp):
                sp.wait_ge(x_zero, 1)
                sp.wait_ge(x_qtl, NQB)
                for src, dst in ((qth, qh), (qtl, ql)):
                    for b in range(NB):
                        g, p0 = b // BH, b % BH * H
                        at = b * NQ - g * G1
                        sp.dma_start(dst[p0:p0 + H, g, at:at + NQ], src[0:H, b * NQ:b * NQ + NQ]).then_inc(x_bd, 16)
                sp.wait_ge(x_bd, 16 * 2 * NB)

            @block.gpsimd
            def _(pool):
                pool.memset(qh, 0.0)
                pool.memset(ql, 0.0).then_inc(x_zero, 1)
                pool.memset(smask, 0.0).then_inc(x_smask, 1)
                pool.wait_ge(x_umax, 1)
                pool.partition_all_reduce(col(UMAX), col(TMP), P, RMAX).then_inc(x_umax, 1)

            @block.tensor
            def _(pe):
                for c in range(CH):
                    for k, acc in enumerate((acc_q, acc_k)):
                        last = nc.tensor.matmul(banks[0][:, k * CH + c:k * CH + c + 1], acc[:, c * P:c * P + P], ones[:, 0:1],
                                                start=True, stop=True, skip_group_check=True)
                last.then_inc(x_pe, 1)
                nc.tensor.matmul(banks[1][0:H, 0:1], fs[:, :], ones[:, 0:1], start=True, stop=True).then_inc(x_pe, 1)
                pe.wait_ge(x_dve, 3)
                for h in range(H):
                    for c in range(CH):
                        at, dst = slice(h * D, h * D + D), banks[2][:, 2 * h:2 * h + 2]
                        nc.tensor.matmul(dst, wh[:, c, at], xmh[:, :, c], start=(c == 0 and h == 0), stop=False, skip_group_check=True)
                        nc.tensor.matmul(dst, wh[:, c, at], xml[:, :, c], start=False, stop=False, skip_group_check=True)
                        last = nc.tensor.matmul(dst, wl[:, c, at], xmh[:, :, c], start=False, stop=(c == CH - 1), skip_group_check=True)
                last.then_inc(x_pe, 1)
                pe.wait_ge(x_dve, 4)
                for k in range(2):
                    last = nc.tensor.matmul(banks[3][0:H, 0:P], feat[:, k, :], w1T[:, k, :], start=(k == 0), stop=(k == 1))
                last.then_inc(x_pe, 1)
                for q in range(NQB):
                    if q >= 2:
                        pe.wait_ge(x_qtl, q - 1)
                    for i in range(q * QB, min(q * QB + QB, QT)):
                        last = nc.tensor.transpose(banks[6 + q % 2][0:H, (i % QB) * P:(i % QB) * P + P], qr[:, i, :], ident[:, :])
                    last.then_inc(x_qt, 1)
                pe.wait_ge(x_a, 1)
                nc.tensor.transpose(banks[4][:, 0:H], h1[0:H, :], ident[0:H, 0:H]).then_inc(x_pe, 1)
                pe.wait_ge(x_a, 2)
                nc.tensor.matmul(banks[5][0:H, 0:3], h1T, w2T[:, :], start=True, stop=True).then_inc(x_pe, 1)
                pe.wait_ge(x_a, 3)
                nc.tensor.matmul(banks[0][:, 0:2 * H], ones[0:H, :], diag[0:H].rearrange("p k h -> p (k h)"), start=True, stop=True).then_inc(x_pe, 1)
                pe.wait_ge(x_smask, 2)
                for g in range(NG):
                    for h in range(H):
                        last = nc.tensor.matmul(banks[1 + g][:, :], smask[:, h, g].rearrange("p b k -> p (b k)"), woT[:, h, :],
                                                start=(h == 0), stop=(h == H - 1))
                    last.then_inc(x_rb, 1)

            @block.scalar
            def _(act):
                link = chain(act, x_act)
                act.wait_ge(x_pe, 2)
                link(nc.scalar.activation(sm[0:H, 0:1], banks[1][0:H, 0:1], ACT.Sqrt))
                for q in range(NQB):
                    act.wait_ge(x_qt, q + 1)
                    w = min(QB, QT - q * QB) * P
                    nc.scalar.activation(qth[0:H, q * QB * P:q * QB * P + w], banks[6 + q % 2][0:H, 0:w], ACT.Copy).then_inc(x_qth, 1)
                act.wait_ge(x_dve, 9)
                link(nc.scalar.activation(sm[0:H, 3:4], sm[0:H, 2:3], ACT.Sqrt, bias=col(EPS_1, H)))
                act.wait_ge(x_dve, 15)
                link(nc.scalar.activation(sm[0:H, 16:19], sm[0:H, 8:11], ACT.Exp, accum_out=sm[0:H, 5:6]))
                link(nc.scalar.activation(sm[0:H, 6:7], sm[0:H, 1:2], ACT.Exp, scale=-5.0 / (4.0 * NR * D * D)))
                act.wait_ge(x_ol, 1)
                for h in range(H):
                    nc.scalar.activation(wh[:, h // 2, h % 2 * DIM:h % 2 * DIM + DIM], woT[:, h, :], ACT.Copy,
                                         scale=aw[:, 0, h:h + 1]).then_inc(x_oh, 1)
                for g in range(NG):
                    act.wait_ge(x_rb, g + 1)
                    nc.scalar.activation(rh[:, g, :], banks[1 + g][:, :], ACT.Copy).then_inc(x_rh, 1)

            @block.vector
            def _(dve):
                v = nc.vector
                link = chain(dve, x_dve)
                dve.wait_ge(x_pe, 1)
                for k, n in enumerate((NR, NB * NK)):
                    last = v.tensor_scalar(xm[:, k, :], banks[0][:, k * CH:k * CH + CH], 1.0 / n, None, ALU.mult)
                link(last)
                link(v.tensor_copy(xmh, xm))
                link(v.tensor_tensor(xml, xm, xmh, ALU.subtract))
                v.tensor_reduce(col(TMP), nmax[:, :], AX.X, ALU.max).then_inc(x_umax, 1)
                dve.wait_ge(x_pe, 3)
                link(v.tensor_scalar(feat, banks[2][:, 0:2 * H].rearrange("p (h k) -> p k h", k=2), col(INV_A), None, ALU.mult))
                for q in range(NQB):
                    dve.wait_ge(x_qth, q + 1)
                    at, w = q * QB * P, min(QB, QT - q * QB) * P
                    v.tensor_tensor(qtl[0:H, at:at + w], banks[6 + q % 2][0:H, 0:w], qth[0:H, at:at + w], ALU.subtract).then_inc(x_qtl, 1)
                dve.wait_ge(x_pe, 4)
                link(v.tensor_tensor(h1[0:H, :], banks[3][0:H, 0:P], b1s[:, :], ALU.add))
                link(v.bn_stats(sm[0:H, 20:26], h1[0:H, :]))
                link(v.bn_aggr(sm[0:H, 26:28], sm[0:H, 20:26]))
                link(v.tensor_copy(sm[0:H, 2:3], sm[0:H, 27:28]))
                dve.wait_ge(x_act, 1)
                link(v.tensor_scalar(sm[0:H, 1:2], sm[0:H, 0:1], col(INV_A2, H), None, ALU.mult))
                dve.wait_ge(x_act, 2)
                link(v.reciprocal(sm[0:H, 4:5], sm[0:H, 3:4]))
                link(v.tensor_scalar(h1[0:H, :], h1[0:H, :], sm[0:H, 26:27], sm[0:H, 4:5], ALU.subtract, ALU.mult))
                link(v.tensor_tensor(h1[0:H, :], h1[0:H, :], g1s[:, :], ALU.mult))
                link(v.tensor_tensor(h1[0:H, :], h1[0:H, :], be1s[:, :], ALU.add))
                v.tensor_scalar(h1[0:H, :], h1[0:H, :], 0.0, None, ALU.max).then_inc(x_a, 1)
                dve.wait_ge(x_pe, 5)
                v.tensor_copy(h1T, banks[4][:, 0:H]).then_inc(x_a, 1)
                dve.wait_ge(x_pe, 6)
                link(v.tensor_tensor(sm[0:H, 8:11], banks[5][0:H, 0:3], b2s[:, :], ALU.add))
                link2 = chain(dve, x_ol, 0)
                x_soft = sem("x_soft")
                link3 = chain(dve, x_soft)
                link3(v.reduce_max(sm[0:H, 7:8], sm[0:H, 8:11], AX.X))
                link(v.tensor_scalar(sm[0:H, 8:11], sm[0:H, 8:11], sm[0:H, 7:8], None, ALU.subtract))
                dve.wait_ge(x_act, 4)
                link3(v.reciprocal(sm[0:H, 11:12], sm[0:H, 5:6]))
                link3(v.tensor_scalar(sm[0:H, 16:19], sm[0:H, 16:19], sm[0:H, 11:12], None, ALU.mult))
                link3(v.scalar_tensor_tensor(out=sm[0:H, 19:20], in0=sm[0:H, 17:18], scalar=sm[0:H, 6:7], in1=sm[0:H, 16:17],
                                             op0=ALU.mult, op1=ALU.add))
                v.tensor_scalar(diag[0:H, 0, :], ident[0:H, 0:H], sm[0:H, 19:20], 0.5, ALU.mult, ALU.mult)
                v.tensor_scalar(diag[0:H, 1, :], ident[0:H, 0:H], sm[0:H, 18:19], 0.5, ALU.mult, ALU.mult).then_inc(x_a, 1)
                dve.wait_ge(x_umax, 2)
                link3(v.tensor_scalar(col(UMAX), col(UMAX), float(NK), None, ALU.mult))
                power_of_two(v, link3, col(UMAX), col(UP), col(US), 2.0 ** 14)
                link3(v.tensor_tensor(col(O_INV), col(UP), col(OP), ALU.mult))
                link3(v.tensor_scalar(col(O_INV), col(O_INV), col(INV_A), 2.0 ** -13, ALU.mult, ALU.mult))
                dve.wait_ge(x_pe, 7)
                link3(v.tensor_scalar(aw, banks[0][:, 0:2 * H].rearrange("p (k h) -> p k h", k=2), col(OS), None, ALU.mult))
                link3(v.tensor_scalar(aw[:, 1, :], aw[:, 1, :], col(US), 1.0 / QR_SCALE, ALU.mult, ALU.mult))
                link2(v.tensor_copy(sm[:, 28:29], ones[:, 0:1]))
                dve.wait_ge(x_smask, 1)
                for h in range(H):
                    last = v.tensor_scalar(smask[:, h, :, :, h], ksum[:, h, :].rearrange("p (g b) -> p g b", g=NG), aw[:, 1, h:h + 1], None,
                                           ALU.mult)
                last.then_inc(x_smask, 1)
                for h in range(H):
                    dve.wait_ge(x_oh, h + 1)
                    at = slice(h % 2 * DIM, h % 2 * DIM + DIM)
                    v.scalar_tensor_tensor(out=wl[:, h // 2, at], in0=woT[:, h, :], scalar=aw[:, 0, h:h + 1], in1=wh[:, h // 2, at],
                                           op0=ALU.mult, op1=ALU.subtract)
                for g in range(NG):
                    dve.wait_ge(x_rh, g + 1)
                    v.tensor_tensor(rl[:, g, :], banks[1 + g][:, :], rh[:, g, :], ALU.subtract)

        cv = Carve(scratch[:, :], 12000)
        cv.at = keep
        res = cv.f32(2 * DIM).rearrange("p (b d) -> p b d", b=2)
        resb = cv.f32(2 * DIM).rearrange("p (b d) -> p b d", b=2)
        x1 = cv.f32(2 * DIM).rearrange("p (b d) -> p b d", b=2)
        x2 = cv.f32(2 * DIM).rearrange("p (b d) -> p b d", b=2)
        uh = cv.f16(2 * HD).rearrange("p (b h n) -> p b h n", b=2, h=H)
        ul = cv.f16(2 * HD).rearrange("p (b h n) -> p b h n", b=2, h=H)
        yTh = cv.f16(DIM).rearrange("p (c n) -> p c n", c=CH)
        yTl = cv.f16(DIM).rearrange("p (c n) -> p c n", c=CH)
        bo = cv.f32(DIM)
        ld_bo = sem("ld_bo")
        b_ld, b_st = [sem("b_ld0"), sem("b_ld1")], [sem("b_st0"), sem("b_st1")]
        (b_uh, b_ul, b_o, b_resb, b_x1, b_bn, b_mv, b_std, b_rinv, b_aff, b_xhat, b_xT, b_hi, b_lo, b_f, b_x2) = (
            sem("b_" + n) for n in "uh ul o resb x1 bn mv std rinv aff xhat xT hi lo f x2".split())
        OO, XT, FF = banks[0:2], banks[2], banks[3:5]

        def wo(w, h):
            return w[:, h // 2, h % 2 * DIM:h % 2 * DIM + DIM]

        def over_out_tiles(eng, step):
            def of(groups):
                return lambda i, k: step(i, k, groups)
            over_tiles(eng, 0, MID - 1, 4, 0, of((0,)))
            step(MID, MID % 2, (0, 1))
            over_tiles(eng, MID + 1, QT - 1, 0, 2, of((1,)))

        with nc.Block() as block:
            @block.sync
            def _(sp):
                sp.dma_start(bo, b_out.partition_broadcast(P)).then_inc(ld_bo, 16)

                def step(i, k, groups):
                    wait(sp, b_resb, i - 1)
                    sp.dma_start(res[:, k, :], xf[rows(i), :]).then_inc(b_ld[k], 16)
                over_out_tiles(sp, step)

            @block.gpsimd
            def _(pool):
                pool.wait_ge(ld_bo, 16)

                def step(i, k, groups):
                    pool.wait_ge(b_ld[k], (i - k) * 8 + 16)
                    wait(pool, b_x1, i - 1)
                    nc.gpsimd.tensor_tensor(resb[:, k, :], res[:, k, :], bo, ALU.add).then_inc(b_resb, 1)
                over_out_tiles(pool, step)

            @block.tensor
            def _(pe):
                def turn(i, k):
                    pe.wait_ge(b_xhat, i + 1)
                    wait(pe, b_lo, i)
                    transpose_rows(XT, xh[:, k, :], P).then_inc(b_xT, 1)

                def routed(i, k):
                    pe.wait_ge(b_lo, i + 1)
                    wait(pe, b_x2, i - 1)
                    for c in range(CH):
                        last = split_product(FF[k], P, yTh[:, c, :], yTl[:, c, :], fh[:, c, :], fl[:, c, :], c == 0, c == CH - 1)
                    last.then_inc(b_f, 1)

                def step(i, k, groups):
                    pe.wait_ge(b_ul, i + 1)
                    wait(pe, b_x1, i - 1)
                    for h in range(H):
                        split_product(OO[k], P, uh[:, k, h, :], ul[:, k, h, :], wo(wh, h), wo(wl, h), h == 0, False)
                        if h == HH and has(i - 1):
                            turn(i - 1, 1 - k)
                    for g in groups:
                        at = slice(i * P - g * G1, i * P - g * G1 + P) if isinstance(i, int) else bass.ds(i * P + (-g * G1), P)
                        last = split_product(OO[k], P, qh[:, g, at], ql[:, g, at], rh[:, g, :], rl[:, g, :], False, g == groups[-1])
                    last.then_inc(b_o, 1)
                    if has(i - 1):
                        routed(i - 1, 1 - k)
                over_out_tiles(pe, step)
                turn(QT - 1, (QT - 1) % 2)
                routed(QT - 1, (QT - 1) % 2)

            @block.scalar
            def _(act):
                def u_high(i, k):
                    wait(act, b_o, i - 1)
                    nc.scalar.activation(uh[:, k], qu[:, :, rows(i)], ACT.Copy, scale=col(US)).then_inc(b_uh, 1)

                def deviation(i, k):
                    act.wait_ge(b_mv, i + 1)
                    nc.scalar.activation(std[:, k:k + 1], mv[:, k, 1:2], ACT.Sqrt, bias=col(EPS_K), scale=1.0 / XS ** 2).then_inc(b_std, 1)

                def normalise(i, k):
                    act.wait_ge(b_aff, i + 1)
                    wait(act, b_xT, i - 1)
                    nc.scalar.activation(xh[:, k, 0:DIM - 1], x1[:, k, 0:DIM - 1], ACT.Identity, bias=aff[:, k, 1:2],
                                         scale=aff[:, k, 0:1]).then_inc(b_xhat, 1)

                def high(i, k):
                    act.wait_ge(b_xT, i + 1)
                    wait(act, b_f, i)
                    nc.scalar.activation(yTh, chunks(XT, P), ACT.Copy).then_inc(b_hi, 1)

                def store(i, k):
                    act.wait_ge(b_x2, i + 1)
                    act.dma_start(outf[rows(i), :], x2[:, k, :]).then_inc(b_st[k], 16)

                u_high(0, 0)

                def step(i, k, groups):
                    if has(i + 1):
                        u_high(i + 1, 1 - k)
                    if has(i - 1):
                        high(i - 1, 1 - k)
                    if has(i - 2):
                        store(i - 2, k)
                    deviation(i, k)
                    normalise(i, k)
                over_out_tiles(act, step)
                high(QT - 1, (QT - 1) % 2)
                store(QT - 2, (QT - 2) % 2)
                store(QT - 1, (QT - 1) % 2)
                act.wait_ge(b_st[0], 16 * ((QT + 1) // 2))
                act.wait_ge(b_st[1], 16 * (QT // 2))

            @block.vector
            def _(dve):
                def u_low(i, k):
                    dve.wait_ge(b_uh, i + 1)
                    nc.vector.scalar_tensor_tensor(out=ul[:, k], in0=qu[:, :, rows(i)], scalar=col(US), in1=uh[:, k],
                                                   op0=ALU.mult, op1=ALU.subtract).then_inc(b_ul, 1)

                def residual(i, k):
                    dve.wait_ge(b_o, i + 1)
                    dve.wait_ge(b_resb, i + 1)
                    wait(dve, b_x2, i - 1)
                    nc.vector.scalar_tensor_tensor(out=x1[:, k, :], in0=OO[k][:, :], scalar=col(O_INV), in1=resb[:, k, :],
                                                   op0=ALU.mult, op1=ALU.add).then_inc(b_x1, 1)

                def moments(i, k):
                    dve.wait_ge(b_x1, i + 1)
                    nc.vector.bn_stats(bst[:, k, :], x1[:, k, :]).then_inc(b_bn, 1)
                    dve.wait_ge(b_bn, i + 1)
                    nc.vector.tensor_copy(bcnt[:, :], bst[:, k, 0:1])
                    nc.vector.bn_aggr(mv[:, k, :], bst[:, k, :]).then_inc(b_mv, 1)
                    dve.wait_ge(b_std, i + 1)
                    nc.vector.reciprocal(aff[:, k, 0:1], std[:, k:k + 1]).then_inc(b_rinv, 1)
                    dve.wait_ge(b_rinv, i + 1)
                    nc.vector.tensor_scalar(aff[:, k, 1:2], mv[:, k, 0:1], aff[:, k, 0:1], -1.0, ALU.mult, ALU.mult).then_inc(b_aff, 1)

                def rest(i, k):
                    dve.wait_ge(b_hi, i + 1)
                    nc.vector.tensor_tensor(yTl, chunks(XT, P), yTh, ALU.subtract).then_inc(b_lo, 1)

                def finish(i, k):
                    dve.wait_ge(b_f, i + 1)
                    if has(i - 2):
                        dve.wait_ge(b_st[k], (i - k) * 8)
                    nc.vector.scalar_tensor_tensor(out=x2[:, k, :], in0=FF[k][:, :], scalar=col(F_INV), in1=x1[:, k, :],
                                                   op0=ALU.mult, op1=ALU.add).then_inc(b_x2, 1)

                u_low(0, 0)

                def step(i, k, groups):
                    if has(i + 1):
                        u_low(i + 1, 1 - k)
                    if has(i - 1):
                        rest(i - 1, 1 - k)
                    if has(i - 2):
                        finish(i - 2, k)
                    residual(i, k)
                    moments(i, k)
                over_out_tiles(dve, step)
                rest(QT - 1, (QT - 1) % 2)
                finish(QT - 2, (QT - 2) % 2)
                finish(QT - 1, (QT - 1) % 2)


_INS = ['x', 'ctx_1024', 'L0_xattn_ln_g', 'L0_xattn_ln_b', 'L0_xattn_w_in', 'L0_xattn_wp_w1', 'L0_xattn_wp_b1',
        'L0_xattn_wp_ln_g', 'L0_xattn_wp_ln_b', 'L0_xattn_wp_w2', 'L0_xattn_wp_b2', 'L0_xattn_w_out', 'L0_xattn_b_out',
        'L0_ffn_W', 'L0_ffn_b', 'L0_ffn_logits', 'L0_ffn_u']
_OUTS = [((32, 100, 512), 'float32')]


def kernel(**inputs):
    import numpy as _np
    import concourse.bacc as _bacc
    from concourse import mybir as _mybir
    from concourse.bass_utils import run_bass_kernel_spmd as _run

    nc = _bacc.Bacc("TRN2", target_bir_lowering=False, num_devices=1)
    arrays, args = {}, []
    for name in _INS:
        a = _np.ascontiguousarray(inputs[name])
        arrays[f"in_{name}_dram"] = a
        args.append(nc.dram_tensor(f"in_{name}_dram", a.shape, _mybir.dt.from_np(a.dtype), kind="ExternalInput").ap())
    for i, (shape, dtype) in enumerate(_OUTS):
        dt = _mybir.dt.from_np(_np.dtype(dtype))
        args.append(nc.dram_tensor(f"out_{i}_dram", shape, dt, kind="ExternalOutput").ap())
    build(nc, *args)
    r = _run(nc, [arrays], core_ids=[0])
    got = tuple(r.results[0][f"out_{i}_dram"] for i in range(len(_OUTS)))
    return got[0]
```

```python
from contextlib import ExitStack

import concourse.bass as bass
from concourse import mybir

ALU = mybir.AluOpType
ACT = mybir.ActivationFunctionType
F32 = mybir.dt.float32
F16 = mybir.dt.float16
I32 = mybir.dt.int32
U32 = mybir.dt.uint32
AX = mybir.AxisListType
RMAX = bass.bass_isa.ReduceOp.max
P = 128
EPS = 1e-5
XS = 16.0
QR_SCALE = 64.0
EXPONENT = 0x7F800000
SCRATCH = 13600


def build(nc, x, ctx_1024, ln_g, ln_b, w_in, wp_w1, wp_b1, wp_ln_g, wp_ln_b, wp_w2, wp_b2,
          w_out, b_out, ffn_W, ffn_b, ffn_logits, ffn_u, out):
    NB, NQ, DIM = x.shape
    NK = ctx_1024.shape[1]
    HD = w_in.shape[0]
    D = P
    H = HD // D
    CH = DIM // P
    HH = H // 2
    HW = HH * D
    NR = NB * NQ
    QT = NR // P
    KT = -(-NK // P)
    KLAST = NK - (KT - 1) * P
    NKT = NB * KT
    MC = D + 2
    MB = 3
    BH = P // H
    NG = NB // BH
    SPLIT = BH * NQ
    QG = -(-SPLIT // P) * P
    G1 = SPLIT // P * P
    MID = SPLIT // P
    assert QT * P == NR and NG == 2 and NR - G1 == QG and QT % 2 == 1 and MID % 2 == 0 and KT % 2 == 0

    xf = x.rearrange("b n d -> (b n) d")
    outf = out.rearrange("b n d -> (b n) d")

    with ExitStack() as ctx:
        def sb(name, shape, dt=F32):
            return ctx.enter_context(nc.sbuf_tensor(name, shape, dt))

        def sem(name):
            return ctx.enter_context(nc.semaphore(name))

        banks = [ctx.enter_context(nc.psum_tensor(f"bank{i}", [P, 512], F32)) for i in range(8)]

        qu = sb("qu", [P, H, NR])
        wh = sb("wh", [P, CH, HD], F16)
        wl = sb("wl", [P, CH, HD], F16)
        woT = sb("woT", [P, H, DIM])
        fh = sb("fh", [P, CH, DIM], F16)
        fl = sb("fl", [P, CH, DIM], F16)
        xh = sb("xh", [P, 2, DIM])
        acc_q = sb("acc_q", [P, DIM])
        acc_k = sb("acc_k", [P, DIM])
        ksum = sb("ksum", [P, H, NB])
        qr = sb("qr", [P, QT, H])
        fs = sb("fs", [P, H])
        ident = sb("ident", [P, P])
        w1T = sb("w1T", [P, 2, P])
        w2T = sb("w2T", [P, 3])
        b1s = sb("b1s", [H, P])
        g1s = sb("g1s", [H, P])
        be1s = sb("be1s", [H, P])
        b2s = sb("b2s", [H, 3])
        ones = sb("ones", [P, P])
        cf = sb("cf", [P, 26])
        nmax = sb("nmax", [P, H])
        bst = sb("bst", [P, 2, 6])
        bcnt = sb("bcnt", [P, 1])
        mv = sb("mv", [P, 2, 2])
        std = sb("std", [P, 2])
        aff = sb("aff", [P, 2, 2])
        hb = sb("hb", [P, 2, H, 6])
        sq = sb("sq", [P, H, 2])
        ss = sb("ss", [P, 2, H])
        nrm = sb("nrm", [P, 2, H])
        rt = sb("rt", [P, 2, H])
        rc = sb("rc", [P, 2, H])
        mean2 = sb("mean2", [P, H])
        rsm = sb("rsm", [P, 9, H])
        scratch = sb("scratch", [P, SCRATCH])

        (EPS_K, EPS_Q, WMAX, WP, WS, INV_A, INV_A2, C_NUM, C_DENK, C_DENQ, FMAX, FP, FSC, F_INV,
         OMAX, OP, OS, UMAX, UP, US, O_INV, TMP, EPS_1, WMAXP, WCOL) = range(25)

        def col(c, n=P):
            return cf[0:n, c:c + 1]

        class Carve:

            def __init__(self, base, limit):
                self.base, self.at, self.limit = base, 0, limit

            def f32(self, n):
                v = self.base[:, self.at:self.at + n]
                self.at += n
                assert self.at <= self.limit
                return v

            def f16(self, n):
                return self.f32(n // 2).bitcast(F16)

        def chain(eng, s, base=0):
            count = [0]

            def link(ins):
                count[0] += 1
                ins.then_inc(s, 1)
                eng.wait_ge(s, base + count[0])
            return link

        def wait(eng, s, v):
            if isinstance(v, int) and v <= 0:
                return
            eng.wait_ge(s, v)

        def power_of_two(eng, link, m, p, inv, scale):
            link(eng.tensor_scalar(m, m, 1e-30, None, ALU.max))
            link(eng.tensor_scalar(p.bitcast(I32), m.bitcast(I32), EXPONENT, None, ALU.bitwise_and))
            link(eng.reciprocal(inv, p))
            link(eng.tensor_scalar(inv, inv, scale, None, ALU.mult))

        area = qu[:, :, :].rearrange("p h n -> p (h n)")
        cw = Carve(area, H * NR)
        w_raw = cw.f32(H * DIM).rearrange("p (h i) -> p h i", h=H)
        wo_raw = cw.f32(CH * HD).rearrange("p (c n) -> p c n", c=CH)
        f_raw = cw.f32(CH * DIM).rearrange("p (c n) -> p c n", c=CH)
        f_last = cw.f32(DIM)
        g_bc = cw.f32(DIM)
        b_bc = cw.f32(DIM)
        junk = cw.f32(DIM)
        last_col = cw.f32(H)
        bias_col = cw.f32(H)
        w1_raw = cw.f32(2 * P)
        w2_raw = cw.f32(P)
        route = cw.f32(64)

        ld_route, ld_w, ld_wo, ld_f, ld_fb, ld_small = (sem(f"ld_{n}") for n in ("route", "w", "wo", "f", "fb", "small"))
        ident_ready, const_ready = sem("ident_ready"), sem("const_ready")
        route_act, route_dve, route_idx = sem("route_act"), sem("route_dve"), sem("route_idx")
        w_dve, w_max, w_all = sem("w_dve"), sem("w_max"), sem("w_all")
        f_sub, f_max, f_all = sem("f_sub"), sem("f_max"), sem("f_all")
        o_max, o_all = sem("o_max"), sem("o_all")
        w_scaled = sem("w_scaled")
        wt_pe, wt_hi, wt_lo = sem("wt_pe"), sem("wt_hi"), sem("wt_lo")
        ot_pe, ot_act = sem("ot_pe"), sem("ot_act")
        small_pe, small_act = sem("small_pe"), sem("small_act")
        f_hi, f_lo = sem("f_hi"), sem("f_lo")

        logits_t, u_t = route[0:1, 0:8], route[0:1, 8:16]
        r_m, r_e, r_s, r_ls = route[0:1, 16:17], route[0:1, 17:25], route[0:1, 25:26], route[0:1, 26:27]
        r_g, r_sc = route[0:1, 27:35], route[0:1, 35:43]
        r_top, r_idx = route[0:1, 43:51], route[0:1, 51:59].bitcast(U32)
        n_ops = ffn_W.shape[0]

        with nc.Block() as block:
            @block.sync
            def _(sp):
                sp.dma_start(logits_t, ffn_logits.rearrange("(a n) -> a n", a=1)).then_inc(ld_route, 16)
                sp.dma_start(u_t, ffn_u.rearrange("(a n) -> a n", a=1)).then_inc(ld_route, 16)
                sp.dma_start(g_bc, ln_g.partition_broadcast(P)).then_inc(ld_w, 16)
                sp.dma_start(b_bc, ln_b.partition_broadcast(P)).then_inc(ld_w, 16)
                sp.dma_start(w_raw, w_in.rearrange("(h d) i -> d h i", d=D)).then_inc(ld_w, 16)
                sp.dma_start(wo_raw, w_out.rearrange("(c p) n -> p c n", p=P)).then_inc(ld_wo, 16)
                sp.wait_ge(route_idx, 1)
                idx = sp.value_load(r_idx[0:1, 0:1], min_val=0, max_val=n_ops - 1)
                sp.dma_start(f_raw, ffn_W[bass.ds(idx, 1), :, :].rearrange("a (c p) n -> p (a c) n", p=P)).then_inc(ld_f, 16)
                sp.dma_start(f_last, ffn_W[bass.ds(idx, 1), DIM - 1, :].rearrange("a n -> (a n)").partition_broadcast(P)).then_inc(ld_f, 16)
                sp.wait_ge(f_sub, 1)
                sp.dma_start(f_raw[P - 1:P, CH - 1, :], ffn_b[bass.ds(idx, 1), :]).then_inc(ld_fb, 16)

            @block.gpsimd
            def _(pool):
                pool.memset(ident[:, :], 0.0).then_inc(ident_ready, 1)
                pool.wait_ge(ident_ready, 1)
                pool.affine_select(out=ident[:, :], in_=ident[:, :], compare_op=ALU.not_equal, fill=1.0, base=0,
                                   pattern=[[-1, P]], channel_multiplier=1).then_inc(ident_ready, 1)
                pool.memset(acc_q[:, :], 0.0)
                pool.memset(acc_k[:, :], 0.0)
                pool.memset(nmax[:, :], 0.0)
                pool.memset(ones[:, :], 1.0)
                pool.memset(xh[:, :, DIM - 1:DIM], XS).then_inc(const_ready, 1)
                pool.wait_ge(w_max, 1)
                pool.partition_all_reduce(col(WMAX), col(WMAXP), P, RMAX).then_inc(w_all, 1)
                pool.wait_ge(o_max, 1)
                pool.partition_all_reduce(col(OMAX), col(TMP), P, RMAX).then_inc(o_all, 1)
                pool.wait_ge(f_max, 1)
                pool.partition_all_reduce(col(FMAX), col(UP), P, RMAX).then_inc(f_all, 1)

            @block.scalar
            def _(act):
                act.dma_start(w1_raw, wp_w1).then_inc(ld_small, 16)
                act.dma_start(w2_raw[0:3, :], wp_w2).then_inc(ld_small, 16)
                act.dma_start(b1s[:, :], wp_b1.partition_broadcast(H)).then_inc(ld_small, 16)
                act.dma_start(g1s[:, :], wp_ln_g.partition_broadcast(H)).then_inc(ld_small, 16)
                act.dma_start(be1s[:, :], wp_ln_b.partition_broadcast(H)).then_inc(ld_small, 16)
                act.dma_start(b2s[:, :], wp_b2.partition_broadcast(H)).then_inc(ld_small, 16)
                act.wait_ge(route_dve, 1)
                link = chain(act, route_act)
                link(nc.scalar.activation(r_e, r_e, ACT.Exp, accum_out=r_s))
                link(nc.scalar.activation(r_ls, r_s, ACT.Ln))
                link(nc.scalar.activation(r_g, u_t, ACT.Ln))
                link(nc.scalar.activation(r_g, r_g, ACT.Ln, scale=-1.0))
                for n in range(H):
                    act.wait_ge(ot_pe, n + 1)
                    nc.scalar.activation(woT[:, n, :], banks[4 + n % 3][:, :], ACT.Copy).then_inc(ot_act, 1)
                act.wait_ge(w_scaled, 1)
                for n in range(2 * CH):
                    act.wait_ge(wt_pe, n + 1)
                    nc.scalar.activation(wh[:, n // 2, n % 2 * HW:n % 2 * HW + HW], banks[n % 4][:, :], ACT.Copy,
                                         scale=col(WS)).then_inc(wt_hi, 1)
                act.wait_ge(small_pe, 1)
                nc.scalar.activation(w1T[:, :, :], banks[7][:, 0:2 * P].rearrange("p (c n) -> p c n", c=2), ACT.Copy)
                nc.scalar.activation(w2T[:, :], banks[7][:, 2 * P:2 * P + 3], ACT.Copy).then_inc(small_act, 1)
                act.wait_ge(f_lo, 1)
                nc.scalar.activation(fh[:, :, :], f_raw, ACT.Copy, scale=col(FSC)).then_inc(f_hi, 1)
                act.wait_ge(ld_small, 96)
                act.wait_ge(f_hi, 1)

            @block.tensor
            def _(pe):
                pe.wait_ge(ident_ready, 2)
                pe.wait_ge(ld_small, 96)
                for c in range(2):
                    nc.tensor.transpose(banks[7][:, c * P:c * P + P], w1_raw[:, c * P:c * P + P], ident[:, :])
                nc.tensor.transpose(banks[7][:, 2 * P:2 * P + 3], w2_raw[0:3, :], ident[0:3, 0:3]).then_inc(small_pe, 1)
                pe.wait_ge(ld_wo, 16)
                for h in range(H):
                    if h >= 3:
                        pe.wait_ge(ot_act, h - 2)
                    for c in range(CH):
                        last = nc.tensor.transpose(banks[4 + h % 3][:, c * P:c * P + P], wo_raw[:, c, h * D:h * D + D], ident[:, :])
                    last.then_inc(ot_pe, 1)
                pe.wait_ge(w_max, 1)
                for n in range(2 * CH):
                    if n >= 4:
                        pe.wait_ge(wt_lo, n - 3)
                    for k in range(HH):
                        last = nc.tensor.transpose(banks[n % 4][:, k * P:k * P + P],
                                                   w_raw[:, n % 2 * HH + k, n // 2 * P:n // 2 * P + P], ident[:, :])
                    last.then_inc(wt_pe, 1)

            @block.vector
            def _(dve):
                for c, v in ((EPS_K, EPS / XS ** 2), (EPS_Q, EPS * EPS / XS ** 2), (EPS_1, EPS)):
                    nc.vector.memset(col(c), v)
                link = chain(dve, route_dve)
                dve.wait_ge(ld_route, 32)
                nc.vector.reduce_max(r_m, logits_t, AX.X).then_inc(w_dve, 1)
                dve.wait_ge(w_dve, 1)
                link(nc.vector.tensor_scalar(r_e, logits_t, r_m, None, ALU.subtract))
                wlink = chain(dve, w_dve, 1)
                wlink(nc.vector.tensor_scalar(r_sc, logits_t, r_m, None, ALU.subtract))
                dve.wait_ge(route_act, 4)
                wlink(nc.vector.tensor_scalar(r_sc, r_sc, r_ls, None, ALU.subtract))
                wlink(nc.vector.tensor_tensor(r_sc, r_sc, r_g, ALU.subtract))
                nc.vector.max(r_top, r_sc).then_inc(w_dve, 1)
                dve.wait_ge(w_dve, 5)
                nc.vector.max_index(r_idx, r_top, r_sc).then_inc(route_idx, 1)
                wlink = chain(dve, w_dve, 5)
                dve.wait_ge(ld_w, 48)
                for h in range(H):
                    wlink(nc.vector.tensor_tensor_reduce(out=junk, in0=w_raw[:, h, :], in1=b_bc, scale=1.0, scalar=0.0,
                                                         op0=ALU.mult, op1=ALU.add, accum_out=bias_col[:, h:h + 1]))
                g_all = g_bc.unsqueeze(1).to_broadcast([P, H, DIM])
                wlink(nc.vector.tensor_tensor(w_raw, w_raw, g_all, ALU.mult))
                wlink(nc.vector.tensor_copy(last_col, w_raw[:, :, DIM - 1]))
                for h in range(H):
                    last = nc.vector.tensor_scalar(w_raw[:, h, :], w_raw[:, h, :], last_col[:, h:h + 1], None, ALU.subtract)
                wlink(last)
                wlink(nc.vector.tensor_copy(w_raw[:, :, DIM - 1], bias_col))
                nc.vector.tensor_reduce(col(WMAXP), w_raw, AX.XY, ALU.max, apply_absolute_value=True).then_inc(w_max, 1)
                dve.wait_ge(ld_wo, 16)
                nc.vector.tensor_reduce(col(TMP), wo_raw, AX.XY, ALU.max, apply_absolute_value=True).then_inc(o_max, 1)
                dve.wait_ge(w_all, 1)
                wlink = chain(dve, w_dve, 5 + H + 4)
                power_of_two(nc.vector, wlink, col(WMAX), col(WP), col(WS), 1.0)
                wlink(nc.vector.tensor_scalar(col(INV_A), col(WP), 1.0 / XS, None, ALU.mult))
                wlink(nc.vector.tensor_tensor(col(INV_A2), col(INV_A), col(INV_A), ALU.mult))
                wlink(nc.vector.tensor_scalar(col(C_NUM), col(INV_A2), 1.0 / (D - 1), None, ALU.mult))
                wlink(nc.vector.tensor_scalar(col(C_DENK), col(C_NUM), 0.5, None, ALU.mult))
                nc.vector.tensor_scalar(col(C_DENQ), col(C_NUM), 0.5 / QR_SCALE, None, ALU.mult).then_inc(w_scaled, 1)
                for n in range(2 * CH):
                    dve.wait_ge(wt_hi, n + 1)
                    at = slice(n % 2 * HW, n % 2 * HW + HW)
                    nc.vector.scalar_tensor_tensor(out=wl[:, n // 2, at], in0=banks[n % 4][:, :], scalar=col(WS),
                                                   in1=wh[:, n // 2, at], op0=ALU.mult, op1=ALU.subtract).then_inc(wt_lo, 1)
                dve.wait_ge(ld_f, 32)
                nc.vector.tensor_tensor(f_raw, f_raw, f_last.unsqueeze(1).to_broadcast([P, CH, DIM]), ALU.subtract).then_inc(f_sub, 1)
                dve.wait_ge(ld_fb, 16)
                nc.vector.tensor_reduce(col(UP), f_raw, AX.XY, ALU.max, apply_absolute_value=True).then_inc(f_max, 1)
                dve.wait_ge(f_all, 1)
                wlink = chain(dve, w_dve, 5 + H + 4 + 8)
                power_of_two(nc.vector, wlink, col(FMAX), col(FP), col(FSC), 2.0)
                nc.vector.tensor_scalar(col(F_INV), col(FP), 1.0 / (2.0 * XS), None, ALU.mult).then_inc(f_lo, 1)
                dve.wait_ge(f_hi, 1)
                for c in range(CH):
                    last = nc.vector.scalar_tensor_tensor(out=fl[:, c, :], in0=f_raw[:, c, :], scalar=col(FSC), in1=fh[:, c, :],
                                                   op0=ALU.mult, op1=ALU.subtract)
                dve.wait_ge(o_all, 1)
                power_of_two(nc.vector, wlink, col(OMAX), col(OP), col(OS), 1.0)


        def head_view(par, n, k):
            return hb[0:n, par, :, :].rearrange("p h (e k) -> p h e k", e=2)[:, :, :, k]

        def transpose_rows(bank, src, n):
            for c in range(CH):
                last = nc.tensor.transpose(bank[:, c * P:c * P + n], src[0:n, c * P:c * P + P], ident[0:n, 0:n])
            return last

        def chunks(bank, n):
            return bank[:, :].rearrange("p (c n) -> p c n", n=P)[:, :, 0:n]

        def split_product(bank, n, hi, lo, w_hi, w_lo, start, stop):
            nc.tensor.matmul(bank[0:n, :], hi, w_hi, start=start, stop=False, skip_group_check=True)
            nc.tensor.matmul(bank[0:n, :], hi, w_lo, start=False, stop=False, skip_group_check=True)
            return nc.tensor.matmul(bank[0:n, :], lo, w_hi, start=False, stop=stop, skip_group_check=True)

        def project(bank, hi, lo, n, half):
            at = slice(half * HW, half * HW + HW)
            for c in range(CH):
                last = split_product(bank, n, hi[:, c, 0:n], lo[:, c, 0:n], wh[:, c, at], wl[:, c, at], c == 0, c == CH - 1)
            return last

        def head_stats(bank, par, n, half):
            for k in range(HH):
                last = nc.vector.bn_stats(hb[0:n, par, half * HH + k, :], bank[0:n, k * D:k * D + D])
            return last

        def head_squares(link, par, n):
            m, v, t = head_view(par, n, 1), head_view(par, n, 2), sq[0:n, :, :]
            link(nc.vector.tensor_tensor(t, m, m, ALU.mult))
            link(nc.vector.scalar_tensor_tensor(out=t, in0=t, scalar=float(D // 2), in1=v, op0=ALU.mult, op1=ALU.add))
            return nc.vector.tensor_tensor(ss[0:n, par, :], t[:, :, 0], t[:, :, 1], ALU.add)

        def ratio_parts(link, par, n):
            def part(k, e):
                return hb[0:n, par, :, 3 * e + k]
            dm, m2 = rsm[0:n, par, :], rsm[0:n, 2 + par, :]
            link(nc.gpsimd.tensor_tensor(dm, part(1, 0), part(1, 1), ALU.subtract))
            link(nc.gpsimd.tensor_tensor(dm, dm, dm, ALU.mult))
            return nc.gpsimd.tensor_tensor(m2, part(2, 0), part(2, 1), ALU.add)

        def ratio_terms(link, par, n, c_den, half_unit):
            dm, m2, num, den = rsm[0:n, par, :], rsm[0:n, 2 + par, :], rsm[0:n, 4 + par, :], rsm[0:n, 6 + par, :]
            link(nc.vector.scalar_tensor_tensor(out=m2, in0=dm, scalar=float(D // 4), in1=m2, op0=ALU.mult, op1=ALU.add))
            nc.vector.tensor_scalar(num, m2, col(C_NUM, n), 1.0, ALU.mult, ALU.min)
            link(nc.vector.tensor_scalar(den, m2, col(c_den, n), half_unit, ALU.mult, ALU.add))
            return nc.vector.reciprocal(den, den)

        def spread(v, n, heads):
            return v.unsqueeze(2).to_broadcast([n, heads, D])

        def by_head(v):
            return v.rearrange("p (h d) -> p h d", d=D)

        def rows(i):
            return slice(i * P, i * P + P) if isinstance(i, int) else bass.ds(i * P, P)

        def over_tiles(eng, first, last, head, tail, step):
            for i in range(first, first + head):
                step(i, i % 2)
            start, pairs = first + head, (last + 1 - first - head - tail) // 2
            with eng.Fori(0, pairs) as j:
                step(j * 2 + start, start % 2)
                step(j * 2 + (start + 1), (start + 1) % 2)
            for i in range(start + 2 * pairs, last + 1):
                step(i, i % 2)

        def has(i):
            return not isinstance(i, int) or 0 <= i < QT

        def either(query, key, i, k):
            if has(i):
                query(i, k)
            else:
                key(0, i - QT)

        cv = Carve(scratch[:, :], SCRATCH)
        xTh = cv.f16(2 * DIM).rearrange("p (b c n) -> p b c n", b=2, c=CH)
        xTl = cv.f16(2 * DIM).rearrange("p (b c n) -> p b c n", b=2, c=CH)
        at_qs = cv.at
        qs = cv.f32(2 * HD).rearrange("p (b n) -> p b n", b=2)
        at_qc = cv.at
        qc = cv.f32(2 * HD).rearrange("p (b n) -> p b n", b=2)
        cv.at += 16
        at_qch = cv.at
        qch = cv.f16(2 * HD).rearrange("p (b n) -> p b n", b=2)
        at_qcl = cv.at
        qcl = cv.f16(2 * HD).rearrange("p (b n) -> p b n", b=2)
        at_fsb = cv.at
        fsb = cv.f32(HD).rearrange("p (h d) -> p h d", h=H)
        at_xin = cv.at
        xin = cv.f32(2 * DIM).rearrange("p (r d) -> p r d", r=2)
        at_cin = cv.at
        cin = cv.f32(KT * DIM).rearrange("p (t d) -> p t d", t=KT)
        at_free = cv.at

        q_ld = [sem("q_ld0"), sem("q_ld1")]
        (q_bn, q_mv, q_std, q_rinv, q_aff, q_xhat, q_acc, q_xT, q_hi, q_lo, q_proj, q_sums, q_ss, q_nrm, q_rc, q_hat,
         q_mean, q_cent, q_qch, q_qcl, q_tr, q_trc, q_fc, q_part, q_parts, q_term, q_rden, q_r, q_fev) = (sem("q_" + n) for n in (
             "bn mv std rinv aff xhat acc xT hi lo proj sums ss nrm rc hat "
             "mean cent qch qcl tr trc fc part parts term rden r fev").split())
        XT, Q_PR, TR, FC = banks[0], banks[1:5], banks[5], banks[6:8]

        cv.at = at_qs
        ks = cv.f32(2 * HD).rearrange("p (b n) -> p b n", b=2)
        assert cv.at == at_qc
        kh = cv.f16(2 * H * MC).rearrange("p (b h m) -> p b h m", b=2, h=H)
        kl = cv.f16(2 * HD).rearrange("p (b h d) -> p b h d", b=2, h=H)
        assert cv.at <= at_qch
        cv.at = at_qch
        msb = cv.f32(H * MC).rearrange("p (h m) -> p h m", h=H)
        after_msb = cv.at

        k_ld = [sem(f"k_ld{t}") for t in range(KT)]
        (k_bn, k_mv, k_std, k_rinv, k_aff, k_xhat, k_acc, k_xT, k_hi, k_lo, k_proj, k_sums, k_ss, k_nrm, k_rt, k_rc, k_kt,
         k_khi, k_klo, k_part, k_parts, k_term, k_rden, k_rstep, k_r, k_m, k_mev, k_sum, k_u, k_uev) = (sem("k_" + n) for n in (
             "bn mv std rinv aff xhat acc xT hi lo proj sums ss nrm rt rc kt "
             "khi klo part parts term rden rstep r m mev sum u uev").split())
        K_PR, MM, UU = (banks[3], banks[4], banks[1]), (banks[2], banks[5], banks[6]), banks[7]
        FULL = (KT - 1) * P

        def size(t):
            return P if t % KT < KT - 1 else KLAST

        def slot(t):
            return (QT + t) % 2

        def at_seam(T):
            return isinstance(T, int) and T < 2

        LASTQ = (QT - 1) % 2

        def over_batches(eng, batch):
            batch(0)
            with eng.Fori(1, NB - 1) as b:
                batch(b)
            batch(NB - 1)

        def there(b, t):
            return not isinstance(b, int) or 0 <= b * KT + t < NKT

        def one(b):
            return slice(b, b + 1) if isinstance(b, int) else bass.ds(b, 1)

        cv.at = after_msb
        xm = cv.f32(2 * CH).rearrange("p (k c) -> p k c", k=2)
        xmh = cv.f16(2 * CH).rearrange("p (k c) -> p k c", k=2)
        xml = cv.f16(2 * CH).rearrange("p (k c) -> p k c", k=2)
        feat = cv.f32(2 * H).rearrange("p (k h) -> p k h", k=2)
        h1 = cv.f32(P)
        h1T = cv.f32(H)
        sm = cv.f32(32)
        diag = cv.f32(2 * H).rearrange("p (k h) -> p k h", k=2)
        aw = cv.f32(2 * H).rearrange("p (k h) -> p k h", k=2)
        wrow = cv.f32(1)
        tiled = cv.f32(P)
        batch_of = cv.f32((QT + 1) * BH).rearrange("p (i b) -> p i b", b=BH)
        assert cv.at <= at_fsb
        cv.at = at_cin
        rh = cv.f16(NG * DIM).rearrange("p (g n) -> p g n", g=NG)
        rl = cv.f16(NG * DIM).rearrange("p (g n) -> p g n", g=NG)
        smask = cv.f32(H * NG * P).rearrange("p (h g b k) -> p h g b k", h=H, g=NG, k=H)
        assert cv.at <= at_free
        wcol = cf[:, WCOL:WCOL + 1]
        (x_zero, x_batch_of, x_sums, x_norm, x_means, x_global, x_feat, x_hidden, x_var, x_std, x_h1, x_h1_turned, x_h1T, x_out,
         x_less_max, x_exp, x_diag, x_spread, x_aw, x_wrow, x_smask, x_rb, x_rh, x_rl, x_woh, x_wol, x_nmax, x_umax, x_us, x_dve) = (
             sem("x_" + n) for n in "zero batch_of sums norm means global feat hidden var std h1 h1_turned h1T out "
             "less_max exp diag spread aw wrow smask rb rh rl woh wol nmax umax us dve".split())
        RB = (banks[3], banks[1])
        N_GLOBAL, N_H1T, N_OUT = XT[:, 16:16 + 2 * H], XT[:, 48:48 + H], XT[0:H, 64:67]
        N_SPREAD, N_WROW, N_HIDDEN = XT[:, 80:80 + 2 * H], XT[:, 112:113], XT[0:H, P:2 * P]

        cv.at = at_qs
        uh = cv.f16(2 * HD).rearrange("p (b h n) -> p b h n", b=2, h=H)
        ul = cv.f16(2 * HD).rearrange("p (b h n) -> p b h n", b=2, h=H)
        assert cv.at == at_qc
        x1 = cv.f32(2 * DIM).rearrange("p (b d) -> p b d", b=2)
        x2 = cv.f32(2 * DIM).rearrange("p (b d) -> p b d", b=2)
        cv.at = at_fsb
        res = cv.f32(2 * DIM).rearrange("p (b d) -> p b d", b=2)
        resb = cv.f32(2 * DIM).rearrange("p (b d) -> p b d", b=2)
        assert cv.at == at_cin
        cv.at = 0
        yTh = cv.f16(DIM).rearrange("p (c n) -> p c n", c=CH)
        yTl = cv.f16(DIM).rearrange("p (c n) -> p c n", c=CH)
        cv.at = at_free
        bo = cv.f32(DIM)
        zf = cv.f32(NG * P).rearrange("p (g b k) -> p g b k", g=NG, k=H)
        zh = cv.f16(2 * NG * P).rearrange("p (s g n) -> p s g n", s=2, g=NG)
        zl = cv.f16(2 * NG * P).rearrange("p (s g n) -> p s g n", s=2, g=NG)
        ld_bo = sem("ld_bo")
        b_ld, b_st = [sem("b_ld0"), sem("b_ld1")], [sem("b_st0"), sem("b_st1")]
        (b_uh, b_ul, b_o, b_resb, b_x1, b_bn, b_mv, b_std, b_rinv, b_aff, b_xhat, b_xT, b_hi, b_lo, b_f, b_x2) = (
            sem("b_" + n) for n in "uh ul o resb x1 bn mv std rinv aff xhat xT hi lo f x2".split())
        OO, B_XT, FF, ZT = banks[4:6], banks[6], (banks[3], banks[7]), banks[2]
        z_f, z_t, z_h, z_l = (sem("z_" + n) for n in "f t h l".split())

        def groups_of(i, groups):
            if not isinstance(i, int):
                return groups
            return (0,) * (i <= MID) + (1,) * (i >= MID)

        def wo(w, h):
            return w[:, h // 2, h % 2 * DIM:h % 2 * DIM + DIM]

        def over_out_tiles(eng, step):
            def of(groups):
                return lambda i, k: step(i, k, groups)
            over_tiles(eng, 0, MID - 1, 4, 2, of((0,)))
            step(MID, MID % 2, (0, 1))
            over_tiles(eng, MID + 1, QT - 1, 0, 2, of((1,)))

        with nc.Block() as block:
            @block.sync
            def _(sp):
                def query_step(i, k):
                    wait(sp, q_xhat, i - 1)
                    sp.dma_start(xin[:, k, :], xf[rows(i), :]).then_inc(q_ld[k], 16)
                over_tiles(sp, 0, QT - 1, 4, 3, query_step)
                def key_batch(b):
                    for t in range(KT):
                        wait(sp, k_xhat, b * KT + (t - KT + 1))
                        if t < KT - 1:
                            src = ctx_1024[one(b), 0:FULL, :].rearrange("a (p j) d -> p (a j) d", j=KT - 1)[:, t, :]
                        else:
                            src = ctx_1024[one(b), FULL:NK, :].rearrange("a p d -> (a p) d")
                        sp.dma_start(cin[0:size(t), t, :], src).then_inc(k_ld[t], 16)
                over_batches(sp, key_batch)
                sp.wait_ge(q_fev, 4)
                sp.wait_ge(q_xhat, QT)
                sp.dma_start(bo, b_out.partition_broadcast(P)).then_inc(ld_bo, 16)

                def out_step(i, k, groups):
                    wait(sp, b_resb, i - 1)
                    sp.dma_start(res[:, k, :], xf[rows(i), :]).then_inc(b_ld[k], 16)
                over_out_tiles(sp, out_step)

            @block.gpsimd
            def _(pool):
                def query_sum_rows(i, k):
                    pool.wait_ge(q_xhat, i + 1)
                    wait(pool, q_acc, i)
                    nc.gpsimd.tensor_tensor(acc_q[:, :], acc_q[:, :], xh[:, k, :], ALU.add).then_inc(q_acc, 1)

                def query_parts(i, k):
                    pool.wait_ge(q_ss, i + 1)
                    wait(pool, q_r, i - 1)
                    ratio_parts(chain(pool, q_part, i * 2), k, P).then_inc(q_parts, 1)

                def query_ratio(i, k):
                    pool.wait_ge(q_rden, i + 1)
                    dst = qr[:, i, :] if isinstance(i, int) else qr[:, bass.ds(i, 1), :].rearrange("p a h -> p (a h)")
                    nc.gpsimd.tensor_tensor(dst, rsm[:, 4 + k, :], rsm[:, 6 + k, :], ALU.mult).then_inc(q_r, 1)

                def query_centred_low(i, k, half):
                    pool.wait_ge(q_qch, 2 * i + half + 1)
                    at = slice(half * HW, half * HW + HW)
                    nc.gpsimd.tensor_tensor(qcl[:, k, at], qc[:, k, at], qch[:, k, at], ALU.subtract).then_inc(q_qcl, 1)

                def key_sum_rows(b, t):
                    T, n, k = b * KT + t, size(t), slot(t)
                    pool.wait_ge(k_xhat, T + 1)
                    wait(pool, k_acc, T)
                    nc.gpsimd.tensor_tensor(acc_k[0:n, :], acc_k[0:n, :], xh[0:n, k, :], ALU.add).then_inc(k_acc, 1)

                def key_parts(b, t):
                    T, n, k = b * KT + t, size(t), slot(t)
                    pool.wait_ge(k_ss, T + 1)
                    ratio_parts(chain(pool, k_part, T * 2), k, n).then_inc(k_parts, 1)

                def key_ratio(b, t):
                    T, n, k = b * KT + t, size(t), slot(t)
                    link = chain(pool, k_rstep, T * 3)
                    r = rsm[0:n, 8, :]
                    pool.wait_ge(k_rden, T + 1)
                    wait(pool, k_m, T - 1)
                    link(nc.gpsimd.tensor_tensor(r, rsm[0:n, 4 + k, :], rsm[0:n, 6 + k, :], ALU.mult))
                    link(nc.gpsimd.tensor_tensor(r, r, rt[0:n, k, :], ALU.mult))
                    link(nc.gpsimd.tensor_tensor(kh[0:n, k, :, D], r, ones[0:n, 0:H], ALU.mult))
                    nc.gpsimd.tensor_tensor(kh[0:n, k, :, D + 1], r, kh[0:n, k, :, D], ALU.subtract).then_inc(k_r, 1)

                def key_k_low(b, t, half):
                    T, n, k = b * KT + t, size(t), slot(t)
                    hs = slice(half * HH, half * HH + HH)
                    pool.wait_ge(k_khi, 2 * T + half + 1)
                    nc.gpsimd.tensor_tensor(kl[0:n, k, hs, :], by_head(ks[0:n, k, half * HW:half * HW + HW]), kh[0:n, k, hs, 0:D],
                                            ALU.subtract).then_inc(k_klo, 1)

                def out_bias(i, k):
                    pool.wait_ge(b_ld[k], (i - k) * 8 + 16)
                    wait(pool, b_x1, i - 1)
                    nc.gpsimd.tensor_tensor(resb[:, k, :], res[:, k, :], bo, ALU.add).then_inc(b_resb, 1)

                def out_ratios(i, groups):
                    wait(pool, z_t, i)
                    for g in groups:
                        mask = batch_of[:, i + g, :] if isinstance(i, int) else batch_of[:, bass.ds(i + g, 1), :].rearrange("p a b -> p (a b)")
                        ratios = qr[:, i, :] if isinstance(i, int) else qr[:, bass.ds(i, 1), :].rearrange("p a h -> p (a h)")
                        last = nc.gpsimd.tensor_tensor(zf[:, g], mask.unsqueeze(2).to_broadcast([P, BH, H]),
                                                       ratios.unsqueeze(1).to_broadcast([P, BH, H]), ALU.mult)
                    last.then_inc(z_f, 1)

                query_sum_rows(0, 0)

                def query_step(i, k):
                    if has(i - 1):
                        query_parts(i - 1, 1 - k)
                    either(query_sum_rows, key_sum_rows, i + 1, 1 - k)
                    if has(i - 1):
                        query_centred_low(i - 1, 1 - k, 0)
                        query_centred_low(i - 1, 1 - k, 1)
                        query_ratio(i - 1, 1 - k)
                over_tiles(pool, 0, QT - 1, 4, 3, query_step)

                def batch(b):
                    for t in range(KT):
                        if there(b, t - 1):
                            key_parts(b, t - 1)
                        else:
                            query_parts(QT - 1, LASTQ)
                        if there(b, t + 1):
                            key_sum_rows(b, t + 1)
                        if there(b, t - 1):
                            key_k_low(b, t - 1, 0)
                            key_ratio(b, t - 1)
                            key_k_low(b, t - 1, 1)
                        else:
                            query_centred_low(QT - 1, LASTQ, 0)
                            query_centred_low(QT - 1, LASTQ, 1)
                            query_ratio(QT - 1, LASTQ)
                over_batches(pool, batch)
                pool.memset(smask, 0.0).then_inc(x_zero, 1)
                key_parts(NB - 1, KT - 1)
                key_k_low(NB - 1, KT - 1, 0)
                key_ratio(NB - 1, KT - 1)
                key_k_low(NB - 1, KT - 1, 1)
                link = chain(pool, x_batch_of)
                link(pool.memset(batch_of, 1.0))
                for e0, e1, shift in ((0, MID + 1, 0), (MID + 1, QT + 1, -P - SPLIT)):
                    part = batch_of[:, e0:e1, :]
                    link(pool.affine_select(out=part, in_=part, compare_op=ALU.is_ge, fill=0.0, base=P * e0 + shift,
                                            pattern=[[P, e1 - e0], [-NQ, BH]], channel_multiplier=1))
                    link(pool.affine_select(out=part, in_=part, compare_op=ALU.is_ge, fill=0.0, base=NQ - 1 - P * e0 - shift,
                                            pattern=[[-P, e1 - e0], [NQ, BH]], channel_multiplier=-1))
                pool.wait_ge(x_umax, 1)
                pool.partition_all_reduce(col(UMAX), col(TMP), P, RMAX).then_inc(x_umax, 1)
                out_ratios(0, (0,))
                pool.wait_ge(ld_bo, 16)

                def out_step(i, k, groups):
                    if has(i + 1):
                        out_ratios(i + 1, groups_of(i + 1, groups))
                    out_bias(i, k)
                over_out_tiles(pool, out_step)

            @block.tensor
            def _(pe):
                def query_turn(i, k):
                    pe.wait_ge(q_xhat, i + 1)
                    wait(pe, q_lo, i)
                    transpose_rows(XT, xh[:, k, :], P).then_inc(q_xT, 1)

                def query_proj(i, k, half):
                    pe.wait_ge(q_lo, i + 1)
                    wait(pe, q_cent, 2 * i + half - 3)
                    project(Q_PR[(2 * k + half) % 4], xTh[:, k], xTl[:, k], P, half).then_inc(q_proj, 1)

                def query_turn_hat(i, k, half):
                    pe.wait_ge(q_hat, 2 * i + half + 1)
                    wait(pe, q_trc, 2 * i + half)
                    for n in range(HH):
                        at = half * HW + n * D
                        last = nc.tensor.transpose(TR[:, n * P:n * P + P], qs[:, k, at:at + D], ident[:, :])
                    last.then_inc(q_tr, 1)

                def query_correlate(i, k):
                    pe.wait_ge(q_qcl, 2 * i + 2)
                    for h in range(H):
                        at = slice(h * D, h * D + D)
                        bank = FC[h // HH][:, (h % HH) * D:(h % HH) * D + D]
                        first, end = isinstance(i, int) and i == 0 and h % HH == 0, isinstance(i, int) and i == QT - 1
                        last = split_product(bank, P, qch[:, k, at], qcl[:, k, at], qch[:, k, at], qcl[:, k, at], first, end)
                    last.then_inc(q_fc, 1)

                def key_turn(b, t):
                    T, n = b * KT + t, size(t)
                    pe.wait_ge(k_xhat, T + 1)
                    wait(pe, k_lo, T)
                    if at_seam(T):
                        pe.wait_ge(q_lo, QT)
                    transpose_rows(XT, xh[:, slot(t), :], n).then_inc(k_xT, 1)

                def key_proj(b, t, half):
                    T, n = b * KT + t, size(t)
                    pe.wait_ge(k_lo, T + 1)
                    wait(pe, k_kt, 2 * T + half - 2)
                    if at_seam(T) and 2 * T + half < 3:
                        pe.wait_ge(q_cent, 2 * QT - 2 + T)
                    project(K_PR[(2 * t + half) % 3], xTh[:, slot(t)], xTl[:, slot(t)], n, half).then_inc(k_proj, 1)

                def key_outer(b, t):
                    T, n, k = b * KT + t, size(t), slot(t)
                    pe.wait_ge(k_klo, 2 * T + 2)
                    pe.wait_ge(k_r, T + 1)
                    if t % KT == 0:
                        wait(pe, k_mev, b + t // KT)
                    if at_seam(T) and T == 0:
                        pe.wait_ge(q_cent, 2 * QT)
                        pe.wait_ge(q_trc, 2 * QT)
                        pe.wait_ge(q_fev, 1)
                    for h in range(H):
                        bank, at = MM[h // MB], h % MB * MC
                        hi, lo = kh[0:n, k, h, 0:D], kl[0:n, k, h, :]
                        end = t % KT == KT - 1
                        nc.tensor.matmul(bank[:, at:at + MC], hi, kh[0:n, k, h, :], start=(t % KT == 0 and h % MB == 0), stop=False,
                                         skip_group_check=True)
                        nc.tensor.matmul(bank[:, at:at + D], hi, lo, start=False, stop=False, skip_group_check=True)
                        last = nc.tensor.matmul(bank[:, at:at + D + 1], lo, kh[0:n, k, h, 0:D + 1], start=False, stop=end,
                                                skip_group_check=True)
                    last.then_inc(k_m, 1)

                def key_apply(b, g):
                    pe.wait_ge(k_mev, b + 1)
                    wait(pe, k_uev, 2 * b + g)
                    if isinstance(b, int) and b == 0:
                        pe.wait_ge(q_fev, 2)
                    for n in range(HH):
                        h = g * HH + n
                        at = slice(b * NQ, b * NQ + NQ) if isinstance(b, int) else bass.ds(b * NQ, NQ)
                        last = nc.tensor.matmul(UU[:, n * NQ:n * NQ + NQ], msb[:, h, 0:D], qu[:, h, at], start=True, stop=True,
                                                skip_group_check=True)
                    last.then_inc(k_u, 1)

                def out_turn(i, k):
                    pe.wait_ge(b_xhat, i + 1)
                    wait(pe, b_lo, i)
                    transpose_rows(B_XT, xh[:, k, :], P).then_inc(b_xT, 1)

                def out_routed(i, k):
                    pe.wait_ge(b_lo, i + 1)
                    wait(pe, b_x2, i - 1)
                    for c in range(CH):
                        last = split_product(FF[k], P, yTh[:, c, :], yTl[:, c, :], fh[:, c, :], fl[:, c, :], c == 0, c == CH - 1)
                    last.then_inc(b_f, 1)

                def out_turn_ratios(i, k, groups):
                    pe.wait_ge(z_f, i + 1)
                    wait(pe, z_l, i)
                    for g in groups:
                        last = nc.tensor.transpose(ZT[:, (2 * k + g) * P:(2 * k + g) * P + P], zf[:, g].rearrange("p b k -> p (b k)"), ident[:, :])
                    last.then_inc(z_t, 1)

                query_turn(0, 0)

                def query_step(i, k):
                    either(query_turn, key_turn, i + 1, 1 - k)
                    query_proj(i, k, 0)
                    if has(i - 2):
                        query_correlate(i - 2, k)
                    if has(i - 1):
                        query_turn_hat(i - 1, 1 - k, 0)
                    query_proj(i, k, 1)
                    if has(i - 1):
                        query_turn_hat(i - 1, 1 - k, 1)
                over_tiles(pe, 0, QT - 1, 4, 3, query_step)

                def batch(b):
                    for t in range(KT):
                        if there(b, t + 1):
                            key_turn(b, t + 1)
                        key_proj(b, t, 0)
                        if there(b, t - 2):
                            key_outer(b, t - 2)
                        else:
                            query_correlate(QT - 2 + t, (QT + t) % 2)
                        if not there(b, t - 1):
                            query_turn_hat(QT - 1, LASTQ, 0)
                        key_proj(b, t, 1)
                        if not there(b, t - 1):
                            query_turn_hat(QT - 1, LASTQ, 1)
                        if t in (2, 3) and there(b, t - KT):
                            key_apply(b - 1, t - 2)
                over_batches(pe, batch)
                pe.wait_ge(k_acc, NKT)
                pe.wait_ge(k_lo, NKT)
                for c in range(CH):
                    for k, acc in enumerate((acc_q, acc_k)):
                        nc.tensor.matmul(XT[:, k * CH + c:k * CH + c + 1], acc[:, c * P:c * P + P], ones[:, 0:1],
                                         start=True, stop=True, skip_group_check=True)
                pe.wait_ge(q_fev, 4)
                nc.tensor.matmul(XT[0:H, 2 * CH:2 * CH + 1], fs[:, :], ones[:, 0:1], start=True, stop=True, skip_group_check=True).then_inc(x_sums, 1)
                key_outer(NB - 1, KT - 2)
                pe.wait_ge(x_means, 3)
                for h in range(H):
                    for c in range(CH):
                        at, dst = slice(h * D, h * D + D), N_GLOBAL[:, 2 * h:2 * h + 2]
                        nc.tensor.matmul(dst, wh[:, c, at], xmh[:, :, c], start=(c == 0 and h == 0), stop=False, skip_group_check=True)
                        nc.tensor.matmul(dst, wh[:, c, at], xml[:, :, c], start=False, stop=False, skip_group_check=True)
                        last = nc.tensor.matmul(dst, wl[:, c, at], xmh[:, :, c], start=False, stop=(c == CH - 1), skip_group_check=True)
                last.then_inc(x_global, 1)

                def rank_product(g, heads):
                    for h in heads:
                        last = nc.tensor.matmul(RB[g][:, :], smask[:, h, g].rearrange("p b k -> p (b k)"), woT[:, h, :],
                                                start=(h == 0), stop=(h == H - 1))
                    return last
                pe.wait_ge(x_smask, 1)
                pe.wait_ge(k_kt, 2 * NKT - 2)
                rank_product(0, range(HH))
                pe.wait_ge(x_feat, 1)
                for k in range(2):
                    last = nc.tensor.matmul(N_HIDDEN, feat[:, k, :], w1T[:, k, :], start=(k == 0), stop=(k == 1), skip_group_check=True)
                last.then_inc(x_hidden, 1)
                rank_product(0, range(HH, H)).then_inc(x_rb, 1)
                pe.wait_ge(x_h1, 1)
                nc.tensor.transpose(N_H1T, h1[0:H, :], ident[0:H, 0:H]).then_inc(x_h1_turned, 1)
                key_outer(NB - 1, KT - 1)
                pe.wait_ge(x_h1T, 1)
                nc.tensor.matmul(N_OUT, h1T, w2T[:, :], start=True, stop=True, skip_group_check=True).then_inc(x_out, 1)
                key_apply(NB - 1, 0)
                key_apply(NB - 1, 1)
                pe.wait_ge(x_smask, 2)
                pe.wait_ge(k_kt, 2 * NKT)
                rank_product(1, range(2))
                pe.wait_ge(x_diag, 1)
                nc.tensor.matmul(N_SPREAD, ones[0:H, :], diag[0:H].rearrange("p k h -> p (k h)"), start=True, stop=True, skip_group_check=True)
                nc.tensor.matmul(N_WROW, tiled[0:H, :], wcol[0:H, :], start=True, stop=True, skip_group_check=True).then_inc(x_spread, 1)
                rank_product(1, range(2, H)).then_inc(x_rb, 1)
                pe.wait_ge(k_uev, 2 * NB)
                out_turn_ratios(0, 0, (0,))

                def out_step(i, k, groups):
                    pe.wait_ge(b_ul, i + 1)
                    wait(pe, b_x1, i - 1)
                    for h in range(H):
                        if isinstance(i, int) and i == 0:
                            pe.wait_ge(x_wol, h + 1)
                        split_product(OO[k], P, uh[:, k, h, :], ul[:, k, h, :], wo(wh, h), wo(wl, h), h == 0, False)
                        if h == 1 and has(i + 1):
                            out_turn_ratios(i + 1, 1 - k, groups_of(i + 1, groups))
                        if h == HH and has(i - 1):
                            out_turn(i - 1, 1 - k)
                    pe.wait_ge(z_l, i + 1)
                    if isinstance(i, int) and i == 0:
                        pe.wait_ge(x_rl, 2)
                    for g in groups:
                        last = split_product(OO[k], P, zh[:, k, g, :], zl[:, k, g, :], rh[:, g, :], rl[:, g, :], False, g == groups[-1])
                    last.then_inc(b_o, 1)
                    if has(i - 1):
                        out_routed(i - 1, 1 - k)
                over_out_tiles(pe, out_step)
                out_turn(QT - 1, (QT - 1) % 2)
                out_routed(QT - 1, (QT - 1) % 2)

            @block.scalar
            def _(act):
                def query_deviation(i, k):
                    act.wait_ge(q_mv, i + 1)
                    nc.scalar.activation(std[:, k:k + 1], mv[:, k, 1:2], ACT.Sqrt, bias=col(EPS_Q),
                                         scale=(1.0 + EPS) / XS ** 2).then_inc(q_std, 1)

                def query_normalise(i, k):
                    act.wait_ge(q_aff, i + 1)
                    wait(act, q_xT, i - 1)
                    wait(act, q_acc, i - 1)
                    nc.scalar.activation(xh[:, k, 0:DIM - 1], xin[:, k, 0:DIM - 1], ACT.Identity, bias=aff[:, k, 1:2],
                                         scale=aff[:, k, 0:1]).then_inc(q_xhat, 1)

                def query_high(i, k):
                    act.wait_ge(q_xT, i + 1)
                    wait(act, q_proj, 2 * i - 2)
                    nc.scalar.activation(xTh[:, k], chunks(XT, P), ACT.Copy).then_inc(q_hi, 1)

                def query_norm(i, k):
                    act.wait_ge(q_ss, i + 1)
                    nc.scalar.activation(nrm[:, k, :], ss[:, k, :], ACT.Sqrt).then_inc(q_nrm, 1)

                def query_hat_out(i, k, half):
                    act.wait_ge(q_tr, 2 * i + half + 1)
                    nc.scalar.activation(qu[:, half * HH:half * HH + HH, rows(i)], by_head(TR[:, :]), ACT.Copy).then_inc(q_trc, 1)

                def query_centred_high(i, k, half):
                    act.wait_ge(q_cent, 2 * i + half + 1)
                    wait(act, q_fc, i - 1)
                    at = slice(half * HW, half * HW + HW)
                    nc.scalar.activation(qch[:, k, at], qc[:, k, at], ACT.Copy).then_inc(q_qch, 1)

                def key_deviation(b, t):
                    T, n, k = b * KT + t, size(t), slot(t)
                    act.wait_ge(k_mv, T + 1)
                    nc.scalar.activation(std[0:n, k:k + 1], mv[0:n, k, 1:2], ACT.Sqrt, bias=col(EPS_K, n),
                                         scale=1.0 / XS ** 2).then_inc(k_std, 1)

                def key_normalise(b, t):
                    T, n, k = b * KT + t, size(t), slot(t)
                    act.wait_ge(k_aff, T + 1)
                    wait(act, k_xT, T - 1)
                    wait(act, k_acc, T - 1)
                    if at_seam(T):
                        act.wait_ge(q_xT, QT + T - 1)
                        act.wait_ge(q_acc, QT + T - 1)
                    nc.scalar.activation(xh[0:n, k, 0:DIM - 1], cin[0:n, t % KT, 0:DIM - 1], ACT.Identity, bias=aff[0:n, k, 1:2],
                                         scale=aff[0:n, k, 0:1]).then_inc(k_xhat, 1)

                def key_high(b, t):
                    T, n, k = b * KT + t, size(t), slot(t)
                    act.wait_ge(k_xT, T + 1)
                    wait(act, k_proj, 2 * T - 2)
                    if at_seam(T):
                        act.wait_ge(q_proj, 2 * (QT + T) - 2)
                    nc.scalar.activation(xTh[:, k, :, 0:n], chunks(XT, n), ACT.Copy).then_inc(k_hi, 1)

                def key_roots(b, t):
                    T, n, k = b * KT + t, size(t), slot(t)
                    act.wait_ge(k_ss, T + 1)
                    nc.scalar.activation(nrm[0:n, k, :], ss[0:n, k, :], ACT.Sqrt).then_inc(k_nrm, 1)
                    act.wait_ge(k_nrm, T + 1)
                    wait(act, k_r, T - 1)
                    nc.scalar.activation(rt[0:n, k, :], nrm[0:n, k, :], ACT.Sqrt).then_inc(k_rt, 1)

                def key_k_high(b, t, half):
                    T, n, k = b * KT + t, size(t), slot(t)
                    act.wait_ge(k_kt, 2 * T + half + 1)
                    wait(act, k_m, T - 1)
                    if at_seam(T):
                        act.wait_ge(q_qcl, 2 * QT)
                    hs = slice(half * HH, half * HH + HH)
                    nc.scalar.activation(kh[0:n, k, hs, 0:D], by_head(ks[0:n, k, half * HW:half * HW + HW]), ACT.Copy).then_inc(k_khi, 1)

                def key_m_out(b):
                    act.wait_ge(k_m, (b + 1) * KT)
                    wait(act, k_u, 2 * b)
                    wait(act, k_sum, b)
                    for g, bank in enumerate(MM):
                        hs = slice(g * MB, min(g * MB + MB, H))
                        w = (hs.stop - hs.start) * MC
                        last = nc.scalar.activation(msb[:, hs, :], bank[:, 0:w].rearrange("p (h m) -> p h m", m=MC), ACT.Copy)
                    last.then_inc(k_mev, 1)

                def key_u_out(b, g):
                    act.wait_ge(k_u, 2 * b + g + 1)
                    at = slice(b * NQ, b * NQ + NQ) if isinstance(b, int) else bass.ds(b * NQ, NQ)
                    nc.scalar.activation(qu[:, g * HH:g * HH + HH, at], UU[:, 0:HH * NQ].rearrange("p (h n) -> p h n", h=HH),
                                         ACT.Copy).then_inc(k_uev, 1)

                def out_u_high(i, k):
                    wait(act, b_o, i - 1)
                    nc.scalar.activation(uh[:, k], qu[:, :, rows(i)], ACT.Copy, scale=col(US)).then_inc(b_uh, 1)

                def out_deviation(i, k):
                    act.wait_ge(b_mv, i + 1)
                    nc.scalar.activation(std[:, k:k + 1], mv[:, k, 1:2], ACT.Sqrt, bias=col(EPS_K), scale=1.0 / XS ** 2).then_inc(b_std, 1)

                def out_normalise(i, k):
                    act.wait_ge(b_aff, i + 1)
                    wait(act, b_xT, i - 1)
                    nc.scalar.activation(xh[:, k, 0:DIM - 1], x1[:, k, 0:DIM - 1], ACT.Identity, bias=aff[:, k, 1:2],
                                         scale=aff[:, k, 0:1]).then_inc(b_xhat, 1)

                def out_high(i, k):
                    act.wait_ge(b_xT, i + 1)
                    wait(act, b_f, i)
                    nc.scalar.activation(yTh, chunks(B_XT, P), ACT.Copy).then_inc(b_hi, 1)

                def out_store(i, k):
                    act.wait_ge(b_x2, i + 1)
                    act.dma_start(outf[rows(i), :], x2[:, k, :]).then_inc(b_st[k], 16)

                def out_ratios_high(i, k, groups):
                    act.wait_ge(z_t, i + 1)
                    wait(act, b_o, i - 1)
                    g, n = groups[0], len(groups)
                    nc.scalar.activation(zh[:, k, g:g + n, :], ZT[:, (2 * k + g) * P:(2 * k + g + n) * P].rearrange("p (g n) -> p g n", g=n),
                                         ACT.Copy).then_inc(z_h, 1)

                for i in range(2):
                    query_deviation(i, i)
                    query_normalise(i, i)
                query_high(0, 0)

                def query_step(i, k):
                    if has(i - 1):
                        query_norm(i - 1, 1 - k)
                    either(query_deviation, key_deviation, i + 2, k)
                    either(query_high, key_high, i + 1, 1 - k)
                    either(query_normalise, key_normalise, i + 2, k)
                    if has(i - 1):
                        query_hat_out(i - 1, 1 - k, 0)
                        query_centred_high(i - 1, 1 - k, 0)
                        query_centred_high(i - 1, 1 - k, 1)
                        query_hat_out(i - 1, 1 - k, 1)
                over_tiles(act, 0, QT - 1, 4, 3, query_step)

                def batch(b):
                    for t in range(KT):
                        if there(b, t - 1):
                            key_roots(b, t - 1)
                        else:
                            query_norm(QT - 1, LASTQ)
                        if there(b, t + 2):
                            key_deviation(b, t + 2)
                        if there(b, t + 1):
                            key_high(b, t + 1)
                        if there(b, t + 2):
                            key_normalise(b, t + 2)
                        if there(b, t - 1):
                            key_k_high(b, t - 1, 0)
                            key_k_high(b, t - 1, 1)
                        else:
                            query_hat_out(QT - 1, LASTQ, 0)
                            query_centred_high(QT - 1, LASTQ, 0)
                            query_centred_high(QT - 1, LASTQ, 1)
                            query_hat_out(QT - 1, LASTQ, 1)
                        if t == 1 and there(b, t - KT):
                            key_m_out(b - 1)
                        if t in (3, 4) and there(b, t - KT):
                            key_u_out(b - 1, t - 3)
                over_batches(act, batch)
                key_roots(NB - 1, KT - 1)
                key_k_high(NB - 1, KT - 1, 0)
                key_k_high(NB - 1, KT - 1, 1)
                act.wait_ge(x_means, 1)
                nc.scalar.activation(sm[0:H, 0:1], sm[0:H, 12:13], ACT.Sqrt).then_inc(x_norm, 1)
                act.wait_ge(x_var, 1)
                nc.scalar.activation(sm[0:H, 3:4], sm[0:H, 2:3], ACT.Sqrt, bias=col(EPS_1, H)).then_inc(x_std, 1)
                key_m_out(NB - 1)
                act.wait_ge(x_less_max, 1)
                nc.scalar.activation(sm[0:H, 16:19], sm[0:H, 8:11], ACT.Exp, accum_out=sm[0:H, 5:6])
                nc.scalar.activation(sm[0:H, 6:7], sm[0:H, 1:2], ACT.Exp, scale=-5.0 / (4.0 * NR * D * D)).then_inc(x_exp, 1)
                key_u_out(NB - 1, 0)
                key_u_out(NB - 1, 1)
                act.wait_ge(x_us, 1)
                act.wait_ge(k_klo, 2 * NKT)
                out_u_high(0, 0)
                act.wait_ge(x_aw, 1)
                act.wait_ge(x_global, 1)
                for h in range(H):
                    nc.scalar.activation(wo(wh, h), woT[:, h, :], ACT.Copy, scale=aw[:, 0, h:h + 1]).then_inc(x_woh, 1)
                out_ratios_high(0, 0, (0,))
                for g in range(NG):
                    act.wait_ge(x_rb, g + 1)
                    act.wait_ge(x_wrow, 1)
                    nc.scalar.activation(rh[:, g, :], RB[g][:, :], ACT.Copy, scale=wrow).then_inc(x_rh, 1)

                def out_step(i, k, groups):
                    if has(i + 1):
                        out_u_high(i + 1, 1 - k)
                        out_ratios_high(i + 1, 1 - k, groups_of(i + 1, groups))
                    if has(i - 1):
                        out_high(i - 1, 1 - k)
                    if has(i - 2):
                        out_store(i - 2, k)
                    out_deviation(i, k)
                    out_normalise(i, k)
                over_out_tiles(act, out_step)
                out_high(QT - 1, (QT - 1) % 2)
                out_store(QT - 2, (QT - 2) % 2)
                out_store(QT - 1, (QT - 1) % 2)
                act.wait_ge(b_st[0], 16 * ((QT + 1) // 2))
                act.wait_ge(b_st[1], 16 * (QT // 2))

            @block.vector
            def _(dve):
                def query_moments(i, k):
                    dve.wait_ge(q_ld[k], (i - k) * 8 + 16)
                    nc.vector.bn_stats(bst[:, k, :], xin[:, k, :]).then_inc(q_bn, 1)
                    dve.wait_ge(q_bn, i + 1)
                    nc.vector.tensor_copy(bcnt[:, :], bst[:, k, 0:1])
                    nc.vector.bn_aggr(mv[:, k, :], bst[:, k, :]).then_inc(q_mv, 1)

                def query_affine(i, k):
                    dve.wait_ge(q_std, i + 1)
                    wait(dve, q_xhat, i - 1)
                    nc.vector.reciprocal(aff[:, k, 0:1], std[:, k:k + 1]).then_inc(q_rinv, 1)
                    dve.wait_ge(q_rinv, i + 1)
                    nc.vector.tensor_scalar(aff[:, k, 1:2], mv[:, k, 0:1], aff[:, k, 0:1], -1.0, ALU.mult, ALU.mult).then_inc(q_aff, 1)

                def query_rest(i, k):
                    dve.wait_ge(q_hi, i + 1)
                    nc.vector.tensor_tensor(xTl[:, k], chunks(XT, P), xTh[:, k], ALU.subtract).then_inc(q_lo, 1)

                def query_stats(i, k, half):
                    dve.wait_ge(q_proj, 2 * i + half + 1)
                    wait(dve, q_parts, i - 1)
                    last = head_stats(Q_PR[(2 * k + half) % 4], k, P, half)
                    if half == 1:
                        link = chain(dve, q_sums, i * 3)
                        link(last)
                        head_squares(link, k, P).then_inc(q_ss, 1)

                def query_hats(i, k):
                    dve.wait_ge(q_nrm, i + 1)
                    nc.vector.reciprocal(rc[:, k, :], nrm[:, k, :]).then_inc(q_rc, 1)
                    dve.wait_ge(q_rc, i + 1)
                    for half in range(2):
                        J = 2 * i + half
                        bank, at, hs = by_head(Q_PR[(2 * k + half) % 4][:, :]), slice(half * HW, half * HW + HW), slice(half * HH, half * HH + HH)
                        wait(dve, q_tr, J - 3)
                        nc.vector.tensor_tensor(by_head(qs[:, k, at]), bank, spread(rc[:, k, hs], P, HH), ALU.mult).then_inc(q_hat, 1)

                def query_centre(i, k):
                    nc.vector.tensor_tensor(mean2[:, :], hb[:, k, :, 1], hb[:, k, :, 4], ALU.add).then_inc(q_mean, 1)
                    dve.wait_ge(q_mean, i + 1)
                    for half in range(2):
                        J = 2 * i + half
                        bank, at, hs = by_head(Q_PR[(2 * k + half) % 4][:, :]), slice(half * HW, half * HW + HW), slice(half * HH, half * HH + HH)
                        wait(dve, q_qcl, J - 3)
                        nc.vector.scalar_tensor_tensor(out=by_head(qc[:, k, at]), in0=bank, scalar=2.0, in1=spread(mean2[:, hs], P, HH),
                                                       op0=ALU.mult, op1=ALU.subtract).then_inc(q_cent, 1)

                def query_invert(i, k):
                    dve.wait_ge(q_parts, i + 1)
                    ratio_terms(chain(dve, q_term, i * 2), k, P, C_DENQ, 0.5 / QR_SCALE).then_inc(q_rden, 1)

                def key_moments(b, t):
                    T, n, k = b * KT + t, size(t), slot(t)
                    dve.wait_ge(k_ld[t % KT], (b + t // KT) * 16 + 16)
                    nc.vector.bn_stats(bst[0:n, k, :], cin[0:n, t % KT, :]).then_inc(k_bn, 1)
                    dve.wait_ge(k_bn, T + 1)
                    nc.vector.tensor_copy(bcnt[0:n, :], bst[0:n, k, 0:1])
                    nc.vector.bn_aggr(mv[0:n, k, :], bst[0:n, k, :]).then_inc(k_mv, 1)

                def key_affine(b, t):
                    T, n, k = b * KT + t, size(t), slot(t)
                    dve.wait_ge(k_std, T + 1)
                    wait(dve, k_xhat, T - 1)
                    if at_seam(T):
                        dve.wait_ge(q_xhat, QT + T - 1)
                    nc.vector.reciprocal(aff[0:n, k, 0:1], std[0:n, k:k + 1]).then_inc(k_rinv, 1)
                    dve.wait_ge(k_rinv, T + 1)
                    nc.vector.tensor_scalar(aff[0:n, k, 1:2], mv[0:n, k, 0:1], aff[0:n, k, 0:1], -1.0, ALU.mult, ALU.mult).then_inc(k_aff, 1)

                def key_rest(b, t):
                    T, n, k = b * KT + t, size(t), slot(t)
                    dve.wait_ge(k_hi, T + 1)
                    nc.vector.tensor_tensor(xTl[:, k, :, 0:n], chunks(XT, n), xTh[:, k, :, 0:n], ALU.subtract).then_inc(k_lo, 1)

                def key_stats(b, t, half):
                    T, n, k = b * KT + t, size(t), slot(t)
                    dve.wait_ge(k_proj, 2 * T + half + 1)
                    wait(dve, k_parts, T - 1)
                    if at_seam(T):
                        dve.wait_ge(q_parts, QT + T - 1)
                    last = head_stats(K_PR[(2 * t + half) % 3], k, n, half)
                    if half == 1:
                        link = chain(dve, k_sums, T * 3)
                        link(last)
                        head_squares(link, k, n).then_inc(k_ss, 1)

                def key_tilde(b, t):
                    T, n, k = b * KT + t, size(t), slot(t)
                    dve.wait_ge(k_rt, T + 1)
                    if at_seam(T):
                        dve.wait_ge(q_tr, 2 * QT)
                    nc.vector.reciprocal(rc[0:n, k, :], rt[0:n, k, :]).then_inc(k_rc, 1)
                    dve.wait_ge(k_rc, T + 1)
                    for half in range(2):
                        hs = slice(half * HH, half * HH + HH)
                        wait(dve, k_klo, 2 * T + half - 3)
                        nc.vector.tensor_tensor(by_head(ks[0:n, k, half * HW:half * HW + HW]), by_head(K_PR[(2 * t + half) % 3][0:n, :]),
                                                spread(rc[0:n, k, hs], n, HH), ALU.mult).then_inc(k_kt, 1)

                def key_invert(b, t):
                    T, n, k = b * KT + t, size(t), slot(t)
                    dve.wait_ge(k_parts, T + 1)
                    ratio_terms(chain(dve, k_term, T * 2), k, n, C_DENK, 0.5).then_inc(k_rden, 1)
                    return nc.vector.tensor_tensor(nmax[0:n, :], nmax[0:n, :], nrm[0:n, k, :], ALU.max)

                def key_sum_out(b):
                    dve.wait_ge(k_mev, b + 1)
                    dst = ksum[:, :, one(b)].rearrange("p h a -> p (h a)")
                    nc.vector.tensor_tensor(dst, msb[:, :, D], msb[:, :, D + 1], ALU.add).then_inc(k_sum, 1)

                def out_u_low(i, k):
                    dve.wait_ge(b_uh, i + 1)
                    nc.vector.scalar_tensor_tensor(out=ul[:, k], in0=qu[:, :, rows(i)], scalar=col(US), in1=uh[:, k],
                                                   op0=ALU.mult, op1=ALU.subtract).then_inc(b_ul, 1)

                def out_residual(i, k):
                    dve.wait_ge(b_o, i + 1)
                    dve.wait_ge(b_resb, i + 1)
                    wait(dve, b_x2, i - 1)
                    nc.vector.scalar_tensor_tensor(out=x1[:, k, :], in0=OO[k][:, :], scalar=col(O_INV), in1=resb[:, k, :],
                                                   op0=ALU.mult, op1=ALU.add).then_inc(b_x1, 1)

                def out_moments(i, k):
                    dve.wait_ge(b_x1, i + 1)
                    nc.vector.bn_stats(bst[:, k, :], x1[:, k, :]).then_inc(b_bn, 1)
                    dve.wait_ge(b_bn, i + 1)
                    nc.vector.tensor_copy(bcnt[:, :], bst[:, k, 0:1])
                    nc.vector.bn_aggr(mv[:, k, :], bst[:, k, :]).then_inc(b_mv, 1)
                    dve.wait_ge(b_std, i + 1)
                    nc.vector.reciprocal(aff[:, k, 0:1], std[:, k:k + 1]).then_inc(b_rinv, 1)
                    dve.wait_ge(b_rinv, i + 1)
                    nc.vector.tensor_scalar(aff[:, k, 1:2], mv[:, k, 0:1], aff[:, k, 0:1], -1.0, ALU.mult, ALU.mult).then_inc(b_aff, 1)

                def out_rest(i, k):
                    dve.wait_ge(b_hi, i + 1)
                    nc.vector.tensor_tensor(yTl, chunks(B_XT, P), yTh, ALU.subtract).then_inc(b_lo, 1)

                def out_finish(i, k):
                    dve.wait_ge(b_f, i + 1)
                    if has(i - 2):
                        dve.wait_ge(b_st[k], (i - k) * 8)
                    nc.vector.scalar_tensor_tensor(out=x2[:, k, :], in0=FF[k][:, :], scalar=col(F_INV), in1=x1[:, k, :],
                                                   op0=ALU.mult, op1=ALU.add).then_inc(b_x2, 1)

                def out_ratios_low(i, k, groups):
                    dve.wait_ge(z_h, i + 1)
                    g, n = groups[0], len(groups)
                    nc.vector.tensor_tensor(zl[:, k, g:g + n, :], ZT[:, (2 * k + g) * P:(2 * k + g + n) * P].rearrange("p (g n) -> p g n", g=n),
                                            zh[:, k, g:g + n, :], ALU.subtract).then_inc(z_l, 1)

                for i in range(2):
                    query_moments(i, i)
                    query_affine(i, i)
                query_rest(0, 0)

                def query_step(i, k):
                    either(query_moments, key_moments, i + 2, k)
                    if has(i - 1):
                        query_hats(i - 1, 1 - k)
                    either(query_affine, key_affine, i + 2, k)
                    if has(i - 1):
                        query_centre(i - 1, 1 - k)
                    either(query_rest, key_rest, i + 1, 1 - k)
                    query_stats(i, k, 0)
                    if has(i - 1):
                        query_invert(i - 1, 1 - k)
                    query_stats(i, k, 1)
                over_tiles(dve, 0, QT - 1, 4, 3, query_step)

                off_diagonal = chain(dve, q_fev)

                def correlations(g):
                    dve.wait_ge(q_fc, QT)
                    off_diagonal(nc.vector.scalar_tensor_tensor(out=fsb[:, g * HH:g * HH + HH, :],
                                                                in0=ident[:, :].unsqueeze(1).to_broadcast([P, HH, D]), scalar=-1.0,
                                                                in1=by_head(FC[g][:, :]), op0=ALU.add, op1=ALU.mult))

                def batch(b):
                    for t in range(KT):
                        if isinstance(b, int) and b == 0:
                            if t == 2:
                                correlations(0)
                            if t == 3:
                                correlations(1)
                            if t == 4:
                                off_diagonal(nc.vector.tensor_tensor(fsb, fsb, fsb, ALU.mult))
                            if t == 5:
                                off_diagonal(nc.vector.tensor_reduce(fs[:, :], fsb, AX.X, ALU.add))
                        if there(b, t + 2):
                            key_moments(b, t + 2)
                        if there(b, t - 1):
                            key_tilde(b, t - 1)
                        else:
                            query_hats(QT - 1, LASTQ)
                        if there(b, t + 2):
                            key_affine(b, t + 2)
                        if not there(b, t - 1):
                            query_centre(QT - 1, LASTQ)
                        if there(b, t + 1):
                            key_rest(b, t + 1)
                        key_stats(b, t, 0)
                        if there(b, t - 1):
                            key_invert(b, t - 1)
                        else:
                            query_invert(QT - 1, LASTQ)
                        if t == 3 and there(b, t - KT):
                            key_sum_out(b - 1)
                        key_stats(b, t, 1)
                over_batches(dve, batch)

                v = nc.vector
                link = chain(dve, x_dve)

                def spread_sums(g):
                    for h in range(H):
                        last = v.tensor_copy(smask[:, h, g, :, h], ksum[:, h, g * BH:g * BH + BH])
                    last.then_inc(x_smask, 1)
                dve.wait_ge(x_zero, 1)
                dve.wait_ge(k_sum, NB - 1)
                spread_sums(0)
                key_tilde(NB - 1, KT - 1)
                means = chain(dve, x_means)
                dve.wait_ge(x_sums, 1)
                for k, n in enumerate((NR, NB * NK)):
                    v.tensor_scalar(xm[:, k, :], XT[:, k * CH:k * CH + CH], 1.0 / n, None, ALU.mult)
                means(v.tensor_copy(sm[0:H, 12:13], XT[0:H, 2 * CH:2 * CH + 1]))
                means(v.tensor_copy(xmh, xm))
                v.tensor_tensor(xml, xm, xmh, ALU.subtract).then_inc(x_means, 1)
                key_invert(NB - 1, KT - 1).then_inc(x_nmax, 1)
                dve.wait_ge(x_nmax, 1)
                v.tensor_reduce(col(TMP), nmax[:, :], AX.X, ALU.max).then_inc(x_umax, 1)
                v.tensor_copy(tiled[0:H, :].rearrange("p (b k) -> p b k", k=H), ident[0:H, 0:H].unsqueeze(1).to_broadcast([H, BH, H]))
                dve.wait_ge(x_global, 1)
                v.tensor_scalar(feat, N_GLOBAL.rearrange("p (h k) -> p k h", k=2), col(INV_A), None, ALU.mult).then_inc(x_feat, 1)
                dve.wait_ge(x_norm, 1)
                v.tensor_scalar(sm[0:H, 1:2], sm[0:H, 0:1], col(INV_A2, H), None, ALU.mult)
                dve.wait_ge(x_hidden, 1)
                link(v.tensor_tensor(h1[0:H, :], N_HIDDEN, b1s[:, :], ALU.add))
                link(v.bn_stats(sm[0:H, 20:26], h1[0:H, :]))
                link(v.bn_aggr(sm[0:H, 26:28], sm[0:H, 20:26]))
                v.tensor_copy(sm[0:H, 2:3], sm[0:H, 27:28]).then_inc(x_var, 1)
                dve.wait_ge(x_std, 1)
                link(v.reciprocal(sm[0:H, 4:5], sm[0:H, 3:4]))
                link(v.tensor_scalar(h1[0:H, :], h1[0:H, :], sm[0:H, 26:27], sm[0:H, 4:5], ALU.subtract, ALU.mult))
                link(v.tensor_tensor(h1[0:H, :], h1[0:H, :], g1s[:, :], ALU.mult))
                link(v.tensor_tensor(h1[0:H, :], h1[0:H, :], be1s[:, :], ALU.add))
                v.tensor_scalar(h1[0:H, :], h1[0:H, :], 0.0, None, ALU.max).then_inc(x_h1, 1)
                dve.wait_ge(x_h1_turned, 1)
                v.tensor_copy(h1T, N_H1T).then_inc(x_h1T, 1)
                dve.wait_ge(x_out, 1)
                link(v.tensor_tensor(sm[0:H, 8:11], N_OUT, b2s[:, :], ALU.add))
                link(v.reduce_max(sm[0:H, 7:8], sm[0:H, 8:11], AX.X))
                v.tensor_scalar(sm[0:H, 8:11], sm[0:H, 8:11], sm[0:H, 7:8], None, ALU.subtract).then_inc(x_less_max, 1)
                key_sum_out(NB - 1)
                dve.wait_ge(k_sum, NB)
                spread_sums(1)
                dve.wait_ge(x_exp, 1)
                link(v.reciprocal(sm[0:H, 11:12], sm[0:H, 5:6]))
                link(v.tensor_scalar(sm[0:H, 16:19], sm[0:H, 16:19], sm[0:H, 11:12], None, ALU.mult))
                link(v.scalar_tensor_tensor(out=sm[0:H, 19:20], in0=sm[0:H, 17:18], scalar=sm[0:H, 6:7], in1=sm[0:H, 16:17],
                                            op0=ALU.mult, op1=ALU.add))
                v.tensor_scalar(diag[0:H, 0, :], ident[0:H, 0:H], sm[0:H, 19:20], 0.5, ALU.mult, ALU.mult)
                v.tensor_scalar(diag[0:H, 1, :], ident[0:H, 0:H], sm[0:H, 18:19], 0.5, ALU.mult, ALU.mult)
                v.tensor_scalar(wcol[0:H, :], sm[0:H, 18:19], 0.5, None, ALU.mult).then_inc(x_diag, 1)
                dve.wait_ge(x_umax, 2)
                link(v.tensor_scalar(col(UMAX), col(UMAX), float(NK), None, ALU.mult))
                power_of_two(v, link, col(UMAX), col(UP), col(US), 2.0 ** 14)
                v.tensor_copy(bcnt[:, :], col(US)).then_inc(x_us, 1)
                link(v.tensor_tensor(col(O_INV), col(UP), col(OP), ALU.mult))
                link(v.tensor_scalar(col(O_INV), col(O_INV), col(INV_A), 2.0 ** -13, ALU.mult, ALU.mult))
                dve.wait_ge(k_uev, 2 * NB)
                out_u_low(0, 0)
                dve.wait_ge(x_spread, 1)
                v.tensor_scalar(aw, N_SPREAD.rearrange("p (k h) -> p k h", k=2), col(OS), None, ALU.mult).then_inc(x_aw, 1)
                link(v.tensor_scalar(wrow, N_WROW, col(OS), 1.0 / QR_SCALE, ALU.mult, ALU.mult))
                v.tensor_scalar(wrow, wrow, col(US), None, ALU.mult).then_inc(x_wrow, 1)
                for h in range(H):
                    dve.wait_ge(x_woh, h + 1)
                    v.scalar_tensor_tensor(out=wo(wl, h), in0=woT[:, h, :], scalar=aw[:, 0, h:h + 1], in1=wo(wh, h),
                                           op0=ALU.mult, op1=ALU.subtract).then_inc(x_wol, 1)
                out_ratios_low(0, 0, (0,))
                for g in range(NG):
                    dve.wait_ge(x_rh, g + 1)
                    v.scalar_tensor_tensor(out=rl[:, g, :], in0=RB[g][:, :], scalar=wrow, in1=rh[:, g, :],
                                           op0=ALU.mult, op1=ALU.subtract).then_inc(x_rl, 1)

                def out_step(i, k, groups):
                    if has(i + 1):
                        out_u_low(i + 1, 1 - k)
                        out_ratios_low(i + 1, 1 - k, groups_of(i + 1, groups))
                    if has(i - 1):
                        out_rest(i - 1, 1 - k)
                    if has(i - 2):
                        out_finish(i - 2, k)
                    out_residual(i, k)
                    out_moments(i, k)
                over_out_tiles(dve, out_step)
                out_rest(QT - 1, (QT - 1) % 2)
                out_finish(QT - 2, (QT - 2) % 2)
                out_finish(QT - 1, (QT - 1) % 2)


_INS = ['x', 'ctx_1024', 'L0_xattn_ln_g', 'L0_xattn_ln_b', 'L0_xattn_w_in', 'L0_xattn_wp_w1', 'L0_xattn_wp_b1',
        'L0_xattn_wp_ln_g', 'L0_xattn_wp_ln_b', 'L0_xattn_wp_w2', 'L0_xattn_wp_b2', 'L0_xattn_w_out', 'L0_xattn_b_out',
        'L0_ffn_W', 'L0_ffn_b', 'L0_ffn_logits', 'L0_ffn_u']
_OUTS = [((32, 100, 512), 'float32')]


def kernel(**inputs):
    import numpy as _np
    import concourse.bacc as _bacc
    from concourse import mybir as _mybir
    from concourse.bass_utils import run_bass_kernel_spmd as _run

    nc = _bacc.Bacc("TRN2", target_bir_lowering=False, num_devices=1)
    arrays, args = {}, []
    for name in _INS:
        a = _np.ascontiguousarray(inputs[name])
        arrays[f"in_{name}_dram"] = a
        args.append(nc.dram_tensor(f"in_{name}_dram", a.shape, _mybir.dt.from_np(a.dtype), kind="ExternalInput").ap())
    for i, (shape, dtype) in enumerate(_OUTS):
        dt = _mybir.dt.from_np(_np.dtype(dtype))
        args.append(nc.dram_tensor(f"out_{i}_dram", shape, dt, kind="ExternalOutput").ap())
    build(nc, *args)
    r = _run(nc, [arrays], core_ids=[0])
    got = tuple(r.results[0][f"out_{i}_dram"] for i in range(len(_OUTS)))
    return got[0]
```

```python
from contextlib import ExitStack

import concourse.bass as bass
from concourse import mybir

ALU = mybir.AluOpType
ACT = mybir.ActivationFunctionType
F32 = mybir.dt.float32
F16 = mybir.dt.float16
I32 = mybir.dt.int32
U32 = mybir.dt.uint32
AX = mybir.AxisListType
RMAX = bass.bass_isa.ReduceOp.max
P = 128
EPS = 1e-5
XS = 16.0
QR_SCALE = 64.0
EXPONENT = 0x7F800000
SCRATCH = 13600


def build(nc, x, ctx_1024, ln_g, ln_b, w_in, wp_w1, wp_b1, wp_ln_g, wp_ln_b, wp_w2, wp_b2,
          w_out, b_out, ffn_W, ffn_b, ffn_logits, ffn_u, out):
    NB, NQ, DIM = x.shape
    NK = ctx_1024.shape[1]
    HD = w_in.shape[0]
    D = P
    H = HD // D
    CH = DIM // P
    HH = H // 2
    HW = HH * D
    NR = NB * NQ
    QT = NR // P
    KT = -(-NK // P)
    KLAST = NK - (KT - 1) * P
    NKT = NB * KT
    RC = 2 + D
    MC = RC + 2
    MB = 3
    BH = P // H
    NG = NB // BH
    SPLIT = BH * NQ
    QG = -(-SPLIT // P) * P
    G1 = SPLIT // P * P
    MID = SPLIT // P
    assert QT * P == NR and NG == 2 and NR - G1 == QG and QT % 2 == 1 and MID % 2 == 0 and KT % 2 == 0

    xf = x.rearrange("b n d -> (b n) d")
    outf = out.rearrange("b n d -> (b n) d")

    with ExitStack() as ctx:
        def sb(name, shape, dt=F32):
            return ctx.enter_context(nc.sbuf_tensor(name, shape, dt))

        def sem(name):
            return ctx.enter_context(nc.semaphore(name))

        banks = [ctx.enter_context(nc.psum_tensor(f"bank{i}", [P, 512], F32)) for i in range(8)]

        qu = sb("qu", [P, H, NR])
        wh = sb("wh", [P, CH, HD], F16)
        wl = sb("wl", [P, CH, HD], F16)
        woT = sb("woT", [P, H, DIM])
        fh = sb("fh", [P, CH, DIM], F16)
        fl = sb("fl", [P, CH, DIM], F16)
        xh = sb("xh", [P, 2, DIM])
        acc_q = sb("acc_q", [P, DIM])
        acc_k = sb("acc_k", [P, DIM])
        ksum = sb("ksum", [P, H, NB])
        qr = sb("qr", [P, QT, H])
        ident = sb("ident", [P, P])
        w1T = sb("w1T", [P, 2, P])
        w2T = sb("w2T", [P, 3])
        b1s = sb("b1s", [H, P])
        g1s = sb("g1s", [H, P])
        be1s = sb("be1s", [H, P])
        b2s = sb("b2s", [H, 3])
        ones = sb("ones", [P, P])
        cf = sb("cf", [P, 28])
        nmax = sb("nmax", [P, H])
        o_tops = sb("o_tops", [P, H])
        bst = sb("bst", [P, 2, 6])
        bcnt = sb("bcnt", [P, 1])
        mv = sb("mv", [P, 2, 2])
        std = sb("std", [P, 2])
        aff = sb("aff", [P, 2, 2])
        hb = sb("hb", [P, 2, H, 6])
        sq = sb("sq", [P, H, 2])
        ss = sb("ss", [P, 2, H])
        nrm = sb("nrm", [P, 2, H])
        rt = sb("rt", [P, 2, H])
        rc = sb("rc", [P, 2, H])
        mean2 = sb("mean2", [P, H])
        rsm = sb("rsm", [P, 9, H])
        scratch = sb("scratch", [P, SCRATCH])

        (EPS_K, EPS_Q, WMAX, WP, WS, INV_A, INV_A2, C_NUM, C_DENK, C_DENQ, FMAX, FP, FSC, F_INV,
         OMAX, OP, OS, UMAX, UP, US, O_INV, TMP, EPS_1, WMAXP, WCOL, FMAXP, OMAXP, HALF) = range(28)

        def col(c, n=P):
            return cf[0:n, c:c + 1]

        class Carve:

            def __init__(self, base, limit):
                self.base, self.at, self.limit = base, 0, limit

            def f32(self, n):
                v = self.base[:, self.at:self.at + n]
                self.at += n
                assert self.at <= self.limit
                return v

            def f16(self, n):
                return self.f32(n // 2).bitcast(F16)

        def chain(eng, s, base=0):
            count = [0]

            def link(ins):
                count[0] += 1
                ins.then_inc(s, 1)
                eng.wait_ge(s, base + count[0])
            return link

        def wait(eng, s, v):
            if isinstance(v, int) and v <= 0:
                return
            eng.wait_ge(s, v)

        def power_of_two(eng, link, m, p, inv, scale):
            link(eng.tensor_scalar(m, m, 1e-30, None, ALU.max))
            link(eng.tensor_scalar(p.bitcast(I32), m.bitcast(I32), EXPONENT, None, ALU.bitwise_and))
            link(eng.reciprocal(inv, p))
            link(eng.tensor_scalar(inv, inv, scale, None, ALU.mult))

        w_raw = qu[:, :, 0:DIM]
        w_g = qu[:, :, 2 * DIM:3 * DIM]
        g_bc, b_bc, junk = (qu[:, n, DIM:2 * DIM] for n in range(3))
        last_col, bias_col = qu[:, 3, DIM:DIM + H], qu[:, 3, DIM + H:DIM + 2 * H]
        w_top = qu[:, 3, DIM + 2 * H:DIM + 3 * H]
        w1_raw, w2_raw = qu[:, 4, DIM:DIM + 2 * P], qu[:, 4, DIM + 2 * P:DIM + 3 * P]
        route = qu[:, 5, DIM:DIM + 64]
        wo_raw = qu[:, HH:H, NR - HD:NR]
        f_raw = qu[:, 0:CH, NR - DIM:NR]
        f_last, f_last3 = qu[:, 0, NR - 2 * DIM:NR - DIM], qu[:, 1, NR - 2 * DIM:NR - DIM]
        f_top = qu[:, 2, NR - 2 * DIM:NR - 2 * DIM + CH]
        assert CH == HH and HD == 2 * DIM and NR - HD >= 3 * DIM

        ld_route, ld_wo, ld_f, ld_g, ld_b, ld_small, ld_zero = (sem(f"ld_{n}") for n in ("route", "wo", "f", "g", "b", "small", "zero"))
        WP2 = H // 2
        ld_w = [sem(f"ld_w{n}") for n in range(WP2)]
        ident_ready, const_ready = sem("ident_ready"), sem("const_ready")
        route_act, route_dve, route_idx = sem("route_act"), sem("route_dve"), sem("route_idx")
        (dve_step, w_bias, w_gain, w_neg, w_sub, w_max, w_all, w_power, w_alpha, wt_pe, wt_hi, wt_lo, ot_pe, ot_act, small_pe, small_act,
         f_sub, f_max, f_all, f_power, f_scaled, f_sc, f_hi, f_lo, o_max, o_top, o_all) = (sem(n) for n in (
             "dve_step w_bias w_gain w_neg w_sub w_max w_all w_power w_alpha wt_pe wt_hi wt_lo ot_pe ot_act small_pe small_act "
             "f_sub f_max f_all f_power f_scaled f_sc f_hi f_lo o_max o_top o_all").split())

        W_BANKS = (*banks[1:8], banks[4])

        logits_t, u_t = route[0:1, 0:8], route[0:1, 8:16]
        r_m, r_e, r_s, r_ls = route[0:1, 16:17], route[0:1, 17:25], route[0:1, 25:26], route[0:1, 26:27]
        r_g, r_sc = route[0:1, 27:35], route[0:1, 35:43]
        r_top, r_idx = route[0:1, 43:51], route[0:1, 51:59].bitcast(U32)
        n_ops = ffn_W.shape[0]


        def head_view(par, n, k):
            return hb[0:n, par, :, :].rearrange("p h (e k) -> p h e k", e=2)[:, :, :, k]

        def transpose_rows(bank, src, n):
            for c in range(CH):
                last = nc.tensor.transpose(bank[:, c * P:c * P + n], src[0:n, c * P:c * P + P], ident[0:n, 0:n])
            return last

        def chunks(bank, n):
            return bank[:, :].rearrange("p (c n) -> p c n", n=P)[:, :, 0:n]

        def split_product(bank, n, hi, lo, w_hi, w_lo, start, stop):
            nc.tensor.matmul(bank[0:n, :], hi, w_hi, start=start, stop=False, skip_group_check=True)
            nc.tensor.matmul(bank[0:n, :], hi, w_lo, start=False, stop=False, skip_group_check=True)
            return nc.tensor.matmul(bank[0:n, :], lo, w_hi, start=False, stop=stop, skip_group_check=True)

        def project(bank, hi, lo, n, half):
            at = slice(half * HW, half * HW + HW)
            for c in range(CH):
                last = split_product(bank, n, hi[:, c, 0:n], lo[:, c, 0:n], wh[:, c, at], wl[:, c, at], c == 0, c == CH - 1)
            return last

        def head_stats(bank, par, n, half):
            for k in range(HH):
                last = nc.vector.bn_stats(hb[0:n, par, half * HH + k, :], bank[0:n, k * D:k * D + D])
            return last

        def head_squares(link, par, n):
            m, v, t = head_view(par, n, 1), head_view(par, n, 2), sq[0:n, :, :]
            link(nc.vector.tensor_tensor(t, m, m, ALU.mult))
            link(nc.vector.scalar_tensor_tensor(out=t, in0=t, scalar=float(D // 2), in1=v, op0=ALU.mult, op1=ALU.add))
            return nc.vector.tensor_tensor(ss[0:n, par, :], t[:, :, 0], t[:, :, 1], ALU.add)

        def ratio_parts(link, par, n):
            def part(k, e):
                return hb[0:n, par, :, 3 * e + k]
            dm, m2 = rsm[0:n, par, :], rsm[0:n, 2 + par, :]
            link(nc.gpsimd.tensor_tensor(dm, part(1, 0), part(1, 1), ALU.subtract))
            link(nc.gpsimd.tensor_tensor(dm, dm, dm, ALU.mult))
            return nc.gpsimd.tensor_tensor(m2, part(2, 0), part(2, 1), ALU.add)

        def ratio_terms(link, par, n, c_den, half_unit):
            dm, m2, num, den = rsm[0:n, par, :], rsm[0:n, 2 + par, :], rsm[0:n, 4 + par, :], rsm[0:n, 6 + par, :]
            link(nc.vector.scalar_tensor_tensor(out=m2, in0=dm, scalar=float(D // 4), in1=m2, op0=ALU.mult, op1=ALU.add))
            nc.vector.tensor_scalar(num, m2, col(C_NUM, n), 1.0, ALU.mult, ALU.min)
            link(nc.vector.tensor_scalar(den, m2, col(c_den, n), half_unit, ALU.mult, ALU.add))
            return nc.vector.reciprocal(den, den)

        def spread(v, n, heads):
            return v.unsqueeze(2).to_broadcast([n, heads, D])

        def by_head(v):
            return v.rearrange("p (h d) -> p h d", d=D)

        def rows(i):
            return slice(i * P, i * P + P) if isinstance(i, int) else bass.ds(i * P, P)

        def over_tiles(eng, first, last, head, tail, step):
            for i in range(first, first + head):
                step(i, i % 2)
            start, pairs = first + head, (last + 1 - first - head - tail) // 2
            with eng.Fori(0, pairs) as j:
                step(j * 2 + start, start % 2)
                step(j * 2 + (start + 1), (start + 1) % 2)
            for i in range(start + 2 * pairs, last + 1):
                step(i, i % 2)

        def has(i):
            return not isinstance(i, int) or 0 <= i < QT

        def either(query, key, i, k):
            if has(i):
                query(i, k)
            else:
                key(0, i - QT)

        cv = Carve(scratch[:, :], SCRATCH)
        xTh = cv.f16(2 * DIM).rearrange("p (b c n) -> p b c n", b=2, c=CH)
        xTl = cv.f16(2 * DIM).rearrange("p (b c n) -> p b c n", b=2, c=CH)
        at_qs = cv.at
        qs = cv.f32(2 * HD).rearrange("p (b n) -> p b n", b=2)
        at_qc = cv.at
        qc = cv.f32(2 * HD).rearrange("p (b n) -> p b n", b=2)
        cv.at += 32
        at_qch = cv.at
        qch = cv.f16(2 * HD).rearrange("p (b n) -> p b n", b=2)
        at_qcl = cv.at
        qcl = cv.f16(2 * HD).rearrange("p (b n) -> p b n", b=2)
        at_fsb = cv.at
        fsb = cv.f32(HD).rearrange("p (h d) -> p h d", h=H)
        at_xin = cv.at
        xin = cv.f32(2 * DIM).rearrange("p (r d) -> p r d", r=2)
        at_cin = cv.at
        cin = cv.f32(KT * DIM).rearrange("p (t d) -> p t d", t=KT)
        at_free = cv.at

        cv.at = at_cin + (KT - 2) * DIM
        qcq = cv.f16(2 * HD).rearrange("p (b n) -> p b n", b=2)
        assert cv.at == at_free
        q_qcq, q_turned = sem("q_qcq"), sem("q_turned")
        q_cent1 = sem("q_cent1")
        q_ld = [sem("q_ld0"), sem("q_ld1")]
        (q_bn, q_mv, q_std, q_rinv, q_aff, q_xhat, q_acc, q_xT, q_hi, q_lo, q_proj, q_sums, q_ss, q_nrm, q_rc, q_hat,
         q_mean, q_cent, q_qch, q_qcl, q_tr, q_trc, q_fc, q_part, q_parts, q_term, q_rden, q_r, q_fev) = (sem("q_" + n) for n in (
             "bn mv std rinv aff xhat acc xT hi lo proj sums ss nrm rc hat "
             "mean cent qch qcl tr trc fc part parts term rden r fev").split())
        XT, Q_PR, TR, FC = banks[0], banks[1:5], banks[5], banks[6:8]

        cv.at = at_qs
        ks = cv.f32(2 * HD).rearrange("p (b n) -> p b n", b=2)
        assert cv.at == at_qc
        kh = cv.f16(2 * H * MC).rearrange("p (b h m) -> p b h m", b=2, h=H)
        kl = cv.f16(2 * HD).rearrange("p (b h d) -> p b h d", b=2, h=H)
        assert cv.at <= at_qch
        cv.at = at_qch
        msb = cv.f32(H * MC).rearrange("p (h m) -> p h m", h=H)
        after_msb = cv.at
        cv.at = at_xin
        kq = cv.f16(2 * HD).rearrange("p (b h d) -> p b h d", b=2, h=H)
        assert cv.at == at_cin

        k_kq, k_turned, k_sym = sem("k_kq"), sem("k_turned"), sem("k_sym")
        k_ld = [sem(f"k_ld{t}") for t in range(KT)]
        (k_bn, k_mv, k_std, k_rinv, k_aff, k_xhat, k_acc, k_xT, k_hi, k_lo, k_proj, k_sums, k_ss, k_nrm, k_rt, k_rc, k_kt,
         k_khi, k_klo, k_part, k_parts, k_term, k_rden, k_rstep, k_r, k_m, k_mev, k_sum, k_u, k_uev) = (sem("k_" + n) for n in (
             "bn mv std rinv aff xhat acc xT hi lo proj sums ss nrm rt rc kt "
             "khi klo part parts term rden rstep r m mev sum u uev").split())
        K_PR, MM, UU = (banks[3], banks[4], banks[1]), (banks[2], banks[5], banks[6]), banks[7]
        FULL = (KT - 1) * P

        def size(t):
            return P if t % KT < KT - 1 else KLAST

        def slot(t):
            return (QT + t) % 2

        def at_seam(T):
            return isinstance(T, int) and T < 2

        LASTQ = (QT - 1) % 2

        def over_batches(eng, batch):
            batch(0)
            with eng.Fori(1, NB - 1) as b:
                batch(b)
            batch(NB - 1)

        def there(b, t):
            return not isinstance(b, int) or 0 <= b * KT + t < NKT

        def one(b):
            return slice(b, b + 1) if isinstance(b, int) else bass.ds(b, 1)

        cv.at = after_msb
        fs = cv.f32(H)
        xm = cv.f32(2 * CH).rearrange("p (k c) -> p k c", k=2)
        xmh = cv.f16(2 * CH).rearrange("p (k c) -> p k c", k=2)
        xml = cv.f16(2 * CH).rearrange("p (k c) -> p k c", k=2)
        feat = cv.f32(2 * H).rearrange("p (k h) -> p k h", k=2)
        h1 = cv.f32(P)
        h1T = cv.f32(H)
        sm = cv.f32(32)
        diag = cv.f32(2 * H).rearrange("p (k h) -> p k h", k=2)
        aw = cv.f32(2 * H).rearrange("p (k h) -> p k h", k=2)
        wrow = cv.f32(1)
        tiled = cv.f32(P)
        batch_of = cv.f32((QT + 1) * BH).rearrange("p (i b) -> p i b", b=BH)
        assert cv.at <= at_fsb
        cv.at = at_cin
        rh = cv.f16(NG * DIM).rearrange("p (g n) -> p g n", g=NG)
        rl = cv.f16(NG * DIM).rearrange("p (g n) -> p g n", g=NG)
        smask = cv.f32(H * NG * P).rearrange("p (h g b k) -> p h g b k", h=H, g=NG, k=H)
        assert cv.at <= at_free
        wcol = cf[:, WCOL:WCOL + 1]
        x_zero, x_means, x_smask, x_rb, x_rh, x_rl, x_woh, x_wol, x_nmax, x_umax = (
            sem("x_" + n) for n in "zero means smask rb rh rl woh wol nmax umax".split())
        net_dve, net_pe, net_act, net_to_act = sem("net_dve"), sem("net_pe"), sem("net_act"), sem("net_to_act")
        FEAT_READY, H1_READY, H1T_READY, DIAG_READY = range(1, 5)
        SUMS_READY, GLOBAL_READY, HIDDEN_READY, H1_TURNED, OUTPUTS_READY, SPREAD_READY = range(1, 7)
        NORM_READY, STD_READY, EXP_READY = range(1, 4)
        VAR_READY, LESS_MAX_READY, US_READY, AW_READY, WROW_READY = range(1, 6)
        RB = (banks[3], banks[1])
        N_GLOBAL, N_H1T, N_OUT = XT[:, 16:16 + 2 * H], XT[:, 48:48 + H], XT[0:H, 64:67]
        N_SPREAD, N_WROW, N_HIDDEN = XT[:, 80:80 + 2 * H], XT[:, 112:113], XT[0:H, P:2 * P]

        cv.at = at_qs
        uh = cv.f16(2 * HD).rearrange("p (b h n) -> p b h n", b=2, h=H)
        ul = cv.f16(2 * HD).rearrange("p (b h n) -> p b h n", b=2, h=H)
        assert cv.at == at_qc
        x1 = cv.f32(2 * DIM).rearrange("p (b d) -> p b d", b=2)
        x2 = cv.f32(2 * DIM).rearrange("p (b d) -> p b d", b=2)
        cv.at = at_fsb
        res = cv.f32(2 * DIM).rearrange("p (b d) -> p b d", b=2)
        resb = cv.f32(2 * DIM).rearrange("p (b d) -> p b d", b=2)
        assert cv.at == at_cin
        cv.at = 0
        yTh = cv.f16(DIM).rearrange("p (c n) -> p c n", c=CH)
        yTl = cv.f16(DIM).rearrange("p (c n) -> p c n", c=CH)
        cv.at = at_free
        bo = cv.f32(DIM)
        zf = cv.f32(NG * P).rearrange("p (g b k) -> p g b k", g=NG, k=H)
        zh = cv.f16(2 * NG * P).rearrange("p (s g n) -> p s g n", s=2, g=NG)
        zl = cv.f16(2 * NG * P).rearrange("p (s g n) -> p s g n", s=2, g=NG)
        ld_bo = sem("ld_bo")
        b_ld, b_st = [sem("b_ld0"), sem("b_ld1")], [sem("b_st0"), sem("b_st1")]
        (b_uh, b_ul, b_o, b_resb, b_x1, b_bn, b_mv, b_std, b_rinv, b_aff, b_xhat, b_xT, b_hi, b_lo, b_f, b_x2) = (
            sem("b_" + n) for n in "uh ul o resb x1 bn mv std rinv aff xhat xT hi lo f x2".split())
        OO, B_XT, FF, ZT = banks[4:6], banks[6], (banks[3], banks[7]), banks[2]
        z_f, z_t, z_h, z_l = (sem("z_" + n) for n in "f t h l".split())

        def groups_of(i, groups):
            if not isinstance(i, int):
                return groups
            return (0,) * (i <= MID) + (1,) * (i >= MID)

        def wo(w, h):
            return w[:, h // 2, h % 2 * DIM:h % 2 * DIM + DIM]

        def over_out_tiles(eng, step):
            def of(groups):
                return lambda i, k: step(i, k, groups)
            over_tiles(eng, 0, MID - 1, 4, 2, of((0,)))
            step(MID, MID % 2, (0, 1))
            over_tiles(eng, MID + 1, QT - 1, 0, 2, of((1,)))

        with nc.Block() as block:
            @block.sync
            def _(sp):
                w_heads = w_in.rearrange("(h d) i -> d h i", d=D)
                sp.dma_start(g_bc, ln_g.partition_broadcast(P)).then_inc(ld_g, 16)
                for n in range(WP2):
                    sp.dma_start(w_raw[:, 2 * n:2 * n + 2, :], w_heads[:, 2 * n:2 * n + 2, :]).then_inc(ld_w[n], 16)
                    if n in (1, 2):
                        sp.dma_start(xin[:, n - 1, :], xf[rows(n - 1), :]).then_inc(q_ld[n - 1], 16)
                sp.dma_start(w1_raw, wp_w1).then_inc(ld_small, 16)
                sp.dma_start(w2_raw[0:3, :], wp_w2).then_inc(ld_small, 16)
                sp.dma_start(b1s[:, :], wp_b1.partition_broadcast(H)).then_inc(ld_small, 16)
                sp.dma_start(g1s[:, :], wp_ln_g.partition_broadcast(H)).then_inc(ld_small, 16)
                sp.dma_start(be1s[:, :], wp_ln_b.partition_broadcast(H)).then_inc(ld_small, 16)
                sp.dma_start(b2s[:, :], wp_b2.partition_broadcast(H)).then_inc(ld_small, 16)
                sp.dma_start(wo_raw, w_out.rearrange("(c p) n -> p c n", p=P)).then_inc(ld_wo, 16)
                sp.wait_ge(route_idx, 1)
                idx = sp.value_load(r_idx[0:1, 0:1], min_val=0, max_val=n_ops - 1)
                f_rows = ffn_W[bass.ds(idx, 1), :, :].rearrange("a (c p) n -> p (a c) n", p=P)
                f_last_row = ffn_W[bass.ds(idx, 1), DIM - 1, :].rearrange("a n -> (a n)")
                sp.dma_start(f_raw[:, 0:CH - 1, :], f_rows[:, 0:CH - 1, :]).then_inc(ld_f, 16)
                sp.dma_start(f_raw[0:P - 1, CH - 1, :], f_rows[0:P - 1, CH - 1, :]).then_inc(ld_f, 16)
                sp.dma_start(f_raw[P - 1:P, CH - 1, :], ffn_b[bass.ds(idx, 1), :]).then_inc(ld_f, 16)
                sp.dma_start(f_last, f_last_row.partition_broadcast(P)).then_inc(ld_f, 16)
                sp.wait_ge(ld_zero, 1)
                sp.dma_start(f_last3[0:P - 1, :], f_last_row.partition_broadcast(P - 1)).then_inc(ld_f, 16)

                def query_step(i, k):
                    if isinstance(i, int) and i < 2:
                        return
                    sp.wait_ge(q_xhat, i - 1)
                    sp.dma_start(xin[:, k, :], xf[rows(i), :]).then_inc(q_ld[k], 16)
                over_tiles(sp, 0, QT - 1, 6, 3, query_step)
                def key_batch(b):
                    for t in range(KT):
                        wait(sp, k_xhat, b * KT + (t - KT + 1))
                        if isinstance(b, int) and b == 0 and t == KT - 2:
                            sp.wait_ge(q_fc, QT)
                        if t < KT - 1:
                            src = ctx_1024[one(b), 0:FULL, :].rearrange("a (p j) d -> p (a j) d", j=KT - 1)[:, t, :]
                        else:
                            src = ctx_1024[one(b), FULL:NK, :].rearrange("a p d -> (a p) d")
                        sp.dma_start(cin[0:size(t), t, :], src).then_inc(k_ld[t], 16)
                over_batches(sp, key_batch)
                sp.wait_ge(q_fev, 6)
                sp.wait_ge(q_xhat, QT)
                sp.dma_start(bo, b_out.partition_broadcast(P)).then_inc(ld_bo, 16)

                def out_step(i, k, groups):
                    wait(sp, b_resb, i - 1)
                    sp.dma_start(res[:, k, :], xf[rows(i), :]).then_inc(b_ld[k], 16)
                over_out_tiles(sp, out_step)

            @block.gpsimd
            def _(pool):
                def query_sum_rows(i, k):
                    pool.wait_ge(q_xhat, i + 1)
                    wait(pool, q_acc, i)
                    nc.gpsimd.tensor_tensor(acc_q[:, :], acc_q[:, :], xh[:, k, :], ALU.add).then_inc(q_acc, 1)

                def query_parts(i, k):
                    pool.wait_ge(q_ss, i + 1)
                    wait(pool, q_r, i - 1)
                    ratio_parts(chain(pool, q_part, i * 2), k, P).then_inc(q_parts, 1)

                def query_ratio(i, k):
                    pool.wait_ge(q_rden, i + 1)
                    dst = qr[:, i, :] if isinstance(i, int) else qr[:, bass.ds(i, 1), :].rearrange("p a h -> p (a h)")
                    nc.gpsimd.tensor_tensor(dst, rsm[:, 4 + k, :], rsm[:, 6 + k, :], ALU.mult).then_inc(q_r, 1)

                def query_centred_low(i, k, half):
                    pool.wait_ge(q_qch, 2 * i + half + 1)
                    at = slice(half * HW, half * HW + HW)
                    nc.gpsimd.tensor_tensor(qcl[:, k, at], qc[:, k, at], qch[:, k, at], ALU.subtract).then_inc(q_qcl, 1)

                def key_sum_rows(b, t):
                    T, n, k = b * KT + t, size(t), slot(t)
                    pool.wait_ge(k_xhat, T + 1)
                    wait(pool, k_acc, T)
                    nc.gpsimd.tensor_tensor(acc_k[0:n, :], acc_k[0:n, :], xh[0:n, k, :], ALU.add).then_inc(k_acc, 1)

                def key_parts(b, t):
                    T, n, k = b * KT + t, size(t), slot(t)
                    pool.wait_ge(k_ss, T + 1)
                    ratio_parts(chain(pool, k_part, T * 2), k, n).then_inc(k_parts, 1)

                def key_ratio(b, t):
                    T, n, k = b * KT + t, size(t), slot(t)
                    link = chain(pool, k_rstep, T * 3)
                    r = rsm[0:n, 8, :]
                    pool.wait_ge(k_rden, T + 1)
                    wait(pool, k_m, T - 1)
                    link(nc.gpsimd.tensor_tensor(r, rsm[0:n, 4 + k, :], rsm[0:n, 6 + k, :], ALU.mult))
                    link(nc.gpsimd.tensor_tensor(r, r, rt[0:n, k, :], ALU.mult))
                    link(nc.gpsimd.tensor_tensor(kh[0:n, k, :, RC], r, ones[0:n, 0:H], ALU.mult))
                    nc.gpsimd.tensor_tensor(kh[0:n, k, :, 0:2], kh[0:n, k, :, RC].unsqueeze(2).to_broadcast([n, H, 2]),
                                            col(HALF, n).unsqueeze(2).to_broadcast([n, H, 2]), ALU.mult)
                    nc.gpsimd.tensor_tensor(kh[0:n, k, :, RC + 1], r, kh[0:n, k, :, RC], ALU.subtract).then_inc(k_r, 1)

                def key_k_low(b, t, half):
                    T, n, k = b * KT + t, size(t), slot(t)
                    hs = slice(half * HH, half * HH + HH)
                    pool.wait_ge(k_khi, 2 * T + half + 1)
                    nc.gpsimd.tensor_tensor(kl[0:n, k, hs, :], by_head(ks[0:n, k, half * HW:half * HW + HW]), kh[0:n, k, hs, 2:RC],
                                            ALU.subtract).then_inc(k_klo, 1)

                def out_bias(i, k):
                    pool.wait_ge(b_ld[k], (i - k) * 8 + 16)
                    wait(pool, b_x1, i - 1)
                    nc.gpsimd.tensor_tensor(resb[:, k, :], res[:, k, :], bo, ALU.add).then_inc(b_resb, 1)

                def out_ratios(i, groups):
                    wait(pool, z_t, i)
                    for g in groups:
                        mask = batch_of[:, i + g, :] if isinstance(i, int) else batch_of[:, bass.ds(i + g, 1), :].rearrange("p a b -> p (a b)")
                        ratios = qr[:, i, :] if isinstance(i, int) else qr[:, bass.ds(i, 1), :].rearrange("p a h -> p (a h)")
                        last = nc.gpsimd.tensor_tensor(zf[:, g], mask.unsqueeze(2).to_broadcast([P, BH, H]),
                                                       ratios.unsqueeze(1).to_broadcast([P, BH, H]), ALU.mult)
                    last.then_inc(z_f, 1)

                def routed_minus_last():
                    pool.wait_ge(ld_f, 80)
                    for c in range(CH):
                        nc.gpsimd.tensor_tensor(f_raw[:, c, :], f_raw[:, c, :], f_last if c < CH - 1 else f_last3, ALU.subtract).then_inc(f_sub, 1)

                def routed_low():
                    for c in range(CH):
                        pool.wait_ge(f_hi, c + 1)
                        nc.gpsimd.tensor_tensor(fl[:, c, :], f_raw[:, c, :], fh[:, c, :], ALU.subtract).then_inc(f_lo, 1)

                pool.memset(ident[:, :], 0.0).then_inc(ident_ready, 1)
                pool.wait_ge(ident_ready, 1)
                pool.affine_select(out=ident[:, :], in_=ident[:, :], compare_op=ALU.not_equal, fill=1.0, base=0,
                                   pattern=[[-1, P]], channel_multiplier=1).then_inc(ident_ready, 1)
                pool.memset(f_last3, 0.0).then_inc(ld_zero, 1)
                pool.memset(acc_q[:, :], 0.0)
                pool.memset(acc_k[:, :], 0.0)
                pool.memset(nmax[:, :], 0.0)
                pool.memset(ones[:, :], 1.0)
                pool.memset(col(HALF), 0.5)
                pool.memset(xh[:, :, DIM - 1:DIM], XS).then_inc(const_ready, 1)
                pool.wait_ge(ld_g, 16)
                for h in range(H):
                    pool.wait_ge(ld_w[h // 2], 16)
                    pool.tensor_tensor(w_g[:, h, :], w_raw[:, h, :], g_bc, ALU.mult).then_inc(w_gain, 1)
                pool.wait_ge(w_max, 1)
                pool.partition_all_reduce(col(WMAX), col(WMAXP), P, RMAX).then_inc(w_all, 1)
                query_sum_rows(0, 0)

                def query_step(i, k):
                    if has(i - 1):
                        query_parts(i - 1, 1 - k)
                    either(query_sum_rows, key_sum_rows, i + 1, 1 - k)
                    if has(i - 1):
                        query_centred_low(i - 1, 1 - k, 0)
                        query_centred_low(i - 1, 1 - k, 1)
                        query_ratio(i - 1, 1 - k)
                    if isinstance(i, int) and i == 0:
                        routed_minus_last()
                    if isinstance(i, int) and i == 3:
                        pool.wait_ge(f_max, 1)
                        pool.partition_all_reduce(col(FMAX), col(FMAXP), P, RMAX).then_inc(f_all, 1)
                    if isinstance(i, int) and i == 5:
                        routed_low()
                over_tiles(pool, 0, QT - 1, 6, 3, query_step)

                def batch(b):
                    for t in range(KT):
                        if there(b, t - 1):
                            key_parts(b, t - 1)
                        else:
                            query_parts(QT - 1, LASTQ)
                        if there(b, t + 1):
                            key_sum_rows(b, t + 1)
                        if there(b, t - 1):
                            key_k_low(b, t - 1, 0)
                            key_ratio(b, t - 1)
                            key_k_low(b, t - 1, 1)
                        else:
                            query_centred_low(QT - 1, LASTQ, 0)
                            query_centred_low(QT - 1, LASTQ, 1)
                            query_ratio(QT - 1, LASTQ)
                        if isinstance(b, int) and b == 0 and t == KT - 1:
                            pool.wait_ge(q_fev, 4)
                            nc.gpsimd.tensor_tensor(fsb, fsb, fsb, ALU.mult).then_inc(q_fev, 1)
                over_batches(pool, batch)
                pool.memset(smask, 0.0).then_inc(x_zero, 1)
                key_parts(NB - 1, KT - 1)
                key_k_low(NB - 1, KT - 1, 0)
                key_ratio(NB - 1, KT - 1)
                key_k_low(NB - 1, KT - 1, 1)
                link = chain(pool, ident_ready, 2)
                link(pool.memset(batch_of, 1.0))
                for e0, e1, shift in ((0, MID + 1, 0), (MID + 1, QT + 1, -P - SPLIT)):
                    part = batch_of[:, e0:e1, :]
                    link(pool.affine_select(out=part, in_=part, compare_op=ALU.is_ge, fill=0.0, base=P * e0 + shift,
                                            pattern=[[P, e1 - e0], [-NQ, BH]], channel_multiplier=1))
                    link(pool.affine_select(out=part, in_=part, compare_op=ALU.is_ge, fill=0.0, base=NQ - 1 - P * e0 - shift,
                                            pattern=[[-P, e1 - e0], [NQ, BH]], channel_multiplier=-1))
                out_ratios(0, (0,))
                pool.wait_ge(o_max, 1)
                pool.partition_all_reduce(col(OMAX), col(OMAXP), P, RMAX).then_inc(o_all, 1)
                pool.wait_ge(x_umax, 1)
                pool.partition_all_reduce(col(UMAX), col(TMP), P, RMAX).then_inc(x_umax, 1)
                pool.wait_ge(ld_bo, 16)
                pool.wait_ge(k_m, NKT)

                def out_step(i, k, groups):
                    if has(i + 1):
                        out_ratios(i + 1, groups_of(i + 1, groups))
                    out_bias(i, k)
                over_out_tiles(pool, out_step)

            @block.tensor
            def _(pe):
                def query_turn(i, k):
                    pe.wait_ge(q_xhat, i + 1)
                    wait(pe, q_lo, i)
                    transpose_rows(XT, xh[:, k, :], P).then_inc(q_xT, 1)

                def query_proj(i, k, half):
                    pe.wait_ge(q_lo, i + 1)
                    if half == 0:
                        wait(pe, q_cent, i - 1)
                    else:
                        wait(pe, q_cent1, i - 1)
                    if isinstance(i, int) and i == 0:
                        pe.wait_ge(wt_lo, 4)
                    project(Q_PR[(2 * k + half) % 4], xTh[:, k], xTl[:, k], P, half).then_inc(q_proj, 1)

                def query_turn_hat(i, k, half):
                    pe.wait_ge(q_hat, 2 * i + half + 1)
                    wait(pe, q_trc, 2 * i + half)
                    for n in range(HH):
                        at = half * HW + n * D
                        last = nc.tensor.transpose(TR[:, n * P:n * P + P], qs[:, k, at:at + D], ident[:, :])
                    last.then_inc(q_tr, 1)

                def query_correlate(i, k):
                    pe.wait_ge(q_qcl, 2 * i + 2)
                    pe.wait_ge(q_qcq, 2 * i + 2)
                    for h in range(H):
                        at = slice(h * D, h * D + D)
                        bank = FC[h // HH][:, (h % HH) * D:(h % HH) * D + D]
                        first, end = isinstance(i, int) and i == 0 and h % HH == 0, isinstance(i, int) and i == QT - 1
                        nc.tensor.matmul(bank, qcq[:, k, at], qch[:, k, at], start=first, stop=False, skip_group_check=True)
                        last = nc.tensor.matmul(bank, qcl[:, k, at], qch[:, k, at], start=False, stop=end, skip_group_check=True)
                    last.then_inc(q_fc, 1)

                def query_turn_correlations(g):
                    pe.wait_ge(q_fev, 2 + g)
                    for n in range(HH):
                        last = nc.tensor.transpose(UU[:, n * D:n * D + D], fsb[:, g * HH + n, :], ident[:, :])
                    last.then_inc(q_turned, 1)

                def key_turn(b, t):
                    T, n = b * KT + t, size(t)
                    pe.wait_ge(k_xhat, T + 1)
                    wait(pe, k_lo, T)
                    if at_seam(T):
                        pe.wait_ge(q_lo, QT)
                    transpose_rows(XT, xh[:, slot(t), :], n).then_inc(k_xT, 1)

                def key_proj(b, t, half):
                    T, n = b * KT + t, size(t)
                    pe.wait_ge(k_lo, T + 1)
                    wait(pe, k_kt, 2 * T + half - 2)
                    if at_seam(T) and 2 * T + half < 3:
                        pe.wait_ge(q_cent, QT - 1 + T)
                        pe.wait_ge(q_cent1, QT - 1 + T)
                    project(K_PR[(2 * t + half) % 3], xTh[:, slot(t)], xTl[:, slot(t)], n, half).then_inc(k_proj, 1)

                def key_outer(b, t):
                    T, n, k = b * KT + t, size(t), slot(t)
                    pe.wait_ge(k_klo, 2 * T + 2)
                    pe.wait_ge(k_kq, 2 * T + 2)
                    pe.wait_ge(k_r, T + 1)
                    if t % KT == 0:
                        wait(pe, k_mev, b + t // KT)
                    if at_seam(T) and T == 0:
                        pe.wait_ge(q_cent1, QT)
                        pe.wait_ge(q_trc, 2 * QT)
                        pe.wait_ge(q_fev, 1)
                    for h in range(H):
                        bank, at = MM[h // MB], h % MB * MC
                        end = t % KT == KT - 1
                        nc.tensor.matmul(bank[:, at + 2:at + MC], kq[0:n, k, h, :], kh[0:n, k, h, 2:MC], start=(t % KT == 0 and h % MB == 0),
                                         stop=False, skip_group_check=True)
                        last = nc.tensor.matmul(bank[:, at:at + RC], kl[0:n, k, h, :], kh[0:n, k, h, 0:RC], start=False, stop=end,
                                                skip_group_check=True)
                    last.then_inc(k_m, 1)

                def key_turn_m(b, g):
                    pe.wait_ge(k_mev, b + 1)
                    if g == 0:
                        wait(pe, k_uev, 2 * b)
                        if isinstance(b, int) and b == 0:
                            pe.wait_ge(q_fev, 4)
                    else:
                        pe.wait_ge(k_sym, 2 * b + 1)
                    for n in range(HH):
                        last = nc.tensor.transpose(UU[:, n * D:n * D + D], msb[:, g * HH + n, 2:RC], ident[:, :])
                    last.then_inc(k_turned, 1)

                def key_apply(b, g):
                    pe.wait_ge(k_sym, 2 * b + 2)
                    if g == 1:
                        pe.wait_ge(k_uev, 2 * b + 1)
                    for n in range(HH):
                        h = g * HH + n
                        at = slice(b * NQ, b * NQ + NQ) if isinstance(b, int) else bass.ds(b * NQ, NQ)
                        last = nc.tensor.matmul(UU[:, n * NQ:n * NQ + NQ], msb[:, h, 2:RC], qu[:, h, at], start=True, stop=True,
                                                skip_group_check=True)
                    last.then_inc(k_u, 1)

                def out_turn(i, k):
                    pe.wait_ge(b_xhat, i + 1)
                    wait(pe, b_lo, i)
                    transpose_rows(B_XT, xh[:, k, :], P).then_inc(b_xT, 1)

                def out_routed(i, k):
                    pe.wait_ge(b_lo, i + 1)
                    wait(pe, b_x2, i - 1)
                    for c in range(CH):
                        last = split_product(FF[k], P, yTh[:, c, :], yTl[:, c, :], fh[:, c, :], fl[:, c, :], c == 0, c == CH - 1)
                    last.then_inc(b_f, 1)

                def out_turn_ratios(i, k, groups):
                    pe.wait_ge(z_f, i + 1)
                    wait(pe, z_l, i)
                    for g in groups:
                        last = nc.tensor.transpose(ZT[:, (2 * k + g) * P:(2 * k + g) * P + P], zf[:, g].rearrange("p b k -> p (b k)"), ident[:, :])
                    last.then_inc(z_t, 1)

                def turn_weights(n):
                    half, c = n // CH, n % CH
                    if n == 7:
                        pe.wait_ge(wt_lo, 4)
                    for k in range(HH):
                        if c == 0:
                            pe.wait_ge(w_sub, half * HH + k + 1)
                        last = nc.tensor.transpose(W_BANKS[n][:, k * P:k * P + P], w_g[:, half * HH + k, c * P:c * P + P], ident[:, :])
                    last.then_inc(wt_pe, 1)

                def turn_out_weights(h):
                    if h >= 3:
                        pe.wait_ge(ot_act, h - 2)
                    else:
                        pe.wait_ge(wt_lo, HH + 1 + h)
                    for c in range(CH):
                        last = nc.tensor.transpose(banks[5 + h % 3][:, c * P:c * P + P], wo_raw[:, c, h * D:h * D + D], ident[:, :])
                    last.then_inc(ot_pe, 1)

                pe.wait_ge(ident_ready, 2)
                for n in range(4):
                    turn_weights(n)
                for n in range(4, 7):
                    turn_weights(n)
                pe.wait_ge(const_ready, 1)
                query_turn(0, 0)
                turn_weights(7)
                query_proj(0, 0, 0)
                query_turn(1, 1)
                pe.wait_ge(wt_lo, 7)
                pe.wait_ge(ld_small, 96)
                for c in range(2):
                    nc.tensor.transpose(banks[7][:, c * P:c * P + P], w1_raw[:, c * P:c * P + P], ident[:, :])
                nc.tensor.transpose(banks[7][:, 2 * P:2 * P + 3], w2_raw[0:3, :], ident[0:3, 0:3]).then_inc(small_pe, 1)
                pe.wait_ge(ld_wo, 16)
                for h in range(3):
                    if h == 2:
                        pe.wait_ge(small_act, 1)
                    turn_out_weights(h)
                pe.wait_ge(wt_lo, 2 * CH)
                query_proj(0, 0, 1)
                for h in range(3, H):
                    turn_out_weights(h)

                def query_step(i, k):
                    if isinstance(i, int) and i == 0:
                        return
                    either(query_turn, key_turn, i + 1, 1 - k)
                    query_proj(i, k, 0)
                    if isinstance(i, int) and i == 1:
                        pe.wait_ge(ot_act, H)
                    if has(i - 2):
                        query_correlate(i - 2, k)
                    if has(i - 1):
                        query_turn_hat(i - 1, 1 - k, 0)
                    query_proj(i, k, 1)
                    if has(i - 1):
                        query_turn_hat(i - 1, 1 - k, 1)
                over_tiles(pe, 0, QT - 1, 6, 3, query_step)

                def batch(b):
                    for t in range(KT):
                        if there(b, t + 1):
                            key_turn(b, t + 1)
                        key_proj(b, t, 0)
                        if there(b, t - 2):
                            key_outer(b, t - 2)
                        else:
                            query_correlate(QT - 2 + t, (QT + t) % 2)
                        if not there(b, t - 1):
                            query_turn_hat(QT - 1, LASTQ, 0)
                        key_proj(b, t, 1)
                        if not there(b, t - 1):
                            query_turn_hat(QT - 1, LASTQ, 1)
                        if isinstance(b, int) and b == 0 and t in (3, 4):
                            query_turn_correlations(t - 3)
                        if t in (2, 3) and there(b, t - KT):
                            key_turn_m(b - 1, t - 2)
                        if t in (4, 5) and there(b, t - KT):
                            key_apply(b - 1, t - 4)
                over_batches(pe, batch)
                pe.wait_ge(k_acc, NKT)
                pe.wait_ge(k_lo, NKT)
                for c in range(CH):
                    for k, acc in enumerate((acc_q, acc_k)):
                        nc.tensor.matmul(XT[:, k * CH + c:k * CH + c + 1], acc[:, c * P:c * P + P], ones[:, 0:1],
                                         start=True, stop=True, skip_group_check=True)
                pe.wait_ge(q_fev, 6)
                nc.tensor.matmul(XT[0:H, 2 * CH:2 * CH + 1], fs[:, :], ones[:, 0:1], start=True, stop=True, skip_group_check=True).then_inc(net_pe, 1)
                key_outer(NB - 1, KT - 2)
                def rank_product(g, heads):
                    for h in heads:
                        last = nc.tensor.matmul(RB[g][:, :], smask[:, h, g].rearrange("p b k -> p (b k)"), woT[:, h, :],
                                                start=(h == 0), stop=(h == H - 1))
                    return last
                pe.wait_ge(x_smask, 1)
                pe.wait_ge(k_kt, 2 * NKT - 2)
                rank_product(0, range(2))
                pe.wait_ge(x_means, 3)
                for h in range(H):
                    for c in range(CH):
                        at, dst = slice(h * D, h * D + D), N_GLOBAL[:, 2 * h:2 * h + 2]
                        nc.tensor.matmul(dst, wh[:, c, at], xmh[:, :, c], start=(c == 0 and h == 0), stop=False, skip_group_check=True)
                        nc.tensor.matmul(dst, wh[:, c, at], xml[:, :, c], start=False, stop=False, skip_group_check=True)
                        last = nc.tensor.matmul(dst, wl[:, c, at], xmh[:, :, c], start=False, stop=(c == CH - 1), skip_group_check=True)
                last.then_inc(net_pe, 1)

                rank_product(0, range(2, HH))
                pe.wait_ge(net_dve, FEAT_READY)
                for k in range(2):
                    last = nc.tensor.matmul(N_HIDDEN, feat[:, k, :], w1T[:, k, :], start=(k == 0), stop=(k == 1), skip_group_check=True)
                last.then_inc(net_pe, 1)
                key_outer(NB - 1, KT - 1)
                rank_product(0, range(HH, H - 2))
                pe.wait_ge(net_dve, H1_READY)
                nc.tensor.transpose(N_H1T, h1[0:H, :], ident[0:H, 0:H]).then_inc(net_pe, 1)
                rank_product(0, range(H - 2, H - 1))
                key_turn_m(NB - 1, 0)
                pe.wait_ge(net_dve, H1T_READY)
                nc.tensor.matmul(N_OUT, h1T, w2T[:, :], start=True, stop=True, skip_group_check=True).then_inc(net_pe, 1)
                rank_product(0, range(H - 1, H)).then_inc(x_rb, 1)
                key_turn_m(NB - 1, 1)
                key_apply(NB - 1, 0)
                pe.wait_ge(x_smask, 2)
                pe.wait_ge(k_kt, 2 * NKT)
                rank_product(1, range(2))
                key_apply(NB - 1, 1)
                out_turn_ratios(0, 0, (0,))
                pe.wait_ge(net_dve, DIAG_READY)
                nc.tensor.matmul(N_SPREAD, ones[0:H, :], diag[0:H].rearrange("p k h -> p (k h)"), start=True, stop=True, skip_group_check=True)
                nc.tensor.matmul(N_WROW, tiled[0:H, :], wcol[0:H, :], start=True, stop=True, skip_group_check=True).then_inc(net_pe, 1)
                rank_product(1, range(2, H)).then_inc(x_rb, 1)
                pe.wait_ge(k_uev, 2 * NB)

                def out_step(i, k, groups):
                    pe.wait_ge(b_ul, i + 1)
                    wait(pe, b_x1, i - 1)
                    for h in range(H):
                        if isinstance(i, int) and i == 0:
                            pe.wait_ge(x_wol, h + 1)
                        split_product(OO[k], P, uh[:, k, h, :], ul[:, k, h, :], wo(wh, h), wo(wl, h), h == 0, False)
                        if h == 1 and has(i + 1):
                            out_turn_ratios(i + 1, 1 - k, groups_of(i + 1, groups))
                        if h == HH and has(i - 1):
                            out_turn(i - 1, 1 - k)
                    pe.wait_ge(z_l, i + 1)
                    if isinstance(i, int) and i == 0:
                        pe.wait_ge(x_rl, 2)
                    for g in groups:
                        last = split_product(OO[k], P, zh[:, k, g, :], zl[:, k, g, :], rh[:, g, :], rl[:, g, :], False, g == groups[-1])
                    last.then_inc(b_o, 1)
                    if has(i - 1):
                        out_routed(i - 1, 1 - k)
                over_out_tiles(pe, out_step)
                out_turn(QT - 1, (QT - 1) % 2)
                out_routed(QT - 1, (QT - 1) % 2)

            @block.scalar
            def _(act):
                def query_deviation(i, k):
                    act.wait_ge(q_mv, i + 1)
                    nc.scalar.activation(std[:, k:k + 1], mv[:, k, 1:2], ACT.Sqrt, bias=col(EPS_Q),
                                         scale=(1.0 + EPS) / XS ** 2).then_inc(q_std, 1)

                def query_normalise(i, k):
                    act.wait_ge(q_aff, i + 1)
                    wait(act, q_xT, i - 1)
                    wait(act, q_acc, i - 1)
                    nc.scalar.activation(xh[:, k, 0:DIM - 1], xin[:, k, 0:DIM - 1], ACT.Identity, bias=aff[:, k, 1:2],
                                         scale=aff[:, k, 0:1]).then_inc(q_xhat, 1)

                def query_high(i, k):
                    act.wait_ge(q_xT, i + 1)
                    wait(act, q_proj, 2 * i - 2)
                    nc.scalar.activation(xTh[:, k], chunks(XT, P), ACT.Copy).then_inc(q_hi, 1)

                def query_norm(i, k):
                    act.wait_ge(q_ss, i + 1)
                    nc.scalar.activation(nrm[:, k, :], ss[:, k, :], ACT.Sqrt).then_inc(q_nrm, 1)

                def query_hat_out(i, k, half):
                    act.wait_ge(q_tr, 2 * i + half + 1)
                    nc.scalar.activation(qu[:, half * HH:half * HH + HH, rows(i)], by_head(TR[:, :]), ACT.Copy).then_inc(q_trc, 1)

                def query_half_high(i, k):
                    for half in range(2):
                        at = slice(half * HW, half * HW + HW)
                        nc.scalar.activation(qcq[:, k, at], qc[:, k, at], ACT.Copy, scale=0.5).then_inc(q_qcq, 1)

                def query_centre_second(i, k):
                    act.wait_ge(q_mean, i + 1)
                    act.wait_ge(q_hat, 2 * i + 2)
                    wait(act, q_qcl, 2 * i - 2)
                    for n in range(HH):
                        last = nc.scalar.activation(qc[:, k, HW + n * D:HW + n * D + D], Q_PR[2 * k + 1][:, n * D:n * D + D], ACT.Identity,
                                                    bias=mean2[:, HH + n:HH + n + 1], scale=2.0)
                    last.then_inc(q_cent1, 1)

                def query_centred_high(i, k, half):
                    act.wait_ge((q_cent, q_cent1)[half], i + 1)
                    wait(act, q_fc, i - 1)
                    at = slice(half * HW, half * HW + HW)
                    nc.scalar.activation(qch[:, k, at], qc[:, k, at], ACT.Copy).then_inc(q_qch, 1)

                def key_deviation(b, t):
                    T, n, k = b * KT + t, size(t), slot(t)
                    act.wait_ge(k_mv, T + 1)
                    nc.scalar.activation(std[0:n, k:k + 1], mv[0:n, k, 1:2], ACT.Sqrt, bias=col(EPS_K, n),
                                         scale=1.0 / XS ** 2).then_inc(k_std, 1)

                def key_normalise(b, t):
                    T, n, k = b * KT + t, size(t), slot(t)
                    act.wait_ge(k_aff, T + 1)
                    wait(act, k_xT, T - 1)
                    wait(act, k_acc, T - 1)
                    if at_seam(T):
                        act.wait_ge(q_xT, QT + T - 1)
                        act.wait_ge(q_acc, QT + T - 1)
                    nc.scalar.activation(xh[0:n, k, 0:DIM - 1], cin[0:n, t % KT, 0:DIM - 1], ACT.Identity, bias=aff[0:n, k, 1:2],
                                         scale=aff[0:n, k, 0:1]).then_inc(k_xhat, 1)

                def key_high(b, t):
                    T, n, k = b * KT + t, size(t), slot(t)
                    act.wait_ge(k_xT, T + 1)
                    wait(act, k_proj, 2 * T - 2)
                    if at_seam(T):
                        act.wait_ge(q_proj, 2 * (QT + T) - 2)
                    nc.scalar.activation(xTh[:, k, :, 0:n], chunks(XT, n), ACT.Copy).then_inc(k_hi, 1)

                def key_roots(b, t):
                    T, n, k = b * KT + t, size(t), slot(t)
                    act.wait_ge(k_ss, T + 1)
                    nc.scalar.activation(nrm[0:n, k, :], ss[0:n, k, :], ACT.Sqrt).then_inc(k_nrm, 1)
                    act.wait_ge(k_nrm, T + 1)
                    wait(act, k_r, T - 1)
                    nc.scalar.activation(rt[0:n, k, :], nrm[0:n, k, :], ACT.Sqrt).then_inc(k_rt, 1)

                def key_k_high(b, t, half):
                    T, n, k = b * KT + t, size(t), slot(t)
                    act.wait_ge(k_kt, 2 * T + half + 1)
                    wait(act, k_m, T - 1)
                    if at_seam(T):
                        act.wait_ge(q_qcl, 2 * QT)
                    hs = slice(half * HH, half * HH + HH)
                    nc.scalar.activation(kh[0:n, k, hs, 2:RC], by_head(ks[0:n, k, half * HW:half * HW + HW]), ACT.Copy).then_inc(k_khi, 1)

                def key_half_high(b, t, half):
                    T, n, k = b * KT + t, size(t), slot(t)
                    hs = slice(half * HH, half * HH + HH)
                    nc.scalar.activation(kq[0:n, k, hs, :], by_head(ks[0:n, k, half * HW:half * HW + HW]), ACT.Copy, scale=0.5).then_inc(k_kq, 1)

                def key_m_out(b):
                    act.wait_ge(k_m, (b + 1) * KT)
                    wait(act, k_u, 2 * b)
                    wait(act, k_sum, 2 * b)
                    for g, bank in enumerate(MM):
                        hs = slice(g * MB, min(g * MB + MB, H))
                        w = (hs.stop - hs.start) * MC
                        last = nc.scalar.activation(msb[:, hs, :], bank[:, 0:w].rearrange("p (h m) -> p h m", m=MC), ACT.Copy)
                    last.then_inc(k_mev, 1)

                def key_u_out(b, g):
                    act.wait_ge(k_u, 2 * b + g + 1)
                    at = slice(b * NQ, b * NQ + NQ) if isinstance(b, int) else bass.ds(b * NQ, NQ)
                    nc.scalar.activation(qu[:, g * HH:g * HH + HH, at], UU[:, 0:HH * NQ].rearrange("p (h n) -> p h n", h=HH),
                                         ACT.Copy).then_inc(k_uev, 1)

                def out_u_high(i, k):
                    wait(act, b_o, i - 1)
                    nc.scalar.activation(uh[:, k], qu[:, :, rows(i)], ACT.Copy, scale=col(US)).then_inc(b_uh, 1)

                def out_deviation(i, k):
                    act.wait_ge(b_mv, i + 1)
                    nc.scalar.activation(std[:, k:k + 1], mv[:, k, 1:2], ACT.Sqrt, bias=col(EPS_K), scale=1.0 / XS ** 2).then_inc(b_std, 1)

                def out_normalise(i, k):
                    act.wait_ge(b_aff, i + 1)
                    wait(act, b_xT, i - 1)
                    nc.scalar.activation(xh[:, k, 0:DIM - 1], x1[:, k, 0:DIM - 1], ACT.Identity, bias=aff[:, k, 1:2],
                                         scale=aff[:, k, 0:1]).then_inc(b_xhat, 1)

                def out_high(i, k):
                    act.wait_ge(b_xT, i + 1)
                    wait(act, b_f, i)
                    nc.scalar.activation(yTh, chunks(B_XT, P), ACT.Copy).then_inc(b_hi, 1)

                def out_store(i, k):
                    act.wait_ge(b_x2, i + 1)
                    act.dma_start(outf[rows(i), :], x2[:, k, :]).then_inc(b_st[k], 16)

                def out_ratios_high(i, k, groups):
                    act.wait_ge(z_t, i + 1)
                    wait(act, b_o, i - 1)
                    g, n = groups[0], len(groups)
                    nc.scalar.activation(zh[:, k, g:g + n, :], ZT[:, (2 * k + g) * P:(2 * k + g + n) * P].rearrange("p (g n) -> p g n", g=n),
                                         ACT.Copy).then_inc(z_h, 1)

                def weights_high(n):
                    act.wait_ge(wt_pe, n + 1)
                    nc.scalar.activation(wh[:, n % CH, n // CH * HW:n // CH * HW + HW], W_BANKS[n][:, :], ACT.Copy,
                                         scale=col(WS)).then_inc(wt_hi, 1)

                def out_weights(h):
                    act.wait_ge(ot_pe, h + 1)
                    nc.scalar.activation(woT[:, h, :], banks[5 + h % 3][:, :], ACT.Copy).then_inc(ot_act, 1)

                def routed_high(parts):
                    act.wait_ge(f_scaled, 1)
                    for c in parts:
                        nc.scalar.activation(f_raw[:, c, :], f_raw[:, c, :], ACT.Copy, scale=col(FSC)).then_inc(f_sc, 1)
                    for c in parts:
                        act.wait_ge(f_sc, c + 1)
                        nc.scalar.activation(fh[:, c, :], f_raw[:, c, :], ACT.Copy).then_inc(f_hi, 1)

                act.dma_start(logits_t, ffn_logits.rearrange("(a n) -> a n", a=1)).then_inc(ld_route, 16)
                act.dma_start(u_t, ffn_u.rearrange("(a n) -> a n", a=1)).then_inc(ld_route, 16)
                act.dma_start(b_bc, ln_b.partition_broadcast(P)).then_inc(ld_b, 16)
                act.wait_ge(ident_ready, 2)
                nc.scalar.activation(route[0:1, 60:61], ident[0:1, 0:1], ACT.Exp)
                act.wait_ge(route_dve, 1)
                link = chain(act, route_act)
                link(nc.scalar.activation(r_e, r_e, ACT.Exp, accum_out=r_s))
                link(nc.scalar.activation(r_ls, r_s, ACT.Ln))
                link(nc.scalar.activation(r_g, u_t, ACT.Ln))
                link(nc.scalar.activation(r_g, r_g, ACT.Ln, scale=-1.0))
                for h in range(H):
                    act.wait_ge(w_gain, h + 1)
                    nc.scalar.activation(last_col[:, h:h + 1], w_g[:, h, DIM - 1:DIM], ACT.Copy, scale=-1.0).then_inc(w_neg, 1)
                    act.wait_ge(w_neg, h + 1)
                    nc.scalar.activation(w_g[:, h, 0:DIM - 1], w_g[:, h, 0:DIM - 1], ACT.Identity, bias=last_col[:, h:h + 1])
                    act.wait_ge(w_bias, h + 1)
                    nc.scalar.activation(w_g[:, h, DIM - 1:DIM], bias_col[:, h:h + 1], ACT.Copy).then_inc(w_sub, 1)
                    if h == 4:
                        query_deviation(0, 0)
                    if h == 5:
                        query_normalise(0, 0)
                    if h == 6:
                        query_deviation(1, 1)
                query_normalise(1, 1)
                act.wait_ge(w_power, 4)
                for n in range(4):
                    weights_high(n)
                query_high(0, 0)
                for n in range(4, 8):
                    weights_high(n)

                def query_step(i, k):
                    if isinstance(i, int) and i == 0:
                        for h in range(H):
                            if h == 0:
                                query_high(1, 1)
                                act.wait_ge(small_pe, 1)
                                nc.scalar.activation(w1T[:, :, :], banks[7][:, 0:2 * P].rearrange("p (c n) -> p c n", c=2), ACT.Copy)
                                nc.scalar.activation(w2T[:, :], banks[7][:, 2 * P:2 * P + 3], ACT.Copy).then_inc(small_act, 1)
                            if h == 3:
                                query_deviation(2, 0)
                                query_normalise(2, 0)
                            out_weights(h)
                        return
                    if has(i - 1):
                        query_norm(i - 1, 1 - k)
                    either(query_deviation, key_deviation, i + 2, k)
                    either(query_high, key_high, i + 1, 1 - k)
                    either(query_normalise, key_normalise, i + 2, k)
                    if has(i - 1):
                        query_centre_second(i - 1, 1 - k)
                        query_hat_out(i - 1, 1 - k, 0)
                        query_centred_high(i - 1, 1 - k, 0)
                        query_centred_high(i - 1, 1 - k, 1)
                        query_half_high(i - 1, 1 - k)
                        query_hat_out(i - 1, 1 - k, 1)
                    if isinstance(i, int) and i == 4:
                        routed_high(range(CH // 2))
                    if isinstance(i, int) and i == 5:
                        routed_high(range(CH // 2, CH))
                over_tiles(act, 0, QT - 1, 6, 3, query_step)

                def batch(b):
                    for t in range(KT):
                        if there(b, t - 1):
                            key_roots(b, t - 1)
                        else:
                            query_norm(QT - 1, LASTQ)
                        if there(b, t + 2):
                            key_deviation(b, t + 2)
                        if there(b, t + 1):
                            key_high(b, t + 1)
                        if there(b, t + 2):
                            key_normalise(b, t + 2)
                        if there(b, t - 1):
                            key_k_high(b, t - 1, 0)
                            key_k_high(b, t - 1, 1)
                            key_half_high(b, t - 1, 0)
                            key_half_high(b, t - 1, 1)
                        else:
                            query_centre_second(QT - 1, LASTQ)
                            query_hat_out(QT - 1, LASTQ, 0)
                            query_centred_high(QT - 1, LASTQ, 0)
                            query_centred_high(QT - 1, LASTQ, 1)
                            query_half_high(QT - 1, LASTQ)
                            query_hat_out(QT - 1, LASTQ, 1)
                        if t == 1 and there(b, t - KT):
                            key_m_out(b - 1)
                        if t in (4, 5) and there(b, t - KT):
                            key_u_out(b - 1, t - 4)
                over_batches(act, batch)
                key_roots(NB - 1, KT - 1)
                key_k_high(NB - 1, KT - 1, 0)
                key_k_high(NB - 1, KT - 1, 1)
                key_half_high(NB - 1, KT - 1, 0)
                key_half_high(NB - 1, KT - 1, 1)
                act.wait_ge(x_means, 1)
                nc.scalar.activation(sm[0:H, 0:1], sm[0:H, 12:13], ACT.Sqrt).then_inc(net_act, 1)
                act.wait_ge(net_to_act, VAR_READY)
                nc.scalar.activation(sm[0:H, 3:4], sm[0:H, 2:3], ACT.Sqrt, bias=col(EPS_1, H)).then_inc(net_act, 1)
                key_m_out(NB - 1)
                act.wait_ge(net_to_act, LESS_MAX_READY)
                nc.scalar.activation(sm[0:H, 16:19], sm[0:H, 8:11], ACT.Exp, accum_out=sm[0:H, 5:6])
                nc.scalar.activation(sm[0:H, 6:7], sm[0:H, 1:2], ACT.Exp, scale=-5.0 / (4.0 * NR * D * D)).then_inc(net_act, 1)
                key_u_out(NB - 1, 0)
                key_u_out(NB - 1, 1)
                act.wait_ge(net_to_act, US_READY)
                act.wait_ge(k_klo, 2 * NKT)
                out_u_high(0, 0)
                out_ratios_high(0, 0, (0,))
                act.wait_ge(net_to_act, AW_READY)
                act.wait_ge(net_pe, GLOBAL_READY)
                for h in range(H):
                    nc.scalar.activation(wo(wh, h), woT[:, h, :], ACT.Copy, scale=aw[:, 0, h:h + 1]).then_inc(x_woh, 1)
                for g in range(NG):
                    act.wait_ge(x_rb, g + 1)
                    act.wait_ge(net_to_act, WROW_READY)
                    nc.scalar.activation(rh[:, g, :], RB[g][:, :], ACT.Copy, scale=wrow).then_inc(x_rh, 1)

                def out_step(i, k, groups):
                    if has(i + 1):
                        out_u_high(i + 1, 1 - k)
                        out_ratios_high(i + 1, 1 - k, groups_of(i + 1, groups))
                    if has(i - 1):
                        out_high(i - 1, 1 - k)
                    if has(i - 2):
                        out_store(i - 2, k)
                    out_deviation(i, k)
                    out_normalise(i, k)
                over_out_tiles(act, out_step)
                out_high(QT - 1, (QT - 1) % 2)
                out_store(QT - 2, (QT - 2) % 2)
                out_store(QT - 1, (QT - 1) % 2)
                act.wait_ge(b_st[0], 16 * ((QT + 1) // 2))
                act.wait_ge(b_st[1], 16 * (QT // 2))

            @block.vector
            def _(dve):
                def query_moments(i, k):
                    dve.wait_ge(q_ld[k], (i - k) * 8 + 16)
                    nc.vector.bn_stats(bst[:, k, :], xin[:, k, :]).then_inc(q_bn, 1)
                    dve.wait_ge(q_bn, i + 1)
                    nc.vector.tensor_copy(bcnt[:, :], bst[:, k, 0:1])
                    nc.vector.bn_aggr(mv[:, k, :], bst[:, k, :]).then_inc(q_mv, 1)

                def query_affine(i, k):
                    dve.wait_ge(q_std, i + 1)
                    wait(dve, q_xhat, i - 1)
                    nc.vector.reciprocal(aff[:, k, 0:1], std[:, k:k + 1]).then_inc(q_rinv, 1)
                    dve.wait_ge(q_rinv, i + 1)
                    nc.vector.tensor_scalar(aff[:, k, 1:2], mv[:, k, 0:1], aff[:, k, 0:1], -1.0, ALU.mult, ALU.mult).then_inc(q_aff, 1)

                def query_rest(i, k):
                    dve.wait_ge(q_hi, i + 1)
                    nc.vector.tensor_tensor(xTl[:, k], chunks(XT, P), xTh[:, k], ALU.subtract).then_inc(q_lo, 1)

                def query_stats(i, k, half):
                    dve.wait_ge(q_proj, 2 * i + half + 1)
                    wait(dve, q_parts, i - 1)
                    last = head_stats(Q_PR[(2 * k + half) % 4], k, P, half)
                    if half == 1:
                        link = chain(dve, q_sums, i * 3)
                        link(last)
                        head_squares(link, k, P).then_inc(q_ss, 1)

                def query_hats(i, k):
                    dve.wait_ge(q_nrm, i + 1)
                    nc.vector.reciprocal(rc[:, k, :], nrm[:, k, :]).then_inc(q_rc, 1)
                    dve.wait_ge(q_rc, i + 1)
                    for half in range(2):
                        J = 2 * i + half
                        bank, at, hs = by_head(Q_PR[(2 * k + half) % 4][:, :]), slice(half * HW, half * HW + HW), slice(half * HH, half * HH + HH)
                        wait(dve, q_tr, J - 3)
                        nc.vector.tensor_tensor(by_head(qs[:, k, at]), bank, spread(rc[:, k, hs], P, HH), ALU.mult).then_inc(q_hat, 1)

                def query_centre(i, k):
                    wait(dve, q_cent1, i)
                    nc.vector.scalar_tensor_tensor(out=mean2[:, :], in0=hb[:, k, :, 1], scalar=-1.0, in1=hb[:, k, :, 4],
                                                   op0=ALU.mult, op1=ALU.subtract).then_inc(q_mean, 1)
                    dve.wait_ge(q_mean, i + 1)
                    wait(dve, q_qcl, 2 * i - 3)
                    wait(dve, q_qcq, 2 * i - 3)
                    nc.vector.scalar_tensor_tensor(out=by_head(qc[:, k, 0:HW]), in0=by_head(Q_PR[2 * k][:, :]), scalar=2.0,
                                                   in1=spread(mean2[:, 0:HH], P, HH), op0=ALU.mult, op1=ALU.add).then_inc(q_cent, 1)

                def query_invert(i, k):
                    dve.wait_ge(q_parts, i + 1)
                    ratio_terms(chain(dve, q_term, i * 2), k, P, C_DENQ, 0.5 / QR_SCALE).then_inc(q_rden, 1)

                def key_moments(b, t):
                    T, n, k = b * KT + t, size(t), slot(t)
                    dve.wait_ge(k_ld[t % KT], (b + t // KT) * 16 + 16)
                    nc.vector.bn_stats(bst[0:n, k, :], cin[0:n, t % KT, :]).then_inc(k_bn, 1)
                    dve.wait_ge(k_bn, T + 1)
                    nc.vector.tensor_copy(bcnt[0:n, :], bst[0:n, k, 0:1])
                    nc.vector.bn_aggr(mv[0:n, k, :], bst[0:n, k, :]).then_inc(k_mv, 1)

                def key_affine(b, t):
                    T, n, k = b * KT + t, size(t), slot(t)
                    dve.wait_ge(k_std, T + 1)
                    wait(dve, k_xhat, T - 1)
                    if at_seam(T):
                        dve.wait_ge(q_xhat, QT + T - 1)
                    nc.vector.reciprocal(aff[0:n, k, 0:1], std[0:n, k:k + 1]).then_inc(k_rinv, 1)
                    dve.wait_ge(k_rinv, T + 1)
                    nc.vector.tensor_scalar(aff[0:n, k, 1:2], mv[0:n, k, 0:1], aff[0:n, k, 0:1], -1.0, ALU.mult, ALU.mult).then_inc(k_aff, 1)

                def key_rest(b, t):
                    T, n, k = b * KT + t, size(t), slot(t)
                    dve.wait_ge(k_hi, T + 1)
                    nc.vector.tensor_tensor(xTl[:, k, :, 0:n], chunks(XT, n), xTh[:, k, :, 0:n], ALU.subtract).then_inc(k_lo, 1)

                def key_stats(b, t, half):
                    T, n, k = b * KT + t, size(t), slot(t)
                    dve.wait_ge(k_proj, 2 * T + half + 1)
                    wait(dve, k_parts, T - 1)
                    if at_seam(T):
                        dve.wait_ge(q_parts, QT + T - 1)
                    last = head_stats(K_PR[(2 * t + half) % 3], k, n, half)
                    if half == 1:
                        link = chain(dve, k_sums, T * 3)
                        link(last)
                        head_squares(link, k, n).then_inc(k_ss, 1)

                def key_tilde(b, t):
                    T, n, k = b * KT + t, size(t), slot(t)
                    dve.wait_ge(k_rt, T + 1)
                    if at_seam(T):
                        dve.wait_ge(q_tr, 2 * QT)
                    nc.vector.reciprocal(rc[0:n, k, :], rt[0:n, k, :]).then_inc(k_rc, 1)
                    dve.wait_ge(k_rc, T + 1)
                    for half in range(2):
                        hs = slice(half * HH, half * HH + HH)
                        wait(dve, k_klo, 2 * T + half - 3)
                        nc.vector.tensor_tensor(by_head(ks[0:n, k, half * HW:half * HW + HW]), by_head(K_PR[(2 * t + half) % 3][0:n, :]),
                                                spread(rc[0:n, k, hs], n, HH), ALU.mult).then_inc(k_kt, 1)

                def key_invert(b, t):
                    T, n, k = b * KT + t, size(t), slot(t)
                    dve.wait_ge(k_parts, T + 1)
                    ratio_terms(chain(dve, k_term, T * 2), k, n, C_DENK, 0.5).then_inc(k_rden, 1)
                    return nc.vector.tensor_tensor(nmax[0:n, :], nmax[0:n, :], nrm[0:n, k, :], ALU.max)

                def key_sum_out(b):
                    dve.wait_ge(k_mev, b + 1)
                    dst = ksum[:, :, one(b)].rearrange("p h a -> p (h a)")
                    nc.vector.tensor_tensor(dst, msb[:, :, 0], msb[:, :, RC], ALU.add).then_inc(k_sum, 1)
                    dve.wait_ge(k_sum, 2 * b + 1)
                    nc.vector.tensor_tensor(dst, dst, msb[:, :, RC + 1], ALU.add).then_inc(k_sum, 1)

                def key_symmetric(b, g):
                    dve.wait_ge(k_turned, 2 * b + g + 1)
                    m = msb[:, g * HH:g * HH + HH, 2:RC]
                    nc.vector.tensor_tensor(m, m, by_head(UU[:, :]), ALU.add).then_inc(k_sym, 1)

                def out_u_low(i, k):
                    dve.wait_ge(b_uh, i + 1)
                    nc.vector.scalar_tensor_tensor(out=ul[:, k], in0=qu[:, :, rows(i)], scalar=col(US), in1=uh[:, k],
                                                   op0=ALU.mult, op1=ALU.subtract).then_inc(b_ul, 1)

                def out_residual(i, k):
                    dve.wait_ge(b_o, i + 1)
                    dve.wait_ge(b_resb, i + 1)
                    wait(dve, b_x2, i - 1)
                    nc.vector.scalar_tensor_tensor(out=x1[:, k, :], in0=OO[k][:, :], scalar=col(O_INV), in1=resb[:, k, :],
                                                   op0=ALU.mult, op1=ALU.add).then_inc(b_x1, 1)

                def out_moments(i, k):
                    dve.wait_ge(b_x1, i + 1)
                    nc.vector.bn_stats(bst[:, k, :], x1[:, k, :]).then_inc(b_bn, 1)
                    dve.wait_ge(b_bn, i + 1)
                    nc.vector.tensor_copy(bcnt[:, :], bst[:, k, 0:1])
                    nc.vector.bn_aggr(mv[:, k, :], bst[:, k, :]).then_inc(b_mv, 1)
                    dve.wait_ge(b_std, i + 1)
                    nc.vector.reciprocal(aff[:, k, 0:1], std[:, k:k + 1]).then_inc(b_rinv, 1)
                    dve.wait_ge(b_rinv, i + 1)
                    nc.vector.tensor_scalar(aff[:, k, 1:2], mv[:, k, 0:1], aff[:, k, 0:1], -1.0, ALU.mult, ALU.mult).then_inc(b_aff, 1)

                def out_rest(i, k):
                    dve.wait_ge(b_hi, i + 1)
                    nc.vector.tensor_tensor(yTl, chunks(B_XT, P), yTh, ALU.subtract).then_inc(b_lo, 1)

                def out_finish(i, k):
                    dve.wait_ge(b_f, i + 1)
                    if has(i - 2):
                        dve.wait_ge(b_st[k], (i - k) * 8)
                    nc.vector.scalar_tensor_tensor(out=x2[:, k, :], in0=FF[k][:, :], scalar=col(F_INV), in1=x1[:, k, :],
                                                   op0=ALU.mult, op1=ALU.add).then_inc(b_x2, 1)

                def out_ratios_low(i, k, groups):
                    dve.wait_ge(z_h, i + 1)
                    g, n = groups[0], len(groups)
                    nc.vector.tensor_tensor(zl[:, k, g:g + n, :], ZT[:, (2 * k + g) * P:(2 * k + g + n) * P].rearrange("p (g n) -> p g n", g=n),
                                            zh[:, k, g:g + n, :], ALU.subtract).then_inc(z_l, 1)

                def weights_low(n):
                    dve.wait_ge(wt_hi, n + 1)
                    at = slice(n // CH * HW, n // CH * HW + HW)
                    nc.vector.scalar_tensor_tensor(out=wl[:, n % CH, at], in0=W_BANKS[n][:, :], scalar=col(WS),
                                                   in1=wh[:, n % CH, at], op0=ALU.mult, op1=ALU.subtract).then_inc(wt_lo, 1)

                def largest(src, tops, n):
                    for c in range(n):
                        last = nc.vector.tensor_reduce(tops[:, c:c + 1], src[:, c, :], AX.X, ALU.max, apply_absolute_value=True)
                    return last

                v = nc.vector
                for c, value in ((EPS_K, EPS / XS ** 2), (EPS_Q, EPS * EPS / XS ** 2), (EPS_1, EPS)):
                    v.memset(col(c), value)
                dve.wait_ge(ld_route, 32)
                link = chain(dve, dve_step)
                link(v.reduce_max(r_m, logits_t, AX.X))
                v.tensor_scalar(r_e, logits_t, r_m, None, ALU.subtract).then_inc(route_dve, 1)
                link(v.tensor_scalar(r_sc, logits_t, r_m, None, ALU.subtract))
                dve.wait_ge(ld_b, 16)

                def fold_bias(h):
                    dve.wait_ge(ld_w[h // 2], 16)
                    v.tensor_tensor_reduce(out=junk, in0=w_raw[:, h, :], in1=b_bc, scale=1.0, scalar=0.0,
                                           op0=ALU.mult, op1=ALU.add, accum_out=bias_col[:, h:h + 1]).then_inc(w_bias, 1)
                    dve.wait_ge(w_bias, h + 1)

                for h in range(HH):
                    fold_bias(h)
                dve.wait_ge(route_act, 4)
                link(v.tensor_scalar(r_sc, r_sc, r_ls, None, ALU.subtract))
                link(v.tensor_tensor(r_sc, r_sc, r_g, ALU.subtract))
                link(v.max(r_top, r_sc))
                v.max_index(r_idx, r_top, r_sc).then_inc(route_idx, 1)
                for h in range(HH, H):
                    fold_bias(h)
                    if h == HH:
                        query_moments(0, 0)
                    if h == HH + 2:
                        query_affine(0, 0)
                        query_moments(1, 1)
                    dve.wait_ge(w_sub, h - HH + 1)
                    v.tensor_reduce(w_top[:, h - HH:h - HH + 1], w_g[:, h - HH, :], AX.X, ALU.max, apply_absolute_value=True)
                for h in range(HH, H):
                    if h == H - 1:
                        query_affine(1, 1)
                    dve.wait_ge(w_sub, h + 1)
                    last = v.tensor_reduce(w_top[:, h:h + 1], w_g[:, h, :], AX.X, ALU.max, apply_absolute_value=True)
                link(last)
                v.tensor_reduce(col(WMAXP), w_top, AX.X, ALU.max).then_inc(w_max, 1)
                dve.wait_ge(w_all, 1)
                power_of_two(v, chain(dve, w_power), col(WMAX), col(WP), col(WS), 1.0)
                alpha = chain(dve, w_alpha)
                alpha(v.tensor_scalar(col(INV_A), col(WP), 1.0 / XS, None, ALU.mult))
                alpha(v.tensor_tensor(col(INV_A2), col(INV_A), col(INV_A), ALU.mult))
                alpha(v.tensor_scalar(col(C_NUM), col(INV_A2), 1.0 / (D - 1), None, ALU.mult))
                v.tensor_scalar(col(C_DENK), col(C_NUM), 0.5, None, ALU.mult)
                alpha(v.tensor_scalar(col(C_DENQ), col(C_NUM), 0.5 / QR_SCALE, None, ALU.mult))
                for n in range(4):
                    weights_low(n)
                query_rest(0, 0)
                for n in range(4, 8):
                    weights_low(n)

                def query_step(i, k):
                    either(query_moments, key_moments, i + 2, k)
                    if has(i - 1):
                        query_hats(i - 1, 1 - k)
                    either(query_affine, key_affine, i + 2, k)
                    if has(i - 1):
                        query_centre(i - 1, 1 - k)
                    either(query_rest, key_rest, i + 1, 1 - k)
                    query_stats(i, k, 0)
                    if has(i - 1):
                        query_invert(i - 1, 1 - k)
                    query_stats(i, k, 1)
                    if isinstance(i, int) and i in (1, 2):
                        dve.wait_ge(f_sub, 2 * i)
                        at = slice(2 * i - 2, 2 * i)
                        largest(f_raw[:, at, :], f_top[:, at], 2).then_inc(f_power, 1)
                    if isinstance(i, int) and i == 2:
                        dve.wait_ge(f_power, 2)
                        v.tensor_reduce(col(FMAXP), f_top, AX.X, ALU.max).then_inc(f_max, 1)
                    if isinstance(i, int) and i == 3:
                        dve.wait_ge(f_all, 1)
                        power_of_two(v, chain(dve, f_power, 2), col(FMAX), col(FP), col(FSC), 2.0)
                        v.tensor_scalar(col(F_INV), col(FP), 1.0 / (2.0 * XS), None, ALU.mult).then_inc(f_scaled, 1)
                over_tiles(dve, 0, QT - 1, 6, 3, query_step)

                off_diagonal = chain(dve, q_fev)

                def correlations(g):
                    dve.wait_ge(q_fc, QT)
                    off_diagonal(nc.vector.scalar_tensor_tensor(out=fsb[:, g * HH:g * HH + HH, :],
                                                                in0=ident[:, :].unsqueeze(1).to_broadcast([P, HH, D]), scalar=-1.0,
                                                                in1=by_head(FC[g][:, :]), op0=ALU.add, op1=ALU.mult))

                def add_turned(g):
                    dve.wait_ge(q_turned, g + 1)
                    part = fsb[:, g * HH:g * HH + HH, :]
                    off_diagonal(nc.vector.tensor_tensor(part, part, by_head(UU[:, :]), ALU.add))

                def batch(b):
                    for t in range(KT):
                        if isinstance(b, int) and b == 0:
                            if t in (4, 5):
                                add_turned(t - 4)
                            if t < 2:
                                largest(woT[:, KT + t:KT + t + 1, :], o_tops[:, KT + t:KT + t + 1], 1).then_inc(o_top, 1)
                            if t == 2:
                                correlations(0)
                            if t == 3:
                                correlations(1)
                        if isinstance(b, int) and b == NB - 1 and t == 0:
                            dve.wait_ge(q_fev, 5)
                            nc.vector.tensor_reduce(fs[:, :], fsb, AX.X, ALU.add).then_inc(q_fev, 1)
                        if isinstance(b, int) and b == NB - 1:
                            largest(woT[:, t:t + 1, :], o_tops[:, t:t + 1], 1).then_inc(o_top, 1)
                        if there(b, t + 2):
                            key_moments(b, t + 2)
                        if there(b, t - 1):
                            key_tilde(b, t - 1)
                        else:
                            query_hats(QT - 1, LASTQ)
                        if there(b, t + 2):
                            key_affine(b, t + 2)
                        if not there(b, t - 1):
                            query_centre(QT - 1, LASTQ)
                        if there(b, t + 1):
                            key_rest(b, t + 1)
                        if t in (3, 4) and there(b, t - KT):
                            key_symmetric(b - 1, t - 3)
                        key_stats(b, t, 0)
                        if there(b, t - 1):
                            key_invert(b, t - 1)
                        else:
                            query_invert(QT - 1, LASTQ)
                        if t == 3 and there(b, t - KT):
                            key_sum_out(b - 1)
                        key_stats(b, t, 1)
                over_batches(dve, batch)

                link = chain(dve, dve_step, 6)

                def spread_sums(g):
                    for h in range(H):
                        last = v.tensor_copy(smask[:, h, g, :, h], ksum[:, h, g * BH:g * BH + BH])
                    last.then_inc(x_smask, 1)
                dve.wait_ge(x_zero, 1)
                dve.wait_ge(k_sum, 2 * (NB - 1))
                spread_sums(0)
                means = chain(dve, x_means)
                dve.wait_ge(net_pe, SUMS_READY)
                for k, n in enumerate((NR, NB * NK)):
                    v.tensor_scalar(xm[:, k, :], XT[:, k * CH:k * CH + CH], 1.0 / n, None, ALU.mult)
                means(v.tensor_copy(sm[0:H, 12:13], XT[0:H, 2 * CH:2 * CH + 1]))
                means(v.tensor_copy(xmh, xm))
                v.tensor_tensor(xml, xm, xmh, ALU.subtract).then_inc(x_means, 1)
                key_tilde(NB - 1, KT - 1)
                dve.wait_ge(o_top, H)
                v.tensor_reduce(col(OMAXP), o_tops[:, :], AX.X, ALU.max).then_inc(o_max, 1)
                key_invert(NB - 1, KT - 1).then_inc(x_nmax, 1)
                dve.wait_ge(x_nmax, 1)
                v.tensor_reduce(col(TMP), nmax[:, :], AX.X, ALU.max).then_inc(x_umax, 1)
                v.tensor_copy(tiled[0:H, :].rearrange("p (b k) -> p b k", k=H), ident[0:H, 0:H].unsqueeze(1).to_broadcast([H, BH, H]))
                dve.wait_ge(ld_small, 96)
                dve.wait_ge(net_pe, GLOBAL_READY)
                v.tensor_scalar(feat, N_GLOBAL.rearrange("p (h k) -> p k h", k=2), col(INV_A), None, ALU.mult).then_inc(net_dve, 1)
                dve.wait_ge(net_act, NORM_READY)
                v.tensor_scalar(sm[0:H, 1:2], sm[0:H, 0:1], col(INV_A2, H), None, ALU.mult)
                dve.wait_ge(net_pe, HIDDEN_READY)
                link(v.tensor_tensor(h1[0:H, :], N_HIDDEN, b1s[:, :], ALU.add))
                link(v.bn_stats(sm[0:H, 20:26], h1[0:H, :]))
                link(v.bn_aggr(sm[0:H, 26:28], sm[0:H, 20:26]))
                v.tensor_copy(sm[0:H, 2:3], sm[0:H, 27:28]).then_inc(net_to_act, 1)
                dve.wait_ge(net_act, STD_READY)
                link(v.reciprocal(sm[0:H, 4:5], sm[0:H, 3:4]))
                link(v.tensor_scalar(h1[0:H, :], h1[0:H, :], sm[0:H, 26:27], sm[0:H, 4:5], ALU.subtract, ALU.mult))
                link(v.tensor_tensor(h1[0:H, :], h1[0:H, :], g1s[:, :], ALU.mult))
                link(v.tensor_tensor(h1[0:H, :], h1[0:H, :], be1s[:, :], ALU.add))
                v.tensor_scalar(h1[0:H, :], h1[0:H, :], 0.0, None, ALU.max).then_inc(net_dve, 1)
                dve.wait_ge(net_pe, H1_TURNED)
                v.tensor_copy(h1T, N_H1T).then_inc(net_dve, 1)
                key_symmetric(NB - 1, 0)
                dve.wait_ge(net_pe, OUTPUTS_READY)
                link(v.tensor_tensor(sm[0:H, 8:11], N_OUT, b2s[:, :], ALU.add))
                link(v.reduce_max(sm[0:H, 7:8], sm[0:H, 8:11], AX.X))
                v.tensor_scalar(sm[0:H, 8:11], sm[0:H, 8:11], sm[0:H, 7:8], None, ALU.subtract).then_inc(net_to_act, 1)
                key_sum_out(NB - 1)
                key_symmetric(NB - 1, 1)
                dve.wait_ge(k_sum, 2 * NB)
                spread_sums(1)
                dve.wait_ge(net_act, EXP_READY)
                link(v.reciprocal(sm[0:H, 11:12], sm[0:H, 5:6]))
                link(v.tensor_scalar(sm[0:H, 16:19], sm[0:H, 16:19], sm[0:H, 11:12], None, ALU.mult))
                link(v.scalar_tensor_tensor(out=sm[0:H, 19:20], in0=sm[0:H, 17:18], scalar=sm[0:H, 6:7], in1=sm[0:H, 16:17],
                                            op0=ALU.mult, op1=ALU.add))
                v.tensor_scalar(diag[0:H, 0, :], ident[0:H, 0:H], sm[0:H, 19:20], 0.5, ALU.mult, ALU.mult)
                v.tensor_scalar(diag[0:H, 1, :], ident[0:H, 0:H], sm[0:H, 18:19], 0.5, ALU.mult, ALU.mult)
                v.tensor_scalar(wcol[0:H, :], sm[0:H, 18:19], 1.0, None, ALU.mult).then_inc(net_dve, 1)
                dve.wait_ge(o_all, 1)
                power_of_two(v, link, col(OMAX), col(OP), col(OS), 1.0)
                dve.wait_ge(x_umax, 2)
                link(v.tensor_scalar(col(UMAX), col(UMAX), float(NK), None, ALU.mult))
                power_of_two(v, link, col(UMAX), col(UP), col(US), 2.0 ** 14)
                v.tensor_copy(bcnt[:, :], col(US)).then_inc(net_to_act, 1)
                link(v.tensor_tensor(col(O_INV), col(UP), col(OP), ALU.mult))
                link(v.tensor_scalar(col(O_INV), col(O_INV), col(INV_A), 2.0 ** -13, ALU.mult, ALU.mult))
                dve.wait_ge(k_uev, 2 * NB)
                out_u_low(0, 0)
                out_ratios_low(0, 0, (0,))
                dve.wait_ge(net_pe, SPREAD_READY)
                v.tensor_scalar(aw, N_SPREAD.rearrange("p (k h) -> p k h", k=2), col(OS), None, ALU.mult).then_inc(net_to_act, 1)
                link(v.tensor_scalar(wrow, N_WROW, col(OS), 1.0 / QR_SCALE, ALU.mult, ALU.mult))
                v.tensor_scalar(wrow, wrow, col(US), None, ALU.mult).then_inc(net_to_act, 1)
                for h in range(H):
                    dve.wait_ge(x_woh, h + 1)
                    v.scalar_tensor_tensor(out=wo(wl, h), in0=woT[:, h, :], scalar=aw[:, 0, h:h + 1], in1=wo(wh, h),
                                           op0=ALU.mult, op1=ALU.subtract).then_inc(x_wol, 1)
                for g in range(NG):
                    dve.wait_ge(x_rh, g + 1)
                    v.scalar_tensor_tensor(out=rl[:, g, :], in0=RB[g][:, :], scalar=wrow, in1=rh[:, g, :],
                                           op0=ALU.mult, op1=ALU.subtract).then_inc(x_rl, 1)

                def out_step(i, k, groups):
                    if has(i + 1):
                        out_u_low(i + 1, 1 - k)
                        out_ratios_low(i + 1, 1 - k, groups_of(i + 1, groups))
                    if has(i - 1):
                        out_rest(i - 1, 1 - k)
                    if has(i - 2):
                        out_finish(i - 2, k)
                    out_residual(i, k)
                    out_moments(i, k)
                over_out_tiles(dve, out_step)
                out_rest(QT - 1, (QT - 1) % 2)
                out_finish(QT - 2, (QT - 2) % 2)
                out_finish(QT - 1, (QT - 1) % 2)


_INS = ['x', 'ctx_1024', 'L0_xattn_ln_g', 'L0_xattn_ln_b', 'L0_xattn_w_in', 'L0_xattn_wp_w1', 'L0_xattn_wp_b1',
        'L0_xattn_wp_ln_g', 'L0_xattn_wp_ln_b', 'L0_xattn_wp_w2', 'L0_xattn_wp_b2', 'L0_xattn_w_out', 'L0_xattn_b_out',
        'L0_ffn_W', 'L0_ffn_b', 'L0_ffn_logits', 'L0_ffn_u']
_OUTS = [((32, 100, 512), 'float32')]


def kernel(**inputs):
    import numpy as _np
    import concourse.bacc as _bacc
    from concourse import mybir as _mybir
    from concourse.bass_utils import run_bass_kernel_spmd as _run

    nc = _bacc.Bacc("TRN2", target_bir_lowering=False, num_devices=1)
    arrays, args = {}, []
    for name in _INS:
        a = _np.ascontiguousarray(inputs[name])
        arrays[f"in_{name}_dram"] = a
        args.append(nc.dram_tensor(f"in_{name}_dram", a.shape, _mybir.dt.from_np(a.dtype), kind="ExternalInput").ap())
    for i, (shape, dtype) in enumerate(_OUTS):
        dt = _mybir.dt.from_np(_np.dtype(dtype))
        args.append(nc.dram_tensor(f"out_{i}_dram", shape, dt, kind="ExternalOutput").ap())
    build(nc, *args)
    r = _run(nc, [arrays], core_ids=[0])
    got = tuple(r.results[0][f"out_{i}_dram"] for i in range(len(_OUTS)))
    return got[0]
```
